# Optimizing a Trainium2 kernel written in Bass

```python
import numpy as np
import jax
import jax.numpy as jnp

def _softmax(x, axis=-1):
    return jax.nn.softmax(x, axis=axis)

def _gelu(x):
    return jax.nn.gelu(x, approximate=True)

def _silu(x):
    return jax.nn.silu(x)

def _sigmoid(x):
    return jax.nn.sigmoid(x)

def _layernorm(x, axis=-1, eps=1e-05):
    m = jnp.mean(x, axis=axis, keepdims=True)
    v = jnp.var(x, axis=axis, keepdims=True)
    return (x - m) / jnp.sqrt(v + eps)

def _scatter_add(tgt, idx, src, axis=0):
    return tgt.at[idx].add(src)

def _segment_sum(src, seg, n):
    return jax.ops.segment_sum(src, seg, n)
kernel_name = 'mk_vit_tower_d1_tok_img768_r4_ab8a28'

def setup_inputs(seed: int=0):
    np.random.seed(seed)
    _w = jnp.asarray

    def _rec_inputs():
        import jax
        import jax.numpy as jnp
        _rk = jax.random.key(seed)
        x = -0.00040386 + 0.999972 * jax.random.normal(jax.random.fold_in(_rk, 1), (64, 3, 128, 128), jnp.float32)
        return x
    x = _rec_inputs()

    def _L0_tok_setup():
        import jax, jax.numpy as jnp
        import numpy as np
        P = 16
        WIN = 64
        NH = 12

        def _layernorm(x, g, b, eps=1e-05):
            m = x.mean(-1, keepdims=True)
            v = ((x - m) ** 2).mean(-1, keepdims=True)
            return (x - m) * jax.lax.rsqrt(v + eps) * g + b

        def _sinusoidal_pe(n, d):
            pos = jnp.arange(n, dtype=jnp.float32)[:, None]
            i = jnp.arange(d // 2, dtype=jnp.float32)[None, :]
            ang = pos / jnp.power(10000.0, 2.0 * i / d)
            pe = jnp.zeros((n, d), jnp.float32)
            pe = pe.at[:, 0::2].set(jnp.sin(ang)).at[:, 1::2].set(jnp.cos(ang))
            return pe
        key = jax.random.key(seed)
        ks = jax.random.split(key, 8)
        B, C, H, W, D, F = (16, 3, 128, 128, 192, 768)
        s = lambda k, shape: jax.random.normal(k, shape, jnp.float32) * 0.02
        return {'input': jax.random.normal(ks[0], (B, C, H, W), jnp.float32), 'patch_w': s(ks[1], (D, C, P, P)), 'patch_b': jnp.zeros((D,), jnp.float32), 'ln_g': jnp.ones((D,), jnp.float32), 'ln_b': jnp.zeros((D,), jnp.float32), 'qkv_w': s(ks[2], (D, 3 * D)), 'qkv_b': jnp.zeros((3 * D,), jnp.float32), 'proj_w': s(ks[3], (D, D)), 'proj_b': jnp.zeros((D,), jnp.float32), 'ff1_w': s(ks[4], (D, F)), 'ff1_b': jnp.zeros((F,), jnp.float32), 'ff2_w': s(ks[5], (F, D)), 'ff2_b': jnp.zeros((D,), jnp.float32)}
    _L0_tok_all = _L0_tok_setup()
    _L0_tok_in = {k: v for k, v in _L0_tok_all.items() if k in ('patch_w', 'patch_b', 'ln_g', 'ln_b', 'qkv_w', 'qkv_b', 'proj_w', 'proj_b', 'ff1_w', 'ff1_b', 'ff2_w', 'ff2_b')}
    del _L0_tok_all

    def _L0_attn_setup():
        import jax, jax.numpy as jnp
        import numpy as np
        import math
        H = 12
        LOGIT_SCALE_MAX = math.log(1.0 / 0.01)

        def _normalize(t, eps=1e-12):
            n = jnp.linalg.norm(t, axis=-1, keepdims=True)
            return t / jnp.maximum(n, eps)
        key = jax.random.key(seed)
        ks = jax.random.split(key, 4)
        L, N, C = (256, 8, 192)
        scale = (C // H) ** (-0.5)
        return {'x': jax.random.normal(ks[0], (L, N, C), jnp.float32), 'in_proj_weight': jax.random.normal(ks[1], (3 * C, C), jnp.float32) * scale, 'in_proj_bias': jnp.zeros((3 * C,), jnp.float32), 'logit_scale': jnp.full((H, 1, 1), jnp.log(10.0), jnp.float32), 'head_scale': jnp.ones((H, 1, 1), jnp.float32), 'out_w': jax.random.normal(ks[2], (C, C), jnp.float32) * scale, 'out_b': jnp.zeros((C,), jnp.float32)}
    _L0_attn_all = _L0_attn_setup()
    _L0_attn_in = {k: v for k, v in _L0_attn_all.items() if k in ('in_proj_weight', 'in_proj_bias', 'logit_scale', 'head_scale', 'out_w', 'out_b')}
    del _L0_attn_all

    def _L0_ffn_setup():
        import jax, jax.numpy as jnp
        import numpy as np
        DIM = 192
        HEADS = 12
        HD = DIM // HEADS
        MLP = 768
        RHD = 128
        RANK = 64
        BS = 2
        RESERVE = 1
        EPS = 1e-05

        def _ln(x, g, b):
            m = jnp.mean(x, axis=-1, keepdims=True)
            v = jnp.var(x, axis=-1, keepdims=True)
            return (x - m) / jnp.sqrt(v + EPS) * g + b

        def _gelu(t):
            return jax.nn.gelu(t, approximate=False)

        def _forward(x, wq, bq, wk, bk, wv, bv, wo, bo, ln1_g, ln1_b, ln2_g, ln2_b, fc1_w, fc1_b, fc2_w, fc2_b, r_ln_g, r_ln_b, r_in_w, r_in_b, r_o1_w, r_o1_b, r_o2_w, r_o2_b, r_o3_w, r_o3_b, lra_down, lra_up):
            B, N, _ = x.shape
            e = _gelu(_ln(x, r_ln_g, r_ln_b) @ r_in_w.T + r_in_b)
            g = jnp.mean(e[:, RESERVE:, :], axis=1, keepdims=True)
            f = jnp.concatenate([e, jnp.broadcast_to(g, e.shape)], axis=-1)
            h1 = _gelu(f @ r_o1_w.T + r_o1_b)
            h2 = _gelu(h1 @ r_o2_w.T + r_o2_b)
            logits = (h2 @ r_o3_w.T + r_o3_b).reshape(B, N, BS, 2)
            hard = jax.nn.one_hot(jnp.argmax(logits, axis=-1), 2, dtype=x.dtype)
            keep = jnp.broadcast_to(jnp.array([0.0, 1.0], dtype=x.dtype), hard[:, :RESERVE].shape)
            hard = hard.at[:, :RESERVE].set(keep)
            hard = jax.lax.stop_gradient(hard)
            bits = hard[..., 1]
            indices = (bits * jnp.array([2.0, 1.0], dtype=x.dtype)).sum(-1).astype(jnp.int32)
            indices = jax.lax.stop_gradient(indices)
            xa = _ln(x, ln1_g, ln1_b)
            q = (xa @ wq.T + bq).reshape(B, N, HEADS, HD).transpose(0, 2, 1, 3)
            k = (xa @ wk.T + bk).reshape(B, N, HEADS, HD).transpose(0, 2, 1, 3)
            v = (xa @ wv.T + bv).reshape(B, N, HEADS, HD).transpose(0, 2, 1, 3)
            s = jax.nn.softmax(jnp.einsum('bhqd,bhkd->bhqk', q, k) / np.float32(np.sqrt(HD)), axis=-1)
            o = jnp.einsum('bhqk,bhkd->bhqd', s, v).transpose(0, 2, 1, 3).reshape(B, N, DIM)
            o = o @ wo.T + bo
            h = x + bits[:, :, 0:1] * o
            xf = _ln(h, ln2_g, ln2_b)
            ff = _gelu(xf @ fc1_w.T + fc1_b) @ fc2_w.T + fc2_b
            out = h + bits[:, :, 1:2] * ff
            down = jnp.einsum('bnd,krd->bknr', out, lra_down)
            up = jnp.einsum('bknr,kdr->bknd', down, lra_up)
            sel = jax.nn.one_hot(indices, 3, dtype=x.dtype)
            out = out + jnp.einsum('bknd,bnk->bnd', up, sel)
            return out
        key = jax.random.key(seed)
        ks = iter(jax.random.split(key, 40))

        def w(shape, std=0.02):
            return (jax.random.normal(next(ks), shape) * std).astype(jnp.float32)
        B, N = (128, 197)
        inp = {'x': jax.random.normal(next(ks), (B, N, DIM), dtype=jnp.float32)}
        inp.update(wq=w((DIM, DIM)), bq=jnp.zeros((DIM,), jnp.float32), wk=w((DIM, DIM)), bk=jnp.zeros((DIM,), jnp.float32), wv=w((DIM, DIM)), bv=jnp.zeros((DIM,), jnp.float32), wo=w((DIM, DIM)), bo=jnp.zeros((DIM,), jnp.float32), ln1_g=jnp.ones((DIM,), jnp.float32), ln1_b=jnp.zeros((DIM,), jnp.float32), ln2_g=jnp.ones((DIM,), jnp.float32), ln2_b=jnp.zeros((DIM,), jnp.float32), fc1_w=w((MLP, DIM)), fc1_b=jnp.zeros((MLP,), jnp.float32), fc2_w=w((DIM, MLP)), fc2_b=jnp.zeros((DIM,), jnp.float32), r_ln_g=jnp.ones((DIM,), jnp.float32), r_ln_b=jnp.zeros((DIM,), jnp.float32), r_in_w=w((RHD, DIM)), r_in_b=jnp.zeros((RHD,), jnp.float32), r_o1_w=w((RHD, 2 * RHD)), r_o1_b=jnp.zeros((RHD,), jnp.float32), r_o2_w=w((RHD // 2, RHD)), r_o2_b=jnp.zeros((RHD // 2,), jnp.float32), r_o3_w=w((2 * BS, RHD // 2), 0.01), r_o3_b=jnp.array([0.0, 5.0, 0.0, 5.0], dtype=jnp.float32), lra_down=w((3, RANK, DIM), 0.01), lra_up=w((3, DIM, RANK), 0.01))
        return inp
    _L0_ffn_all = _L0_ffn_setup()
    _L0_ffn_in = {k: v for k, v in _L0_ffn_all.items() if k in ('wq', 'bq', 'wk', 'bk', 'wv', 'bv', 'wo', 'bo', 'ln1_g', 'ln1_b', 'ln2_g', 'ln2_b', 'fc1_w', 'fc1_b', 'fc2_w', 'fc2_b', 'r_ln_g', 'r_ln_b', 'r_in_w', 'r_in_b', 'r_o1_w', 'r_o1_b', 'r_o2_w', 'r_o2_b', 'r_o3_w', 'r_o3_b', 'lra_down', 'lra_up')}
    del _L0_ffn_all
    return {'x': x, 'L0_tok_patch_w': _L0_tok_in['patch_w'], 'L0_tok_patch_b': _L0_tok_in['patch_b'], 'L0_tok_ln_g': _L0_tok_in['ln_g'], 'L0_tok_ln_b': _L0_tok_in['ln_b'], 'L0_tok_qkv_w': _L0_tok_in['qkv_w'], 'L0_tok_qkv_b': _L0_tok_in['qkv_b'], 'L0_tok_proj_w': _L0_tok_in['proj_w'], 'L0_tok_proj_b': _L0_tok_in['proj_b'], 'L0_tok_ff1_w': _L0_tok_in['ff1_w'], 'L0_tok_ff1_b': _L0_tok_in['ff1_b'], 'L0_tok_ff2_w': _L0_tok_in['ff2_w'], 'L0_tok_ff2_b': _L0_tok_in['ff2_b'], 'L0_attn_in_proj_weight': _L0_attn_in['in_proj_weight'], 'L0_attn_in_proj_bias': _L0_attn_in['in_proj_bias'], 'L0_attn_logit_scale': _L0_attn_in['logit_scale'], 'L0_attn_head_scale': _L0_attn_in['head_scale'], 'L0_attn_out_w': _L0_attn_in['out_w'], 'L0_attn_out_b': _L0_attn_in['out_b'], 'L0_ffn_wq': _L0_ffn_in['wq'], 'L0_ffn_bq': _L0_ffn_in['bq'], 'L0_ffn_wk': _L0_ffn_in['wk'], 'L0_ffn_bk': _L0_ffn_in['bk'], 'L0_ffn_wv': _L0_ffn_in['wv'], 'L0_ffn_bv': _L0_ffn_in['bv'], 'L0_ffn_wo': _L0_ffn_in['wo'], 'L0_ffn_bo': _L0_ffn_in['bo'], 'L0_ffn_ln1_g': _L0_ffn_in['ln1_g'], 'L0_ffn_ln1_b': _L0_ffn_in['ln1_b'], 'L0_ffn_ln2_g': _L0_ffn_in['ln2_g'], 'L0_ffn_ln2_b': _L0_ffn_in['ln2_b'], 'L0_ffn_fc1_w': _L0_ffn_in['fc1_w'], 'L0_ffn_fc1_b': _L0_ffn_in['fc1_b'], 'L0_ffn_fc2_w': _L0_ffn_in['fc2_w'], 'L0_ffn_fc2_b': _L0_ffn_in['fc2_b'], 'L0_ffn_r_ln_g': _L0_ffn_in['r_ln_g'], 'L0_ffn_r_ln_b': _L0_ffn_in['r_ln_b'], 'L0_ffn_r_in_w': _L0_ffn_in['r_in_w'], 'L0_ffn_r_in_b': _L0_ffn_in['r_in_b'], 'L0_ffn_r_o1_w': _L0_ffn_in['r_o1_w'], 'L0_ffn_r_o1_b': _L0_ffn_in['r_o1_b'], 'L0_ffn_r_o2_w': _L0_ffn_in['r_o2_w'], 'L0_ffn_r_o2_b': _L0_ffn_in['r_o2_b'], 'L0_ffn_r_o3_w': _L0_ffn_in['r_o3_w'], 'L0_ffn_r_o3_b': _L0_ffn_in['r_o3_b'], 'L0_ffn_lra_down': _L0_ffn_in['lra_down'], 'L0_ffn_lra_up': _L0_ffn_in['lra_up']}

def reference(x, L0_tok_patch_w, L0_tok_patch_b, L0_tok_ln_g, L0_tok_ln_b, L0_tok_qkv_w, L0_tok_qkv_b, L0_tok_proj_w, L0_tok_proj_b, L0_tok_ff1_w, L0_tok_ff1_b, L0_tok_ff2_w, L0_tok_ff2_b, L0_attn_in_proj_weight, L0_attn_in_proj_bias, L0_attn_logit_scale, L0_attn_head_scale, L0_attn_out_w, L0_attn_out_b, L0_ffn_wq, L0_ffn_bq, L0_ffn_wk, L0_ffn_bk, L0_ffn_wv, L0_ffn_bv, L0_ffn_wo, L0_ffn_bo, L0_ffn_ln1_g, L0_ffn_ln1_b, L0_ffn_ln2_g, L0_ffn_ln2_b, L0_ffn_fc1_w, L0_ffn_fc1_b, L0_ffn_fc2_w, L0_ffn_fc2_b, L0_ffn_r_ln_g, L0_ffn_r_ln_b, L0_ffn_r_in_w, L0_ffn_r_in_b, L0_ffn_r_o1_w, L0_ffn_r_o1_b, L0_ffn_r_o2_w, L0_ffn_r_o2_b, L0_ffn_r_o3_w, L0_ffn_r_o3_b, L0_ffn_lra_down, L0_ffn_lra_up):
    import jax
    import jax.numpy as jnp

    def _L0_tok_ref(input, patch_w, patch_b, ln_g, ln_b, qkv_w, qkv_b, proj_w, proj_b, ff1_w, ff1_b, ff2_w, ff2_b):
        import jax, jax.numpy as jnp
        import numpy as np
        P = 16
        WIN = 64
        NH = 12

        def _layernorm(x, g, b, eps=1e-05):
            m = x.mean(-1, keepdims=True)
            v = ((x - m) ** 2).mean(-1, keepdims=True)
            return (x - m) * jax.lax.rsqrt(v + eps) * g + b

        def _sinusoidal_pe(n, d):
            pos = jnp.arange(n, dtype=jnp.float32)[:, None]
            i = jnp.arange(d // 2, dtype=jnp.float32)[None, :]
            ang = pos / jnp.power(10000.0, 2.0 * i / d)
            pe = jnp.zeros((n, d), jnp.float32)
            pe = pe.at[:, 0::2].set(jnp.sin(ang)).at[:, 1::2].set(jnp.cos(ang))
            return pe
        B, C, H, W = input.shape
        D = patch_w.shape[0]
        dh = D // NH
        xp = input.reshape(B, C, H // P, P, W // P, P)
        x = jnp.einsum('bchpwq,dcpq->bhwd', xp, patch_w) + patch_b
        x = x.reshape(B, -1, D)
        x = _layernorm(x, ln_g, ln_b)
        N = x.shape[1]
        x = x + _sinusoidal_pe(N, D)

        def ff(y):
            return jax.nn.gelu(y @ ff1_w + ff1_b) @ ff2_w + ff2_b

        def sparse_attn(y):
            nW = N // WIN
            qkv = (y @ qkv_w + qkv_b).reshape(B, nW, WIN, 3, NH, dh)
            q, k, v = (qkv[:, :, :, 0], qkv[:, :, :, 1], qkv[:, :, :, 2])
            scores = jnp.einsum('bwqhd,bwkhd->bwhqk', q, k) * dh ** (-0.5)
            a = jax.nn.softmax(scores, axis=-1)
            o = jnp.einsum('bwhqk,bwkhd->bwqhd', a, v).reshape(B, N, D)
            return o @ proj_w + proj_b
        identity = x
        x = ff(x)
        x = sparse_attn(x)
        x = x + identity
        identity = x
        x = ff(x)
        x = x + identity
        return x

    def _L0_attn_ref(x, in_proj_weight, in_proj_bias, logit_scale, head_scale, out_w, out_b):
        import jax, jax.numpy as jnp
        import numpy as np
        import math
        H = 12
        LOGIT_SCALE_MAX = math.log(1.0 / 0.01)

        def _normalize(t, eps=1e-12):
            n = jnp.linalg.norm(t, axis=-1, keepdims=True)
            return t / jnp.maximum(n, eps)
        L, N, C = x.shape
        D = C // H
        qkv = x @ in_proj_weight.T + in_proj_bias
        q, k, v = jnp.split(qkv, 3, axis=-1)

        def to_heads(t):
            return t.reshape(L, N, H, D).transpose(1, 2, 0, 3)
        q, k, v = (to_heads(q), to_heads(k), to_heads(v))
        attn = jnp.einsum('nhld,nhmd->nhlm', _normalize(q), _normalize(k))
        ls = jnp.exp(jnp.minimum(logit_scale, LOGIT_SCALE_MAX))
        attn = attn * ls[None]
        attn = jax.nn.softmax(attn, axis=-1)
        o = jnp.einsum('nhlm,nhmd->nhld', attn, v)
        o = o * head_scale[None]
        o = o.transpose(2, 0, 1, 3).reshape(L, N, C)
        return o @ out_w.T + out_b

    def _L0_ffn_ref(x, wq, bq, wk, bk, wv, bv, wo, bo, ln1_g, ln1_b, ln2_g, ln2_b, fc1_w, fc1_b, fc2_w, fc2_b, r_ln_g, r_ln_b, r_in_w, r_in_b, r_o1_w, r_o1_b, r_o2_w, r_o2_b, r_o3_w, r_o3_b, lra_down, lra_up):
        import jax, jax.numpy as jnp
        import numpy as np
        DIM = 192
        HEADS = 12
        HD = DIM // HEADS
        MLP = 768
        RHD = 128
        RANK = 64
        BS = 2
        RESERVE = 1
        EPS = 1e-05

        def _ln(x, g, b):
            m = jnp.mean(x, axis=-1, keepdims=True)
            v = jnp.var(x, axis=-1, keepdims=True)
            return (x - m) / jnp.sqrt(v + EPS) * g + b

        def _gelu(t):
            return jax.nn.gelu(t, approximate=False)

        def _forward(x, wq, bq, wk, bk, wv, bv, wo, bo, ln1_g, ln1_b, ln2_g, ln2_b, fc1_w, fc1_b, fc2_w, fc2_b, r_ln_g, r_ln_b, r_in_w, r_in_b, r_o1_w, r_o1_b, r_o2_w, r_o2_b, r_o3_w, r_o3_b, lra_down, lra_up):
            B, N, _ = x.shape
            e = _gelu(_ln(x, r_ln_g, r_ln_b) @ r_in_w.T + r_in_b)
            g = jnp.mean(e[:, RESERVE:, :], axis=1, keepdims=True)
            f = jnp.concatenate([e, jnp.broadcast_to(g, e.shape)], axis=-1)
            h1 = _gelu(f @ r_o1_w.T + r_o1_b)
            h2 = _gelu(h1 @ r_o2_w.T + r_o2_b)
            logits = (h2 @ r_o3_w.T + r_o3_b).reshape(B, N, BS, 2)
            hard = jax.nn.one_hot(jnp.argmax(logits, axis=-1), 2, dtype=x.dtype)
            keep = jnp.broadcast_to(jnp.array([0.0, 1.0], dtype=x.dtype), hard[:, :RESERVE].shape)
            hard = hard.at[:, :RESERVE].set(keep)
            hard = jax.lax.stop_gradient(hard)
            bits = hard[..., 1]
            indices = (bits * jnp.array([2.0, 1.0], dtype=x.dtype)).sum(-1).astype(jnp.int32)
            indices = jax.lax.stop_gradient(indices)
            xa = _ln(x, ln1_g, ln1_b)
            q = (xa @ wq.T + bq).reshape(B, N, HEADS, HD).transpose(0, 2, 1, 3)
            k = (xa @ wk.T + bk).reshape(B, N, HEADS, HD).transpose(0, 2, 1, 3)
            v = (xa @ wv.T + bv).reshape(B, N, HEADS, HD).transpose(0, 2, 1, 3)
            s = jax.nn.softmax(jnp.einsum('bhqd,bhkd->bhqk', q, k) / np.float32(np.sqrt(HD)), axis=-1)
            o = jnp.einsum('bhqk,bhkd->bhqd', s, v).transpose(0, 2, 1, 3).reshape(B, N, DIM)
            o = o @ wo.T + bo
            h = x + bits[:, :, 0:1] * o
            xf = _ln(h, ln2_g, ln2_b)
            ff = _gelu(xf @ fc1_w.T + fc1_b) @ fc2_w.T + fc2_b
            out = h + bits[:, :, 1:2] * ff
            down = jnp.einsum('bnd,krd->bknr', out, lra_down)
            up = jnp.einsum('bknr,kdr->bknd', down, lra_up)
            sel = jax.nn.one_hot(indices, 3, dtype=x.dtype)
            out = out + jnp.einsum('bknd,bnk->bnd', up, sel)
            return out
        return _forward(x, wq, bq, wk, bk, wv, bv, wo, bo, ln1_g, ln1_b, ln2_g, ln2_b, fc1_w, fc1_b, fc2_w, fc2_b, r_ln_g, r_ln_b, r_in_w, r_in_b, r_o1_w, r_o1_b, r_o2_w, r_o2_b, r_o3_w, r_o3_b, lra_down, lra_up)
    h = _L0_tok_ref(x, L0_tok_patch_w, L0_tok_patch_b, L0_tok_ln_g, L0_tok_ln_b, L0_tok_qkv_w, L0_tok_qkv_b, L0_tok_proj_w, L0_tok_proj_b, L0_tok_ff1_w, L0_tok_ff1_b, L0_tok_ff2_w, L0_tok_ff2_b)
    h = h + _L0_attn_ref(_layernorm(h, axis=-1), L0_attn_in_proj_weight, L0_attn_in_proj_bias, L0_attn_logit_scale, L0_attn_head_scale, L0_attn_out_w, L0_attn_out_b)
    h = h + _L0_ffn_ref(_layernorm(h, axis=-1), L0_ffn_wq, L0_ffn_bq, L0_ffn_wk, L0_ffn_bk, L0_ffn_wv, L0_ffn_bv, L0_ffn_wo, L0_ffn_bo, L0_ffn_ln1_g, L0_ffn_ln1_b, L0_ffn_ln2_g, L0_ffn_ln2_b, L0_ffn_fc1_w, L0_ffn_fc1_b, L0_ffn_fc2_w, L0_ffn_fc2_b, L0_ffn_r_ln_g, L0_ffn_r_ln_b, L0_ffn_r_in_w, L0_ffn_r_in_b, L0_ffn_r_o1_w, L0_ffn_r_o1_b, L0_ffn_r_o2_w, L0_ffn_r_o2_b, L0_ffn_r_o3_w, L0_ffn_r_o3_b, L0_ffn_lra_down, L0_ffn_lra_up)
    return h

_drawn_inputs = setup_inputs


def setup_inputs(seed=0):
    import zlib

    import numpy as np

    out = dict(_drawn_inputs(seed))
    spreads = {'L0_tok_patch_b': (0.0, 0.1),
     'L0_tok_ln_g': (1.0, 0.2),
     'L0_tok_ln_b': (0.0, 0.1),
     'L0_tok_qkv_b': (0.0, 0.1),
     'L0_tok_proj_b': (0.0, 0.1),
     'L0_tok_ff1_b': (0.0, 0.1),
     'L0_tok_ff2_b': (0.0, 0.1),
     'L0_attn_in_proj_bias': (0.0, 0.1),
     'L0_attn_logit_scale': (2.3025851249694824, 0.2),
     'L0_attn_head_scale': (1.0, 0.2),
     'L0_attn_out_b': (0.0, 0.651),
     'L0_ffn_bq': (0.0, 0.8),
     'L0_ffn_bk': (0.0, 0.8),
     'L0_ffn_bv': (0.0, 0.8),
     'L0_ffn_bo': (0.0, 0.67),
     'L0_ffn_ln1_g': (1.0, 0.6),
     'L0_ffn_ln1_b': (0.0, 0.8),
     'L0_ffn_ln2_g': (1.0, 0.6),
     'L0_ffn_ln2_b': (0.0, 0.8),
     'L0_ffn_fc1_b': (0.0, 0.8),
     'L0_ffn_fc2_b': (0.0, 0.687),
     'L0_ffn_r_ln_g': (1.0, 0.2),
     'L0_ffn_r_ln_b': (0.0, 0.1),
     'L0_ffn_r_in_b': (0.0, 0.1),
     'L0_ffn_r_o1_b': (0.0, 0.1),
     'L0_ffn_r_o2_b': (0.0, 0.1)}
    factors = {'L0_tok_qkv_w': 3.763,
     'L0_ffn_wq': 8.0,
     'L0_ffn_wk': 8.0,
     'L0_ffn_wv': 8.0,
     'L0_ffn_wo': 7.131,
     'L0_ffn_fc1_w': 5.954,
     'L0_ffn_fc2_w': 5.635}
    for name, (base, spread) in spreads.items():
        noise = np.random.default_rng([zlib.crc32(name.encode()), seed]).standard_normal(out[name].shape)
        drawn = base * np.exp(spread * noise) if base else spread * noise
        out[name] = jnp.asarray(drawn.astype(out[name].dtype))
    for name, factor in factors.items():
        out[name] = (out[name] * factor).astype(out[name].dtype)
    return out
```

```python
from contextlib import ExitStack

import numpy as np

import concourse.bass as bass
from concourse import mybir

F32 = mybir.dt.float32
ALU = mybir.AluOpType
ACT = mybir.ActivationFunctionType
AX = mybir.AxisListType.X

IMAGES, SEQ, DIM, HEADS, MLP = 64, 64, 192, 12, 768
PATCH, CHANNELS = 16, 3
FEATS = CHANNELS * PATCH * PATCH
P = 128
HALF = DIM // 2
HD = DIM // HEADS
HH = HEADS // 2
TOKENS = IMAGES * SEQ
GROUP = 512
TILES = GROUP // P
GROUPS = TOKENS // GROUP
KP = FEATS // P
KM = MLP // P
PART = 256
PARTS = TOKENS // PART
UNITS = 2 * TOKENS // P
UPP = 2 * PART // P
UPG = 8
RHD, RH2, BITS = 128, 64, 2
RANK3 = 192
ROW = DIM + 8
EPS = 1e-5
LOGIT_SCALE_MAX = float(np.log(100.0))
NORM_MIN2 = 1e-24


def sweep(engine, turns, lags, body):
    for i in range(lags + 1):
        body(i, lambda lag, i=i: 0 <= i - lag < turns)
    with engine.Fori(lags + 1, turns) as i:
        body(i, lambda lag: True)
    for i in range(turns, turns + lags):
        body(i, lambda lag, i=i: 0 <= i - lag < turns)


def wait(engine, sem, value):
    if isinstance(value, int) and value <= 0:
        return
    engine.wait_ge(sem, value)


def waits(engine, *pairs):
    values = [v for _, v in pairs]
    for v in values:
        if not isinstance(v, int):
            engine.compute_val(v)
    for (sem, _), value in zip(pairs, values):
        wait(engine, sem, value)


class Memory:

    def __init__(self, nc, ctx, phase):
        self.nc, self.ctx, self.phase, self.held = nc, ctx, phase, []
        ctx.callback(self.clear)

    def clear(self):
        self.nc.clear_and_free_semaphores(self.held)
        self.nc.all_engine_barrier()

    def sb(self, name, shape):
        return self.ctx.enter_context(self.nc.sbuf_tensor(f"{self.phase}_{name}", shape, F32))

    def ps(self, name, shape=(P, 512)):
        return self.ctx.enter_context(self.nc.psum_tensor(f"{self.phase}_{name}", list(shape), F32))

    def sem(self, name):
        self.held.append(self.nc.alloc_semaphore(f"{self.phase}_{name}"))
        return self.held[-1]

    def sems(self, name, n):
        return [self.sem(f"{name}{i}") for i in range(n)]


def load_weights(nc, mem, w, ins):
    done = {k: mem.sem(f"loaded_{k}") for k in ("patch", "ff", "tok", "cos", "ffn")}
    counts = dict.fromkeys(done, 0)
    plan = {k: [] for k in done}

    def take(which, dst, src):
        plan[which].append((dst, src))
        counts[which] += 16

    def chunked(which, name, key, rows, chunks, cols, bias=None):
        w[name] = mem.sb(name, [rows + (bias is not None), chunks, cols])
        take(which, w[name][0:rows, :, :], ins[key].rearrange("(c p) n -> p c n", p=rows))
        if bias:
            take(which, w[name][rows:rows + 1, chunks - 1, :], ins[bias].rearrange("(a n) -> a n", a=1))

    def column(which, name, key, rows, chunks):
        w[name] = mem.sb(name, [rows, chunks])
        take(which, w[name][:, :], ins[key + "_col"])

    def spread(which, name, key, cols):
        w[name] = mem.sb(name, [P, cols])
        take(which, w[name][:, :], ins[key].rearrange("(a n) -> a n", a=1).to_broadcast([P, cols]))

    def plain(which, name, key, rows, cols):
        w[name] = mem.sb(name, [rows, cols])
        take(which, w[name][:, :], ins[key])

    chunked("patch", "patch_w", "patch_w", P, KP, DIM)
    spread("patch", "patch_b", "tok_patch_b", DIM)
    spread("patch", "ln_g", "tok_ln_g", DIM)
    spread("patch", "ln_b", "tok_ln_b", DIM)
    plain("patch", "pe", "pe", P, DIM)
    plain("patch", "ident", "ident", P, P)
    chunked("ff", "ff1", "tok_ff1_w", HALF, 2, MLP, "tok_ff1_b")
    chunked("ff", "ff2", "tok_ff2_w", P, KM, DIM)
    column("ff", "ff2_col", "tok_ff2_b", HALF, 2)
    spread("ff", "ff2_b", "tok_ff2_b", DIM)
    chunked("tok", "tok_qkv", "tok_qkv_w", HALF, 2, 3 * DIM, "tok_qkv_b")
    chunked("tok", "tok_proj", "tok_proj_w", HALF, 2, DIM, "tok_proj_b")
    chunked("cos", "cos_qkv", "cos_qkv_w", HALF, 2, 3 * DIM, "cos_qkv_b")
    chunked("cos", "cos_proj", "cos_proj_w", HALF, 2, DIM, "attn_out_b")
    spread("cos", "logit_scale", "logit_scale", HEADS)
    column("cos", "head_scale", "head_scale", HALF, 2)
    plain("ffn", "first_token", "first_token", P, 1)
    chunked("ffn", "r_in_raw", "r_in_w", HALF, 2, RHD)
    chunked("ffn", "ffn_qkv_raw", "ffn_qkv_w", HALF, 2, 3 * DIM)
    chunked("ffn", "fc1_raw", "fc1_w", HALF, 2, MLP)
    chunked("ffn", "ffn_proj", "ffn_proj_w", HALF, 2, DIM, "ffn_bo")
    chunked("ffn", "fc2", "fc2_w", P, KM, DIM)
    spread("ffn", "fc2_b", "ffn_fc2_b", DIM)
    chunked("ffn", "r_o1", "r_o1_w", RHD, 2, RHD)
    column("ffn", "r_o1_b", "ffn_r_o1_b", RHD, 1)
    plain("ffn", "r_o2", "r_o2_w", RHD, RH2)
    column("ffn", "r_o2_b", "ffn_r_o2_b", RH2, 1)
    w["r_o3"] = mem.sb("r_o3", [RH2 + 1, 2 * BITS])
    take("ffn", w["r_o3"][0:RH2, :], ins["r_o3_w"])
    take("ffn", w["r_o3"][RH2:RH2 + 1, :], ins["ffn_r_o3_b"].rearrange("(a n) -> a n", a=1))
    chunked("ffn", "lra_down", "lra_down", HALF, 2, RANK3)
    chunked("ffn", "lra_up", "lra_up", HALF, 2, DIM)
    for name in ("r_ln_g", "r_ln_b", "ln1_g", "ln1_b", "ln2_g", "ln2_b"):
        column("ffn", name, "ffn_" + name, HALF, 2)
    w["fold_bias"] = mem.sb("fold_bias", [1, RHD + 3 * DIM + MLP])
    for at, key, n in ((0, "ffn_r_in_b", RHD), (RHD, "ffn_qkv_b", 3 * DIM), (RHD + 3 * DIM, "ffn_fc1_b", MLP)):
        take("ffn", w["fold_bias"][0:1, at:at + n], ins[key].rearrange("(a n) -> a n", a=1))
    w["done"], w["counts"], w["plan"] = done, counts, plan


def start_loads(engine, w, which):
    for dst, src in w["plan"][which]:
        engine.dma_start(dst, src).then_inc(w["done"][which], 16)


def layer(pe, out, lhs, rhs):
    for n, (a, b) in enumerate(zip(lhs, rhs)):
        last = pe.matmul(out, a, b, start=(n == 0), stop=(n == len(lhs) - 1))
    return last


def halves(x, cols):
    return [x[0:HALF, 0, cols], x[0:HALF + 1, 1, cols]]


def span(n, size):
    return slice(n * size, (n + 1) * size)



def patch_phase(nc, w, patches, x1_dram, y_dram):
    with ExitStack() as ctx:
        mem = Memory(nc, ctx, "patch")
        raw = mem.sb("raw", [P, KP, GROUP])
        xr = mem.sb("xr", [P, TILES, DIM])
        stats = mem.sb("stats", [P, TILES, 6])
        mv = mem.sb("mv", [P, TILES, 2])
        vare = mem.sb("vare", [P, TILES])
        power = mem.sb("power", [P, TILES])
        rstd = mem.sb("rstd", [P, TILES])
        posb = mem.sb("posb", [P, DIM])
        xn = mem.sb("xn", [P, TILES, DIM])
        xg = mem.sb("xg", [P, TILES, DIM])
        x1 = mem.sb("x1", [P, TILES, DIM])
        xT = mem.sb("xT", [HALF + 1, 2, GROUP])
        hT = mem.sb("hT", [P, KM, GROUP])
        yT = mem.sb("yT", [HALF, 2, GROUP])
        ps_patch = [mem.ps(f"ps_patch{i}") for i in range(2)]
        ps_t = [mem.ps(f"ps_t{i}") for i in range(2)]
        ps_h = [mem.ps(f"ps_h{i}") for i in range(2)]
        ps_y = [mem.ps(f"ps_y{i}") for i in range(2)]

        raw_loaded = mem.sem("raw_loaded")
        const_set = mem.sem("const_set")
        posb_set = mem.sem("posb_set")
        patched = mem.sem("patched")
        evacuated = mem.sem("evacuated")
        counted = mem.sem("counted")
        measured = mem.sem("measured")
        varied = mem.sem("varied")
        rooted = mem.sem("rooted")
        normed = mem.sem("normed")
        gained = mem.sem("gained")
        placed = mem.sem("placed")
        turned = mem.sem("turned")
        xt_ready = mem.sem("xt_ready")
        hidden = mem.sem("hidden")
        gelued = mem.sem("gelued")
        y_summed = mem.sem("y_summed")
        y_ready = mem.sem("y_ready")
        x1_stored = mem.sem("x1_stored")
        y_stored = mem.sem("y_stored")

        with nc.Block() as block:

            @block.sync
            def _(sp):
                start_loads(sp, w, "patch")

                def turn(i, active):
                    if active(0):
                        wait(sp, patched, TILES * i)
                        sp.dma_start(raw[:, :, :], patches[i]).then_inc(raw_loaded, 16)
                    if isinstance(i, int) and i == 0:
                        for which in ("ff", "tok", "cos", "ffn"):
                            start_loads(sp, w, which)
                    if active(1):
                        wait(sp, placed, TILES * i)
                        sp.dma_start(x1_dram[i - 1], x1[:, :, :]).then_inc(x1_stored, 16)
                        wait(sp, y_ready, 2 * i)
                        for a in range(2):
                            sp.dma_start(y_dram[2 * (i - 1) + a], yT[:, :, span(a, PART)]).then_inc(y_stored, 16)

                sweep(sp, GROUPS, 1, turn)
                sp.wait_ge(x1_stored, 16 * GROUPS)
                sp.wait_ge(y_stored, 32 * GROUPS)

            @block.tensor
            def _(pe):
                pe.wait_ge(w["done"]["patch"], w["counts"]["patch"])
                pe.wait_ge(const_set, 2)

                def turn(i, active):
                    if active(1):
                        wait(pe, placed, TILES * i)
                        for c in range(2):
                            wait(pe, xt_ready, 2 * (i - 2) + c + 1 if not (isinstance(i, int) and i < 2) else 0)
                            for t in range(TILES):
                                last = pe.transpose(ps_t[c][0:HALF, span(t, P)], x1[:, t, span(c, HALF)], w["ident"][:, :])
                            last.then_inc(turned, 1)
                    if active(0):
                        wait(pe, raw_loaded, 16 * i + 16)
                        for t in range(TILES):
                            wait(pe, evacuated, TILES * i + t - 1)
                            layer(pe, ps_patch[t % 2][:, 0:DIM],
                                  [raw[:, k, span(t, P)] for k in range(KP)],
                                  [w["patch_w"][:, k, :] for k in range(KP)]).then_inc(patched, 1)
                    if active(1):
                        wait(pe, w["done"]["ff"], w["counts"]["ff"])
                        wait(pe, xt_ready, 2 * i)
                        for k in range(KM):
                            wait(pe, gelued, KM * (i - 1) + k - 1)
                            layer(pe, ps_h[k % 2][:, :], [w["ff1"][0:HALF, 0, span(k, P)], w["ff1"][0:HALF + 1, 1, span(k, P)]],
                                  halves(xT, slice(0, GROUP))).then_inc(hidden, 1)
                        for m in range(2):
                            wait(pe, y_ready, 2 * (i - 1) + m - 1)
                            for k in range(KM):
                                if m == 0:
                                    wait(pe, gelued, KM * (i - 1) + k + 1)
                                last = pe.matmul(ps_y[m][0:HALF, :], w["ff2"][:, k, span(m, HALF)], hT[:, k, :],
                                                 start=(k == 0), stop=(k == KM - 1))
                            last.then_inc(y_summed, 1)

                sweep(pe, GROUPS, 1, turn)

            @block.scalar
            def _(act):
                act.wait_ge(w["done"]["ff"], w["counts"]["ff"])

                def turn(i, active):
                    if active(1):
                        for k in range(KM):
                            wait(act, hidden, KM * (i - 1) + k + 1)
                            act.activation(hT[:, k, :], ps_h[k % 2][:, :], ACT.Gelu_apprx_tanh).then_inc(gelued, 1)
                        for m in range(2):
                            wait(act, y_summed, 2 * (i - 1) + m + 1)
                            wait(act, y_stored, 32 * (i - 1))
                            act.activation(yT[:, m, :], ps_y[m][0:HALF, :], ACT.Identity,
                                           bias=w["ff2_col"][:, m:m + 1]).then_inc(y_ready, 1)

                sweep(act, GROUPS, 1, turn)

            @block.gpsimd
            def _(pool):
                pool.memset(power[:, :], -0.5).then_inc(const_set, 1)
                pool.wait_ge(w["done"]["patch"], w["counts"]["patch"])
                pool.tensor_tensor(posb[:, :], w["ln_b"][:, :], w["pe"][:, :], ALU.add).then_inc(posb_set, 1)
                pool.wait_ge(const_set, 2)
                pool.wait_ge(posb_set, 1)

                def turn(i, active):
                    if active(0):
                        wait(pool, varied, i + 1)
                        pool.tensor_tensor(rstd[:, :], vare[:, :], power[:, :], ALU.pow).then_inc(rooted, 1)
                        for t in range(TILES):
                            wait(pool, normed, TILES * i + t + 1)
                            pool.tensor_tensor(xg[:, t, :], xn[:, t, :], w["ln_g"][:, :], ALU.mult).then_inc(gained, 1)
                        wait(pool, x1_stored, 16 * i)
                        wait(pool, turned, 2 * i)
                        for t in range(TILES):
                            wait(pool, gained, TILES * i + t + 1)
                            pool.tensor_tensor(x1[:, t, :], xg[:, t, :], posb[:, :], ALU.add).then_inc(placed, 1)

                sweep(pool, GROUPS, 1, turn)

            @block.vector
            def _(dve):
                dve.memset(xT[HALF:HALF + 1, :, :], 1.0).then_inc(const_set, 1)
                dve.wait_ge(w["done"]["patch"], w["counts"]["patch"])

                def turn(i, active):
                    if active(1):
                        for c in range(2):
                            wait(dve, turned, 2 * (i - 1) + c + 1)
                            wait(dve, hidden, KM * (i - 1))
                            dve.tensor_copy(xT[0:HALF, c, :], ps_t[c][0:HALF, :]).then_inc(xt_ready, 1)
                    if active(0):
                        for t in range(TILES):
                            wait(dve, patched, TILES * i + t + 1)
                            dve.tensor_tensor(xr[:, t, :], ps_patch[t % 2][:, 0:DIM], w["patch_b"][:, :], ALU.add).then_inc(evacuated, 1)
                            wait(dve, evacuated, TILES * i + t + 1)
                            dve.bn_stats(stats[:, t, :], xr[:, t, :]).then_inc(counted, 1)
                            dve.drain()
                            dve.bn_aggr(mv[:, t, :], stats[:, t, :]).then_inc(measured, 1)
                        wait(dve, measured, TILES * i + TILES)
                        dve.tensor_scalar(vare[:, :], mv[:, :, 1], EPS, None, ALU.add).then_inc(varied, 1)
                        wait(dve, rooted, i + 1)
                        wait(dve, gained, TILES * i)
                        for t in range(TILES):
                            dve.tensor_scalar(xn[:, t, :], xr[:, t, :], mv[:, t, 0:1], rstd[:, t:t + 1],
                                              ALU.subtract, ALU.mult).then_inc(normed, 1)

                sweep(dve, GROUPS, 1, turn)



def attention_phase(nc, w, kind, x_src, res_dram, out_dram, big):
    cos = kind == "cos"
    qkv_w = w[{"tok": "tok_qkv", "cos": "cos_qkv", "ffn": "ffn_qkv"}[kind]]
    proj_w = w[{"tok": "tok_proj", "cos": "cos_proj", "ffn": "ffn_proj"}[kind]]
    loaded = w["done"][kind], w["counts"][kind]
    L_S = 6 if cos else 4
    L_SUM, L_T, L_PV, L_V = L_S + 1, L_S + 3, L_S + 4, 5
    L_PROJ = L_PV + 1
    row = ROW if kind == "ffn" else DIM
    score_scale = 1.0 if cos else float(HD) ** -0.5
    Q0, K0, V0 = 0, DIM, 2 * DIM

    with ExitStack() as ctx:
        mem = Memory(nc, ctx, kind)
        xT = mem.sb("xT", [HALF + 1, 2, 2, PART])
        qkT = mem.sb("qkT", [P, 2, 4, PART])
        kmask = mem.sb("kmask", [P, 2, 2, HH, PART])
        vblk = mem.sb("vblk", [P, 2, 4, HH, 2 * HD])
        rowmax = mem.sb("rowmax", [P, 2, HH])
        shifted = mem.sb("shifted", [P, 2, HH, SEQ])
        probs = mem.sb("probs", [P, 4, HH, SEQ])
        total = mem.sb("total", [P, 2, HH])
        rtotal = mem.sb("rtotal", [P, 2, HH])
        probsT = mem.sb("probsT", [P, 2, 3, P])
        if cos:
            square = mem.sb("square", [P, 2, 2 * DIM])
            norm2 = mem.sb("norm2", [P, 2, 2 * HEADS])
            floor2 = mem.sb("floor2", [P, 2, 2 * HEADS])
            rnorm = mem.sb("rnorm", [P, 2, 2 * HEADS])
            power = mem.sb("power", [P, 2, 2 * HEADS])
            qk_scale = mem.sb("qk_scale", [P, 2, 2 * HEADS])
            scale_min = mem.sb("scale_min", [P, HEADS])
            gain = mem.sb("gain", [P, 2 * HEADS])
            qkn = mem.sb("qkn", [P, 2, 2 * DIM])
        else:
            oT = mem.sb("oT", [HALF + 1, 2, 2, P])
            res = mem.sb("res", [P, 2, 2, row])
            outb = mem.sb("outb", [P, 2, 2, DIM])
        ps_s = [mem.ps(f"ps_s{i}") for i in range(2)]
        ps_pt = [mem.ps(f"ps_pt{i}") for i in range(2)]
        ps_o = mem.ps("ps_o")
        ps_x = [mem.ps(f"ps_x{i}") for i in range(2)]
        ps_r = mem.ps("ps_r")
        ps_v = ps_r if cos else ps_x[0]

        const_set = mem.sem("const_set")
        x_loaded = mem.sems("x_loaded", 2)
        v_mm, v_ready = mem.sem("v_mm"), mem.sem("v_ready")
        kmask_loaded = mem.sems("kmask_loaded", 2)
        scored = mem.sem("scored")
        maxed = mem.sem("maxed")
        shift_done = mem.sem("shift_done")
        exped = mem.sem("exped")
        summed = mem.sem("summed")
        inverted = mem.sem("inverted")
        weighted = mem.sem("weighted")
        turned = mem.sem("turned")
        pt_ready = mem.sem("pt_ready")
        mixed = mem.sem("mixed")
        o_ready = mem.sem("o_ready")
        if cos:
            qk_mm = mem.sem("qk_mm")
            squared = mem.sem("squared")
            norm_summed = mem.sem("norm_summed")
            floored = mem.sem("floored")
            norm_inv = mem.sem("norm_inv")
            norm_ready = mem.sem("norm_ready")
            qkn_ready = mem.sem("qkn_ready")
            qkt = mem.sem("qkt")
            qk_ready = mem.sem("qk_ready")
            power_set, capped, gain_set = mem.sem("power_set"), mem.sem("capped"), mem.sem("gain_set")
        else:
            k_mm, q_mm = mem.sem("k_mm"), mem.sem("q_mm")
            k_ready, q_ready = mem.sem("k_ready"), mem.sem("q_ready")
            projected = mem.sem("projected")
            out_ready = mem.sem("out_ready")
            res_loaded = mem.sems("res_loaded", 2)
            stored = mem.sems("stored", 2)

        def part(i, u, lag):
            q, r = divmod(u - lag, UPP)
            return 2 * i + q, q % 2, i + q // 2, r

        def run(engine, step, peeled=0):
            turns = UNITS // UPG
            for i in range(2):
                for u in range(UPG):
                    step(i, u, lambda lag, i=i, u=u: 0 <= i * UPG + u - lag < UNITS)
            with engine.Fori(2, turns - peeled) as i:
                for u in range(UPG):
                    step(i, u, lambda lag: True)
            for i in range(turns - peeled, turns + 2):
                for u in range(UPG):
                    step(i, u, lambda lag, i=i, u=u: 0 <= i * UPG + u - lag < UNITS)

        with nc.Block() as block:

            @block.sync
            def _(sp):
                def load(j, par):
                    wait(sp, v_mm, j - 1)
                    sp.dma_start(xT[0:HALF, par, :, :], x_src(j)).then_inc(x_loaded[par], 16)

                def load_res(j, par):
                    wait(sp, out_ready, 2 * (j - 1))
                    sp.dma_start(res[:, par, :, :], res_dram[j]).then_inc(res_loaded[par], 16)

                for j in range(2):
                    load(j, j)
                    if not cos:
                        load_res(j, j)
                sp.wait_ge(const_set, 5)

                def step(i, u, active):
                    at = 3 if cos else 1
                    j, par, _, r = part(i, u, 0)
                    if active(0) and r == at:
                        waits(sp, (qk_ready if cos else k_ready, 2 * j + 2 if cos else j + 1), (scored, UPP * (j - 1)))
                        for h in range(HH):
                            rows = span(h, HD)
                            sp.dma_start(kmask[rows, par, :, h, :], qkT[rows, par, 2:4, :]).then_inc(kmask_loaded[par], 16)
                    if not cos:
                        j, par, _, r = part(i, u, L_PROJ + 1)
                        if active(L_PROJ + 1) and r == UPP - 1:
                            wait(sp, out_ready, 2 * (j + 1))
                            sp.dma_start(out_dram[j], outb[:, par, :, :]).then_inc(stored[par], 16)
                            if not (isinstance(j, int) and j + 2 >= PARTS):
                                load_res(j + 2, par)
                    j, par, _, r = part(i, u, L_V)
                    if active(L_V) and r == 0 and not (isinstance(j, int) and j + 2 >= PARTS):
                        load(j + 2, par)

                run(sp, step, peeled=1)
                if not cos:
                    for s in stored:
                        sp.wait_ge(s, 16 * PARTS // 2)

            @block.tensor
            def _(pe):
                pe.wait_ge(*loaded)
                pe.wait_ge(const_set, 5)

                def project_part(out, cols, par, into):
                    for m in range(2):
                        c0 = cols + m * HALF
                        last = layer(pe, out[0:HALF, span(m, PART)],
                                     [qkv_w[0:HALF, 0, c0:c0 + HALF], qkv_w[0:HALF + 1, 1, c0:c0 + HALF]],
                                     [xT[0:HALF, par, 0, :], xT[0:HALF + 1, par, 1, :]])
                    last.then_inc(into, 1)

                def step(i, u, active):
                    if active(L_S):
                        n, (j, par, before, r) = UPG * i + (u - L_S), part(i, u, L_S)
                        c, t, ring = r % 2, r // 2, (u - L_S) % 2
                        if r == 0:
                            wait(pe, kmask_loaded[par], 16 * HH * (before + 1))
                            wait(pe, qk_ready if cos else q_ready, 2 * j + 2 if cos else j + 1)
                        wait(pe, shift_done, n - 1)
                        for a in range(2):
                            cols = slice(t * P + a * SEQ, t * P + (a + 1) * SEQ)
                            last = pe.matmul(ps_s[ring][span(a, SEQ), 0:HH * SEQ], qkT[:, par, c, cols],
                                             kmask[:, par, c, :, cols], start=True, stop=True)
                        last.then_inc(scored, 1)
                    if active(L_T):
                        n, ring = UPG * i + (u - L_T), (u - L_T) % 2
                        wait(pe, weighted, n + 1)
                        wait(pe, pt_ready, n - 1)
                        for b in range(3):
                            last = pe.transpose(ps_pt[ring][:, span(b, P)],
                                                probs[:, (u - L_T) % 4, 2 * b:2 * b + 2, :].rearrange("p h k -> p (h k)"),
                                                w["ident"][:, :])
                        last.then_inc(turned, 1)
                    j, par, before, r = part(i, u, 0)
                    if active(0) and cos and r == 0:
                        wait(pe, x_loaded[par], 16 * (before + 1))
                        for t in range(2):
                            wait(pe, qk_ready, 2 * (j - 1) + t + 1 if not (isinstance(j, int) and j == 0) else 0)
                            layer(pe, ps_x[t][:, 0:2 * DIM], [xT[0:HALF, par, 0, span(t, P)], xT[0:HALF + 1, par, 1, span(t, P)]],
                                  [qkv_w[0:HALF, 0, 0:2 * DIM], qkv_w[0:HALF + 1, 1, 0:2 * DIM]]).then_inc(qk_mm, 1)
                    if active(0) and cos and r == 2:
                        for t in range(2):
                            wait(pe, qkn_ready, 2 * j + t + 1)
                            for m in range(4):
                                last = pe.transpose(ps_x[t][0:HALF, span(m, P)], qkn[:, t, span(m, HALF)], w["ident"][:, :])
                            last.then_inc(qkt, 1)
                    if active(0) and not cos and r == 0:
                        wait(pe, x_loaded[par], 16 * (before + 1))
                        wait(pe, v_ready, j - 1)
                        project_part(ps_x[0], K0, par, k_mm)
                    if active(0) and not cos and r == 1:
                        wait(pe, q_ready, j)
                        project_part(ps_x[1], Q0, par, q_mm)
                    j, par, before, r = part(i, u, L_V)
                    if active(L_V) and r == 0:
                        if cos:
                            wait(pe, v_ready, j)
                        else:
                            wait(pe, k_ready, min(j + 2, PARTS) if isinstance(j, int) else j + 2)
                        for a in range(4):
                            for odd in range(2):
                                c0 = V0 + odd * HALF
                                last = layer(pe, ps_v[span(odd, SEQ), span(a, HALF)],
                                             [xT[0:HALF, par, 0, span(a, SEQ)], xT[0:HALF + 1, par, 1, span(a, SEQ)]],
                                             [qkv_w[0:HALF, 0, c0:c0 + HALF], qkv_w[0:HALF + 1, 1, c0:c0 + HALF]])
                        last.then_inc(v_mm, 1)
                    if active(L_PV):
                        n, (j, par, before, r) = UPG * i + (u - L_PV), part(i, u, L_PV)
                        c, t, ring = r % 2, r // 2, (u - L_PV) % 2
                        if r == 0:
                            wait(pe, v_ready, j + 1)
                        wait(pe, pt_ready, n + 1)
                        if c == 0:
                            wait(pe, o_ready, 2 * j + t)
                        for a in range(2):
                            for b in range(3):
                                last = pe.matmul(ps_o[span(b, 2 * HD), c * P + a * SEQ:c * P + (a + 1) * SEQ],
                                                 vblk[:, par, 2 * t + a, 3 * c + b, :], probsT[:, ring, b, span(a, SEQ)],
                                                 start=True, stop=True)
                        last.then_inc(mixed, 1)
                    if not cos and active(L_PROJ):
                        j, par, before, r = part(i, u, L_PROJ)
                        if r % 2:
                            t = r // 2
                            wait(pe, o_ready, 2 * j + t + 1)
                            wait(pe, out_ready, 2 * j + t)
                            layer(pe, ps_r[:, 0:DIM], [oT[0:HALF, t, 0, :], oT[0:HALF + 1, t, 1, :]],
                                  [proj_w[0:HALF, 0, :], proj_w[0:HALF + 1, 1, :]]).then_inc(projected, 1)

                run(pe, step)

            @block.scalar
            def _(act):
                if cos:
                    act.wait_ge(capped, 1)
                    act.activation(gain[:, 0:HEADS], scale_min[:, :], ACT.Exp).then_inc(gain_set, 1)

                def step(i, u, active):
                    if active(L_T):
                        n, ring = UPG * i + (u - L_T), (u - L_T) % 2
                        wait(act, turned, n + 1)
                        wait(act, mixed, n - 1)
                        act.activation(probsT[:, ring, :, :].rearrange("p b q -> p (b q)"), ps_pt[ring][:, 0:3 * P],
                                       ACT.Copy).then_inc(pt_ready, 1)
                    if active(L_S):
                        n = UPG * i + (u - L_S)
                        wait(act, shift_done, n + 1)
                        wait(act, turned, n - 3)
                        act.activation(probs[:, (u - L_S) % 4, :, :], shifted[:, (u - L_S) % 2, :, :], ACT.Exp,
                                       scale=score_scale).then_inc(exped, 1)
                    j, par, before, r = part(i, u, 0)
                    if active(0) and not cos and r == 1:
                        wait(act, q_mm, j + 1)
                        wait(act, scored, UPP * (j - 1))
                        act.activation(qkT[0:HALF, par, 0:2, :], ps_x[1][0:HALF, :].rearrange("p (c t) -> p c t", c=2),
                                       ACT.Copy).then_inc(q_ready, 1)
                    if active(0) and cos and r == 0:
                        for t in range(2):
                            wait(act, qk_mm, 2 * j + t + 1)
                            wait(act, norm_summed, 2 * (j - 1) + t + 1 if not (isinstance(j, int) and j == 0) else 0)
                            act.activation(square[:, t, :], ps_x[t][:, 0:2 * DIM], ACT.Square).then_inc(squared, 1)
                    if active(0) and cos and r == 2:
                        for t in range(2):
                            wait(act, qkt, 2 * j + t + 1)
                            if t == 0:
                                wait(act, scored, UPP * (j - 1))
                                wait(act, kmask_loaded[par], 16 * HH * before)
                            act.activation(qkT[0:HALF, par, :, span(t, P)],
                                           ps_x[t][0:HALF, :].rearrange("p (c t) -> p c t", c=4), ACT.Copy).then_inc(qk_ready, 1)

                run(act, step)

            @block.gpsimd
            def _(pool):
                pool.memset(kmask[:, 0, :, :, :], 0.0).then_inc(const_set, 1)
                pool.memset(kmask[:, 1, :, :, :], 0.0).then_inc(const_set, 1)
                if cos:
                    pool.memset(power[:, :, :], -0.5).then_inc(power_set, 1)
                    pool.wait_ge(power_set, 1)
                    pool.wait_ge(gain_set, 2)
                    pool.wait_ge(const_set, 5)

                def step(i, u, active):
                    j, par, before, r = part(i, u, 0)
                    if cos and active(0) and r == 0:
                        wait(pool, floored, j + 1)
                        pool.tensor_tensor(rnorm[:, :, :], floor2[:, :, :], power[:, :, :], ALU.pow).then_inc(norm_inv, 1)
                        wait(pool, norm_inv, j + 1)
                        wait(pool, qkn_ready, 2 * j)
                        for t in range(2):
                            pool.tensor_tensor(qk_scale[:, t, :], rnorm[:, t, :], gain[:, :], ALU.mult).then_inc(norm_ready, 1)
                    if active(L_SUM):
                        n, ring = UPG * i + (u - L_SUM), (u - L_SUM) % 4
                        wait(pool, inverted, n + 1)
                        pool.tensor_tensor(probs[:, ring, :, :], probs[:, ring, :, :],
                                           rtotal[:, ring % 2, :].unsqueeze(2).to_broadcast([P, HH, SEQ]),
                                           ALU.mult).then_inc(weighted, 1)

                run(pool, step)

            @block.vector
            def _(dve):
                dve.memset(xT[HALF:HALF + 1, :, :, :], 1.0).then_inc(const_set, 1)
                dve.memset(qkT[HALF:P, :, :, :], 0.0).then_inc(const_set, 1)
                if not cos:
                    dve.memset(oT[HALF:HALF + 1, :, :, :], 1.0)
                dve.memset(vblk[:, :, :, :, :], 0.0).then_inc(const_set, 1)
                if cos:
                    dve.wait_ge(*loaded)
                    dve.tensor_scalar(scale_min[:, :], w["logit_scale"][:, :], LOGIT_SCALE_MAX, None, ALU.min).then_inc(capped, 1)
                    dve.memset(gain[:, HEADS:2 * HEADS], 1.0).then_inc(gain_set, 1)
                dve.wait_ge(const_set, 5)

                def step(i, u, active):
                    j, par, before, r = part(i, u, L_PV + 1)
                    if active(L_PV + 1) and r % 2:
                        t = r // 2
                        wait(dve, mixed, UPP * j + 2 * t + 2)
                        source = ps_o[0:HALF, 0:2 * P].rearrange("p (c t) -> p c t", c=2)
                        if cos:
                            dve.tensor_copy(big[0:HALF, :, bass.ds(P * (2 * j + t), P)], source).then_inc(o_ready, 1)
                        else:
                            wait(dve, projected, 2 * j + t - 1)
                            dve.tensor_copy(oT[0:HALF, t, :, :], source).then_inc(o_ready, 1)
                    if not cos:
                        j, par, before, r = part(i, u, L_PROJ + 1)
                        if active(L_PROJ + 1) and r % 2:
                            t = r // 2
                            wait(dve, projected, 2 * j + t + 1)
                            wait(dve, res_loaded[par], 16 * (before + 1))
                            wait(dve, stored[par], 16 * before)
                            if kind == "tok":
                                dve.tensor_tensor(outb[:, par, t, :], ps_r[:, 0:DIM], res[:, par, t, :], ALU.add).then_inc(out_ready, 1)
                            else:
                                dve.scalar_tensor_tensor(outb[:, par, t, :], ps_r[:, 0:DIM], res[:, par, t, DIM:DIM + 1],
                                                         res[:, par, t, 0:DIM], ALU.mult, ALU.add).then_inc(out_ready, 1)
                    j, par, before, r = part(i, u, 0)
                    if cos and active(0) and r == 1:
                        for t in range(2):
                            wait(dve, norm_ready, 2 * j + t + 1)
                            wait(dve, qkt, 2 * (j - 1) + t + 1 if not (isinstance(j, int) and j == 0) else 0)
                            dve.tensor_tensor(qkn[:, t, :].rearrange("p (h d) -> p h d", d=HD),
                                              ps_x[t][:, 0:2 * DIM].rearrange("p (h d) -> p h d", d=HD),
                                              qk_scale[:, t, :].unsqueeze(2).to_broadcast([P, 2 * HEADS, HD]),
                                              ALU.mult).then_inc(qkn_ready, 1)
                    if active(L_S):
                        n, ring = UPG * i + (u - L_S), (u - L_S) % 2
                        scores = ps_s[ring][:, 0:HH * SEQ].rearrange("p (h k) -> p h k", k=SEQ)
                        wait(dve, scored, n + 1)
                        dve.tensor_reduce(rowmax[:, ring, :], scores, AX, ALU.max).then_inc(maxed, 1)
                        wait(dve, maxed, n + 1)
                        wait(dve, exped, n - 1)
                        dve.tensor_tensor(shifted[:, ring, :, :], scores,
                                          rowmax[:, ring, :].unsqueeze(2).to_broadcast([P, HH, SEQ]), ALU.subtract).then_inc(shift_done, 1)
                    if active(L_SUM):
                        n, ring = UPG * i + (u - L_SUM), (u - L_SUM) % 2
                        wait(dve, exped, n + 1)
                        dve.tensor_reduce(total[:, ring, :], probs[:, (u - L_SUM) % 4, :, :], AX, ALU.add).then_inc(summed, 1)
                        wait(dve, summed, n + 1)
                        wait(dve, weighted, n - 1)
                        dve.reciprocal(rtotal[:, ring, :], total[:, ring, :]).then_inc(inverted, 1)
                    j, par, before, r = part(i, u, 0)
                    if cos and active(0) and r == 0:
                        for t in range(2):
                            wait(dve, squared, 2 * j + t + 1)
                            dve.tensor_reduce(norm2[:, t, :], square[:, t, :].rearrange("p (h d) -> p h d", d=HD), AX,
                                              ALU.add).then_inc(norm_summed, 1)
                        wait(dve, norm_summed, 2 * j + 2)
                        wait(dve, norm_inv, j)
                        dve.tensor_scalar(floor2[:, :, :], norm2[:, :, :], NORM_MIN2, None, ALU.max).then_inc(floored, 1)
                    if not cos and active(0) and r == 0:
                        wait(dve, k_mm, j + 1)
                        wait(dve, kmask_loaded[par], 16 * HH * before)
                        dve.tensor_copy(qkT[0:HALF, par, 2:4, :],
                                        ps_x[0][0:HALF, :].rearrange("p (c t) -> p c t", c=2)).then_inc(k_ready, 1)
                    j, par, before, r = part(i, u, L_V)
                    if active(L_V) and r == 0:
                        wait(dve, v_mm, j + 1)
                        wait(dve, mixed, UPP * (j - 1))
                        for odd in range(2):
                            last = dve.tensor_copy(vblk[span(odd, SEQ), par, :, :, span(odd, HD)],
                                                   ps_v[span(odd, SEQ), 0:4 * HALF].rearrange("p (a b d) -> p a b d", a=4, d=HD))
                        last.then_inc(v_ready, 1)

                run(dve, step)



def mlp_phase(nc, w, x2_dram, h_dram, big):
    with ExitStack() as ctx:
        mem = Memory(nc, ctx, "mlp")
        x2 = mem.sb("x2", [P, TILES, DIM])
        x2b = mem.sb("x2b", [P, TILES, DIM])
        xT = mem.sb("xT", [HALF + 1, 2, GROUP])
        hT = mem.sb("hT", [P, KM, GROUP])
        h = mem.sb("h", [P, TILES, DIM])
        stats = mem.sb("stats", [P, TILES, 6])
        mv = mem.sb("mv", [P, TILES, 2])
        vare = mem.sb("vare", [P, TILES])
        power = mem.sb("power", [P, TILES])
        rstd = mem.sb("rstd", [P, TILES])
        un = mem.sb("un", [P, TILES, DIM])
        ps_t = [mem.ps(f"ps_t{i}") for i in range(2)]
        ps_u = [mem.ps(f"ps_u{i}") for i in range(2)]
        ps_h = [mem.ps(f"ps_h{i}") for i in range(2)]
        ps_f = [mem.ps(f"ps_f{i}") for i in range(2)]
        const_set = mem.sem("const_set")
        x2_loaded = mem.sem("x2_loaded")
        biased = mem.sem("biased")
        turned = mem.sem("turned")
        xt_ready = mem.sem("xt_ready")
        hidden = mem.sem("hidden")
        gelued = mem.sem("gelued")
        summed = mem.sem("summed")
        added = mem.sem("added")
        counted, measured = mem.sem("counted"), mem.sem("measured")
        varied, rooted = mem.sem("varied"), mem.sem("rooted")
        normed = mem.sem("normed")
        u_turned = mem.sem("u_turned")
        u_ready = mem.sem("u_ready")
        h_stored = mem.sem("h_stored")

        with nc.Block() as block:

            @block.sync
            def _(sp):
                def turn(i, active):
                    if active(0):
                        waits(sp, (biased, i), (turned, 2 * i))
                        sp.dma_start(x2[:, :, :], x2_dram[i]).then_inc(x2_loaded, 16)
                    if active(1):
                        wait(sp, added, TILES * i)
                        sp.dma_start(h_dram[i - 1], h[:, :, :]).then_inc(h_stored, 16)

                sweep(sp, GROUPS, 2, turn)
                sp.wait_ge(h_stored, 16 * GROUPS)

            @block.tensor
            def _(pe):
                pe.wait_ge(const_set, 2)

                def turn(i, active):
                    if active(1):
                        wait(pe, xt_ready, 2 * i)
                        for k in range(KM):
                            wait(pe, gelued, KM * (i - 1) + k - 1)
                            layer(pe, ps_h[k % 2][:, :], [w["ff1"][0:HALF, 0, span(k, P)], w["ff1"][0:HALF + 1, 1, span(k, P)]],
                                  halves(xT, slice(0, GROUP))).then_inc(hidden, 1)
                    if active(2):
                        wait(pe, normed, i - 1)
                        for c in range(2):
                            wait(pe, u_ready, 2 * (i - 3) + c + 1 if not (isinstance(i, int) and i < 3) else 0)
                            for t in range(TILES):
                                last = pe.transpose(ps_u[c][0:HALF, span(t, P)], un[:, t, span(c, HALF)], w["ident"][:, :])
                            last.then_inc(u_turned, 1)
                    if active(0):
                        wait(pe, x2_loaded, 16 * (i + 1))
                        for c in range(2):
                            wait(pe, xt_ready, 2 * (i - 1) + c + 1 if not (isinstance(i, int) and i < 1) else 0)
                            for t in range(TILES):
                                last = pe.transpose(ps_t[c][0:HALF, span(t, P)], x2[:, t, span(c, HALF)], w["ident"][:, :])
                            last.then_inc(turned, 1)
                    if active(1):
                        wait(pe, gelued, KM * i)
                        for t in range(TILES):
                            wait(pe, added, TILES * (i - 1) + t - 1)
                            layer(pe, ps_f[t % 2][:, 0:DIM], [hT[:, k, span(t, P)] for k in range(KM)],
                                  [w["ff2"][:, k, :] for k in range(KM)]).then_inc(summed, 1)

                sweep(pe, GROUPS, 2, turn)

            @block.scalar
            def _(act):
                def turn(i, active):
                    if active(1):
                        for k in range(KM):
                            wait(act, hidden, KM * (i - 1) + k + 1)
                            wait(act, summed, TILES * (i - 1))
                            act.activation(hT[:, k, :], ps_h[k % 2][:, :], ACT.Gelu_apprx_tanh).then_inc(gelued, 1)
                    if active(2):
                        for c in range(2):
                            wait(act, u_turned, 2 * (i - 2) + c + 1)
                            columns = big[0:HALF, c, :].rearrange("p (n b) -> p b n", b=IMAGES)
                            act.activation(columns[:, bass.ds(8 * (i - 2), 8), :],
                                           ps_u[c][0:HALF, :].rearrange("p (b n) -> p b n", n=SEQ), ACT.Copy).then_inc(u_ready, 1)

                sweep(act, GROUPS, 2, turn)

            @block.gpsimd
            def _(pool):
                pool.memset(power[:, :], -0.5).then_inc(const_set, 1)
                pool.wait_ge(const_set, 2)

                def turn(i, active):
                    if active(1):
                        wait(pool, x2_loaded, 16 * i)
                        wait(pool, added, TILES * (i - 1))
                        pool.tensor_tensor(x2b[:, :, :], x2[:, :, :],
                                           w["ff2_b"][:, :].unsqueeze(1).to_broadcast([P, TILES, DIM]), ALU.add).then_inc(biased, 1)
                        wait(pool, varied, i)
                        pool.tensor_tensor(rstd[:, :], vare[:, :], power[:, :], ALU.pow).then_inc(rooted, 1)

                sweep(pool, GROUPS, 2, turn)

            @block.vector
            def _(dve):
                dve.memset(xT[HALF:HALF + 1, :, :], 1.0).then_inc(const_set, 1)

                def turn(i, active):
                    if active(0):
                        for c in range(2):
                            wait(dve, turned, 2 * i + c + 1)
                            wait(dve, hidden, KM * i)
                            dve.tensor_copy(xT[0:HALF, c, :], ps_t[c][0:HALF, :]).then_inc(xt_ready, 1)
                    if active(1):
                        wait(dve, biased, i)
                        wait(dve, h_stored, 16 * (i - 1))
                        for t in range(TILES):
                            n = TILES * (i - 1) + t + 1
                            wait(dve, summed, n)
                            dve.tensor_tensor(h[:, t, :], ps_f[t % 2][:, 0:DIM], x2b[:, t, :], ALU.add).then_inc(added, 1)
                            wait(dve, added, n)
                            dve.bn_stats(stats[:, t, :], h[:, t, :]).then_inc(counted, 1)
                            dve.drain()
                            dve.bn_aggr(mv[:, t, :], stats[:, t, :]).then_inc(measured, 1)
                        wait(dve, measured, TILES * i)
                        dve.tensor_scalar(vare[:, :], mv[:, :, 1], EPS, None, ALU.add).then_inc(varied, 1)
                        wait(dve, rooted, i)
                        wait(dve, u_turned, 2 * (i - 1))
                        for t in range(TILES):
                            last = dve.tensor_scalar(un[:, t, :], h[:, t, :], mv[:, t, 0:1], rstd[:, t:t + 1],
                                                     ALU.subtract, ALU.mult)
                        last.then_inc(normed, 1)

                sweep(dve, GROUPS, 2, turn)



def fold_phase(nc, w):
    jobs = (("r_in", "r_ln", RHD, 0), ("ffn_qkv", "ln1", 3 * DIM, RHD), ("fc1", "ln2", MLP, RHD + 3 * DIM))
    pieces = [(name, norm, a, min(a + 512, n), at) for name, norm, n, at in jobs for a in range(0, n, 512)]
    with ExitStack() as ctx:
        mem = Memory(nc, ctx, "fold")
        bias_row = mem.sb("bias_row", [1, RHD + 3 * DIM + MLP])
        banks = [mem.ps(f"bank{n}") for n in range(len(pieces))]
        shifted = mem.sem("shifted")
        rowed = mem.sem("rowed")
        scaled = mem.sem("scaled")
        placed = mem.sem("placed")
        with nc.Block() as block:

            @block.tensor
            def _(pe):
                pe.wait_ge(w["done"]["ffn"], w["counts"]["ffn"])
                for (name, norm, a, b, at), bank in zip(pieces, banks):
                    raw = w[name + "_raw"]
                    layer(pe, bank[0:1, 0:b - a], [w[norm + "_b"][:, c:c + 1] for c in range(2)],
                          [raw[:, c, a:b] for c in range(2)]).then_inc(shifted, 1)

            @block.vector
            def _(dve):
                dve.wait_ge(w["done"]["ffn"], w["counts"]["ffn"])
                dve.wait_ge(w["done"]["cos"], w["counts"]["cos"])
                for name, norm, n, at in jobs:
                    for c in range(2):
                        dve.tensor_scalar(w[name][0:HALF, c, :], w[name + "_raw"][:, c, :], w[norm + "_g"][:, c:c + 1], None,
                                          ALU.mult).then_inc(scaled, 1)
                for c in range(2):
                    dve.tensor_scalar(w["cos_proj"][0:HALF, c, :], w["cos_proj"][0:HALF, c, :], w["head_scale"][:, c:c + 1], None,
                                      ALU.mult).then_inc(scaled, 1)
                for n, (name, norm, a, b, at) in enumerate(pieces):
                    dve.wait_ge(shifted, n + 1)
                    dve.tensor_tensor(bias_row[0:1, at + a:at + b], banks[n][0:1, 0:b - a], w["fold_bias"][0:1, at + a:at + b],
                                      ALU.add).then_inc(rowed, 1)
                dve.wait_ge(scaled, 2 * len(jobs) + 2)

            @block.sync
            def _(sp):
                sp.wait_ge(rowed, len(pieces))
                for name, norm, n, at in jobs:
                    sp.dma_start(w[name][HALF:HALF + 1, 1, :], bias_row[0:1, at:at + n]).then_inc(placed, 16)
                sp.wait_ge(placed, 16 * len(jobs))



def router_phase(nc, w, big, h_dram, h4_dram, z_dram, bits_dram, zn_dram):
    with ExitStack() as ctx:
        mem = Memory(nc, ctx, "router")
        oT = mem.sb("oT", [HALF + 1, 2, GROUP])
        h = mem.sb("h", [P, TILES, DIM])
        h4 = mem.sb("h4", [P, TILES, DIM])
        stats = mem.sb("stats", [P, TILES, 6])
        mv = mem.sb("mv", [P, TILES, 2])
        vare = mem.sb("vare", [P, TILES])
        power = mem.sb("power", [P, TILES])
        rstd = mem.sb("rstd", [P, TILES])
        varz = mem.sb("varz", [P, TILES])
        varz2 = mem.sb("varz2", [P, TILES])
        varz3 = mem.sb("varz3", [P, TILES])
        rz = mem.sb("rz", [P, TILES])
        z = mem.sb("z", [P, TILES, DIM])
        zn = mem.sb("zn", [P, TILES, DIM])
        znT = mem.sb("znT", [HALF + 1, 2, GROUP])
        eT = mem.sb("eT", [P, GROUP])
        esum = mem.sb("esum", [P, 8])
        emean = mem.sb("emean", [P, 8])
        h1 = mem.sb("h1", [P, GROUP])
        h2 = mem.sb("h2", [RH2 + 1, GROUP])
        logits = mem.sb("logits", [P, TILES, 2 * BITS])
        beat = mem.sb("beat", [P, TILES, BITS])
        both = mem.sb("both", [P, TILES])
        route = mem.sb("route", [P, TILES, 8])
        ps_a = [mem.ps(f"ps_a{i}") for i in range(2)]
        ps_t = [mem.ps(f"ps_t{i}") for i in range(2)]
        ps_e, ps_1, ps_2, ps_l = (mem.ps(f"ps_{x}") for x in "e12l")
        const_set = mem.sem("const_set")
        h_loaded = mem.sem("h_loaded")
        o_ready = mem.sem("o_ready")
        projected = mem.sem("projected")
        added = mem.sem("added")
        counted, measured = mem.sem("counted"), mem.sem("measured")
        varied = mem.sem("varied")
        rooted = mem.sem("rooted")
        var_step = mem.sem("var_step")
        z_rooted = mem.sem("z_rooted")
        z_ready = mem.sem("z_ready")
        zn_ready = mem.sem("zn_ready")
        turned = mem.sem("turned")
        znt_ready = mem.sem("znt_ready")
        e_mm, e_ready = mem.sem("e_mm"), mem.sem("e_ready")
        e_summed, mean_ready = mem.sem("e_summed"), mem.sem("mean_ready")
        h1_mm, h1_ready = mem.sem("h1_mm"), mem.sem("h1_ready")
        h2_mm, h2_ready = mem.sem("h2_mm"), mem.sem("h2_ready")
        l_mm = mem.sem("l_mm")
        route_step = mem.sem("route_step")
        h4_stored, z_stored, zn_stored, bits_stored = (mem.sem(x) for x in ("h4_stored", "z_stored", "zn_stored", "bits_stored"))
        RS = 7

        with nc.Block() as block:

            @block.sync
            def _(sp):
                def turn(i, active):
                    if active(0):
                        wait(sp, added, TILES * i)
                        sp.dma_start(h[:, :, :], h_dram[i]).then_inc(h_loaded, 16)
                    if active(1):
                        wait(sp, added, TILES * i)
                        sp.dma_start(h4_dram[i - 1], h4[:, :, :]).then_inc(h4_stored, 16)
                        wait(sp, z_ready, TILES * i)
                        sp.dma_start(z_dram[i - 1], z[:, :, :]).then_inc(z_stored, 16)
                    if active(2):
                        wait(sp, znt_ready, 2 * (i - 1))
                        for a in range(2):
                            sp.dma_start(zn_dram[2 * (i - 2) + a], znT[0:HALF, :, span(a, PART)]).then_inc(zn_stored, 16)
                    if active(3):
                        wait(sp, route_step, RS * (i - 2))
                        sp.dma_start(bits_dram[i - 3], route[:, :, :]).then_inc(bits_stored, 16)

                sweep(sp, GROUPS, 3, turn)
                sp.wait_ge(h4_stored, 16 * GROUPS)
                sp.wait_ge(z_stored, 16 * GROUPS)
                sp.wait_ge(zn_stored, 32 * GROUPS)
                sp.wait_ge(bits_stored, 16 * GROUPS)

            @block.tensor
            def _(pe):
                pe.wait_ge(const_set, 5)

                def turn(i, active):
                    if active(3):
                        wait(pe, mean_ready, i - 2)
                        wait(pe, h1_ready, i - 3)
                        layer(pe, ps_1[:, :].rearrange("p (b n) -> p b n", n=SEQ), [w["r_o1"][:, 0, :], w["r_o1"][:, 1, :]],
                              [eT[:, :].rearrange("p (b n) -> p b n", n=SEQ),
                               emean[:, :].unsqueeze(2).to_broadcast([P, 8, SEQ])]).then_inc(h1_mm, 1)
                    if active(1):
                        wait(pe, o_ready, 2 * i)
                        for t in range(TILES):
                            wait(pe, added, TILES * (i - 1) + t - 1)
                            layer(pe, ps_a[t % 2][:, 0:DIM], halves(oT, span(t, P)),
                                  [w["cos_proj"][0:HALF, 0, :], w["cos_proj"][0:HALF + 1, 1, :]]).then_inc(projected, 1)
                    if active(3):
                        wait(pe, h1_ready, i - 2)
                        wait(pe, h2_ready, i - 3)
                        pe.matmul(ps_2[0:RH2, :], w["r_o2"][:, :], h1[:, :], start=True, stop=True).then_inc(h2_mm, 1)
                    if active(2):
                        wait(pe, zn_ready, i - 1)
                        for c in range(2):
                            wait(pe, znt_ready, 2 * (i - 3) + c + 1 if not (isinstance(i, int) and i < 3) else 0)
                            for t in range(TILES):
                                last = pe.transpose(ps_t[c][0:HALF, span(t, P)], zn[:, t, span(c, HALF)], w["ident"][:, :])
                            last.then_inc(turned, 1)
                    if active(3):
                        wait(pe, h2_ready, i - 2)
                        wait(pe, route_step, RS * (i - 3))
                        for t in range(TILES):
                            last = pe.matmul(ps_l[:, span(t, 2 * BITS)], h2[:, span(t, P)], w["r_o3"][:, :], start=True, stop=True)
                        last.then_inc(l_mm, 1)
                    if active(2):
                        wait(pe, znt_ready, 2 * (i - 1))
                        wait(pe, e_ready, i - 2)
                        layer(pe, ps_e[:, :], [w["r_in"][0:HALF, 0, :], w["r_in"][0:HALF + 1, 1, :]],
                              halves(znT, slice(0, GROUP))).then_inc(e_mm, 1)

                sweep(pe, GROUPS, 3, turn)

            @block.scalar
            def _(act):
                def turn(i, active):
                    if active(3):
                        wait(act, h1_mm, i - 2)
                        wait(act, h2_mm, i - 3)
                        act.activation(h1[:, :], ps_1[:, :], ACT.Gelu, bias=w["r_o1_b"][:, 0:1]).then_inc(h1_ready, 1)
                    if active(0):
                        wait(act, projected, TILES * i)
                        for c in range(2):
                            columns = big[0:HALF, c, :].rearrange("p (n b) -> p b n", b=IMAGES)
                            act.activation(oT[0:HALF, c, :].rearrange("p (b n) -> p b n", n=SEQ), columns[:, bass.ds(8 * i, 8), :],
                                           ACT.Copy).then_inc(o_ready, 1)
                    if active(3):
                        wait(act, h2_mm, i - 2)
                        wait(act, l_mm, i - 3)
                        act.activation(h2[0:RH2, :], ps_2[0:RH2, :], ACT.Gelu, bias=w["r_o2_b"][:, 0:1]).then_inc(h2_ready, 1)
                    if active(2):
                        for c in range(2):
                            wait(act, turned, 2 * (i - 2) + c + 1)
                            wait(act, e_mm, i - 2)
                            wait(act, zn_stored, 32 * (i - 2))
                            act.activation(znT[0:HALF, c, :], ps_t[c][0:HALF, :], ACT.Copy).then_inc(znt_ready, 1)
                        wait(act, e_mm, i - 1)
                        wait(act, h1_mm, i - 2)
                        act.activation(eT[:, :], ps_e[:, :], ACT.Gelu).then_inc(e_ready, 1)

                sweep(act, GROUPS, 3, turn)

            @block.gpsimd
            def _(pool):
                pool.memset(power[:, :], -0.5).then_inc(const_set, 1)
                pool.wait_ge(const_set, 5)

                def turn(i, active):
                    if active(1):
                        wait(pool, varied, i)
                        pool.tensor_tensor(rstd[:, :], vare[:, :], power[:, :], ALU.pow).then_inc(rooted, 1)
                        wait(pool, var_step, 3 * i)
                        pool.tensor_tensor(rz[:, :], varz3[:, :], power[:, :], ALU.pow).then_inc(z_rooted, 1)

                sweep(pool, GROUPS, 3, turn)

            @block.vector
            def _(dve):
                dve.memset(oT[HALF:HALF + 1, :, :], 1.0).then_inc(const_set, 1)
                dve.memset(znT[HALF:HALF + 1, :, :], 1.0).then_inc(const_set, 1)
                dve.memset(h2[RH2:RH2 + 1, :], 1.0).then_inc(const_set, 1)
                dve.memset(route[:, :, :], 0.0).then_inc(const_set, 1)
                dve.wait_ge(const_set, 5)

                def turn(i, active):
                    if active(1):
                        wait(dve, h_loaded, 16 * i)
                        wait(dve, h4_stored, 16 * (i - 1))
                        for t in range(TILES):
                            n = TILES * (i - 1) + t + 1
                            wait(dve, projected, n)
                            dve.tensor_tensor(h4[:, t, :], ps_a[t % 2][:, 0:DIM], h[:, t, :], ALU.add).then_inc(added, 1)
                            wait(dve, added, n)
                            dve.bn_stats(stats[:, t, :], h4[:, t, :]).then_inc(counted, 1)
                            dve.drain()
                            dve.bn_aggr(mv[:, t, :], stats[:, t, :]).then_inc(measured, 1)
                        wait(dve, measured, TILES * i)
                        dve.tensor_scalar(vare[:, :], mv[:, :, 1], EPS, None, ALU.add).then_inc(varied, 1)
                        wait(dve, rooted, i)
                        dve.tensor_tensor(varz[:, :], mv[:, :, 1], rstd[:, :], ALU.mult).then_inc(var_step, 1)
                        wait(dve, var_step, 3 * (i - 1) + 1)
                        dve.tensor_tensor(varz2[:, :], varz[:, :], rstd[:, :], ALU.mult).then_inc(var_step, 1)
                        wait(dve, var_step, 3 * (i - 1) + 2)
                        dve.tensor_scalar(varz3[:, :], varz2[:, :], EPS, None, ALU.add).then_inc(var_step, 1)
                        wait(dve, z_stored, 16 * (i - 1))
                        for t in range(TILES):
                            dve.tensor_scalar(z[:, t, :], h4[:, t, :], mv[:, t, 0:1], rstd[:, t:t + 1],
                                              ALU.subtract, ALU.mult).then_inc(z_ready, 1)
                        wait(dve, z_rooted, i)
                        wait(dve, z_ready, TILES * i)
                        wait(dve, turned, 2 * (i - 1))
                        for t in range(TILES):
                            last = dve.tensor_scalar(zn[:, t, :], z[:, t, :], rz[:, t:t + 1], None, ALU.mult)
                        last.then_inc(zn_ready, 1)
                    if active(3):
                        n = RS * (i - 3)
                        wait(dve, l_mm, i - 2)
                        wait(dve, bits_stored, 16 * (i - 3))
                        dve.tensor_copy(logits[:, :, :], ps_l[:, 0:TILES * 2 * BITS].rearrange("p (t l) -> p t l", t=TILES)).then_inc(route_step, 1)
                        wait(dve, route_step, n + 1)
                        pairs = logits[:, :, :].rearrange("p t (b l) -> p t b l", l=2)
                        dve.tensor_tensor(beat[:, :, :], pairs[:, :, :, 1], pairs[:, :, :, 0], ALU.is_gt).then_inc(route_step, 1)
                        wait(dve, route_step, n + 2)
                        dve.tensor_scalar(route[:, :, 0:BITS], beat[:, :, :], w["first_token"][:, 0:1], None, ALU.max).then_inc(route_step, 1)
                        wait(dve, route_step, n + 3)
                        dve.tensor_tensor(both[:, :], route[:, :, 0], route[:, :, 1], ALU.mult).then_inc(route_step, 1)
                        wait(dve, route_step, n + 4)
                        dve.tensor_tensor(route[:, :, 3], route[:, :, 1], both[:, :], ALU.subtract).then_inc(route_step, 1)
                        dve.tensor_tensor(route[:, :, 4], route[:, :, 0], both[:, :], ALU.subtract).then_inc(route_step, 1)
                        dve.scalar_tensor_tensor(beat[:, :, 0], route[:, :, 0], -1.0, route[:, :, 1], ALU.mult, ALU.subtract).then_inc(select_step, 1)
                        wait(dve, select_step, 2 * (i - 3) + 1)
                        dve.scalar_tensor_tensor(beat[:, :, 1], beat[:, :, 0], 1.0, both[:, :], ALU.add, ALU.add).then_inc(select_step, 1)
                        wait(dve, select_step, 2 * (i - 3) + 2)
                        dve.tensor_copy(route[:, :, 2], beat[:, :, 1]).then_inc(route_step, 1)
                    if active(2):
                        wait(dve, e_ready, i - 1)
                        dve.tensor_reduce(esum[:, :], eT[:, :].rearrange("p (b n) -> p b n", n=SEQ)[:, :, 1:SEQ], AX, ALU.add).then_inc(e_summed, 1)
                        wait(dve, e_summed, i - 1)
                        wait(dve, h1_mm, i - 2)
                        dve.tensor_scalar(emean[:, :], esum[:, :], 1.0 / (SEQ - 1), None, ALU.mult).then_inc(mean_ready, 1)

                select_step = mem.sem("select_step")
                sweep(dve, GROUPS, 3, turn)



def last_phase(nc, w, h5_dram, bits_dram, h4_dram, out_dram):
    with ExitStack() as ctx:
        mem = Memory(nc, ctx, "last")
        h5 = mem.sb("h5", [P, TILES, DIM])
        h5r = mem.sb("h5r", [P, TILES, DIM])
        bits = mem.sb("bits", [P, TILES, 8])
        h4 = mem.sb("h4", [P, TILES, DIM])
        select = mem.sb("select", [P, TILES, 8])
        stats = mem.sb("stats", [P, TILES, 6])
        mv = mem.sb("mv", [P, TILES, 2])
        vare = mem.sb("vare", [P, TILES])
        power = mem.sb("power", [P, TILES])
        rstd = mem.sb("rstd", [P, TILES])
        xn = mem.sb("xn", [P, TILES, DIM])
        xT = mem.sb("xT", [HALF + 1, 2, GROUP])
        hT = mem.sb("hT", [P, KM, GROUP])
        ffb = mem.sb("ffb", [P, 2, DIM])
        out = mem.sb("out", [P, TILES, DIM])
        outT = mem.sb("outT", [HALF, 2, GROUP])
        down = mem.sb("down", [P, TILES, RANK3])
        downT = mem.sb("downT", [HALF, 2, GROUP])
        base = mem.sb("base", [P, TILES, DIM])
        fin = mem.sb("fin", [P, TILES, DIM])
        ps_t = [mem.ps(f"ps_t{i}") for i in range(2)]
        ps_h = [mem.ps(f"ps_h{i}") for i in range(2)]
        ps_f = [mem.ps(f"ps_f{i}") for i in range(2)]
        ps_d = [mem.ps(f"ps_d{i}") for i in range(2)]
        const_set = mem.sem("const_set")
        h5_loaded, r_loaded, s_loaded = mem.sem("h5_loaded"), mem.sem("r_loaded"), mem.sem("s_loaded")
        counted, measured = mem.sem("counted"), mem.sem("measured")
        varied, rooted = mem.sem("varied"), mem.sem("rooted")
        normed = mem.sem("normed")
        turned = mem.sem("turned")
        xt_ready = mem.sem("xt_ready")
        hidden, gelued = mem.sem("hidden"), mem.sem("gelued")
        summed = mem.sem("summed")
        biased = mem.sem("biased")
        out_ready = mem.sem("out_ready")
        o_turned, ot_ready = mem.sem("o_turned"), mem.sem("ot_ready")
        downed, down_ready = mem.sem("downed"), mem.sem("down_ready")
        d_turned, dt_ready = mem.sem("d_turned"), mem.sem("dt_ready")
        upped = mem.sem("upped")
        based = mem.sem("based")
        fin_ready = mem.sem("fin_ready")
        stored = mem.sem("stored")

        with nc.Block() as block:

            @block.sync
            def _(sp):
                def turn(i, active):
                    if active(0):
                        wait(sp, normed, i)
                        sp.dma_start(h5[:, :, :], h5_dram[i]).then_inc(h5_loaded, 16)
                    if active(1):
                        wait(sp, out_ready, TILES * (i - 1))
                        sp.dma_start(h5r[:, :, :], h5_dram[i - 1]).then_inc(r_loaded, 16)
                        sp.dma_start(bits[:, :, :], bits_dram[i - 1]).then_inc(r_loaded, 16)
                    if active(2):
                        waits(sp, (based, i - 2), (down_ready, TILES * (i - 2)))
                        sp.dma_start(h4[:, :, :], h4_dram[i - 2]).then_inc(s_loaded, 16)
                        sp.dma_start(select[:, :, :], bits_dram[i - 2]).then_inc(s_loaded, 16)
                    if active(3):
                        wait(sp, fin_ready, TILES * (i - 2))
                        sp.dma_start(out_dram[i - 3], fin[:, :, :]).then_inc(stored, 16)

                sweep(sp, GROUPS, 3, turn)
                sp.wait_ge(stored, 16 * GROUPS)

            @block.tensor
            def _(pe):
                pe.wait_ge(const_set, 2)

                def transposes(source, into, rows=HALF):
                    for c in range(2):
                        for t in range(TILES):
                            last = pe.transpose(ps_t[c][0:rows, span(t, P)], source[:, t, span(c, HALF)], w["ident"][:, :])
                        last.then_inc(into, 1)

                def second(i, t):
                    wait(pe, biased, TILES * (i - 2) + t - 1)
                    layer(pe, ps_f[t % 2][:, 0:DIM], [hT[:, k, span(t, P)] for k in range(KM)],
                          [w["fc2"][:, k, :] for k in range(KM)]).then_inc(summed, 1)

                def turn(i, active):
                    if active(2):
                        wait(pe, xt_ready, 2 * (i - 1))
                        for k in range(KM):
                            wait(pe, gelued, KM * (i - 2) + k - 1)
                            layer(pe, ps_h[k % 2][:, :], [w["fc1"][0:HALF, 0, span(k, P)], w["fc1"][0:HALF + 1, 1, span(k, P)]],
                                  halves(xT, slice(0, GROUP))).then_inc(hidden, 1)
                    if active(3):
                        wait(pe, out_ready, TILES * (i - 2))
                        wait(pe, dt_ready, 2 * (i - 3))
                        wait(pe, xt_ready, 2 * (i - 1) if not isinstance(i, int) else 2 * min(i - 1, GROUPS))
                        transposes(out, o_turned)
                    if active(1):
                        wait(pe, normed, i)
                        wait(pe, ot_ready, 2 * (i - 2))
                        if isinstance(i, int):
                            wait(pe, dt_ready, 2 * (i - 3))
                        transposes(xn, turned)
                    if active(3):
                        wait(pe, ot_ready, 2 * (i - 2))
                        for t in range(TILES):
                            n = TILES * (i - 3) + t
                            if t < 2:
                                wait(pe, fin_ready, n - t)
                            else:
                                wait(pe, down_ready, n - 1)
                            layer(pe, ps_d[t % 2][:, 0:RANK3], [outT[:, c, span(t, P)] for c in range(2)],
                                  [w["lra_down"][:, c, :] for c in range(2)]).then_inc(downed, 1)
                    if active(2):
                        wait(pe, gelued, KM * (i - 1))
                        second(i, 0)
                        second(i, 1)
                    if active(3):
                        wait(pe, down_ready, TILES * (i - 2))
                        wait(pe, xt_ready, 2 * i if not isinstance(i, int) else 2 * min(i, GROUPS))
                        transposes(down, d_turned)
                    if active(2):
                        second(i, 2)
                        second(i, 3)
                    if active(3):
                        wait(pe, dt_ready, 2 * (i - 2))
                        for t in range(TILES):
                            if t >= 2:
                                wait(pe, fin_ready, TILES * (i - 3) + t - 1)
                            layer(pe, ps_d[t % 2][:, 0:DIM], [downT[:, c, span(t, P)] for c in range(2)],
                                  [w["lra_up"][:, c, :] for c in range(2)]).then_inc(upped, 1)

                sweep(pe, GROUPS, 3, turn)

            @block.scalar
            def _(act):
                def turn(i, active):
                    if active(2):
                        for k in range(KM):
                            wait(act, hidden, KM * (i - 2) + k + 1)
                            wait(act, summed, TILES * (i - 2))
                            act.activation(hT[:, k, :], ps_h[k % 2][:, :], ACT.Gelu).then_inc(gelued, 1)
                    if active(3):
                        for c in range(2):
                            wait(act, o_turned, 2 * (i - 3) + c + 1)
                            wait(act, downed, TILES * (i - 3))
                            act.activation(outT[:, c, :], ps_t[c][0:HALF, :], ACT.Copy).then_inc(ot_ready, 1)
                        for c in range(2):
                            wait(act, d_turned, 2 * (i - 3) + c + 1)
                            wait(act, upped, TILES * (i - 3))
                            act.activation(downT[:, c, :], ps_t[c][0:HALF, :], ACT.Copy).then_inc(dt_ready, 1)

                sweep(act, GROUPS, 3, turn)

            @block.gpsimd
            def _(pool):
                pool.memset(power[:, :], -0.5).then_inc(const_set, 1)
                pool.wait_ge(const_set, 2)

                def turn(i, active):
                    if active(1):
                        wait(pool, varied, i)
                        pool.tensor_tensor(rstd[:, :], vare[:, :], power[:, :], ALU.pow).then_inc(rooted, 1)
                    if active(3):
                        wait(pool, s_loaded, 32 * (i - 2))
                        wait(pool, out_ready, TILES * (i - 2))
                        wait(pool, fin_ready, TILES * (i - 3))
                        pool.tensor_tensor(base[:, :, :], h4[:, :, :], out[:, :, :], ALU.add).then_inc(based, 1)

                sweep(pool, GROUPS, 3, turn)

            @block.vector
            def _(dve):
                dve.memset(xT[HALF:HALF + 1, :, :], 1.0).then_inc(const_set, 1)

                def turn(i, active):
                    if active(1):
                        wait(dve, h5_loaded, 16 * i)
                        for t in range(TILES):
                            n = TILES * (i - 1) + t + 1
                            dve.bn_stats(stats[:, t, :], h5[:, t, :]).then_inc(counted, 1)
                            dve.drain()
                            dve.bn_aggr(mv[:, t, :], stats[:, t, :]).then_inc(measured, 1)
                        wait(dve, measured, TILES * i)
                        dve.tensor_scalar(vare[:, :], mv[:, :, 1], EPS, None, ALU.add).then_inc(varied, 1)
                        wait(dve, rooted, i)
                        wait(dve, turned, 2 * (i - 1))
                        for t in range(TILES):
                            last = dve.tensor_scalar(xn[:, t, :], h5[:, t, :], mv[:, t, 0:1], rstd[:, t:t + 1],
                                                     ALU.subtract, ALU.mult)
                        last.then_inc(normed, 1)
                        for c in range(2):
                            wait(dve, turned, 2 * (i - 1) + c + 1)
                            wait(dve, hidden, KM * (i - 1))
                            dve.tensor_copy(xT[0:HALF, c, :], ps_t[c][0:HALF, :]).then_inc(xt_ready, 1)
                    if active(3):
                        wait(dve, s_loaded, 32 * (i - 2))
                        for t in range(TILES):
                            wait(dve, downed, TILES * (i - 3) + t + 1)
                            if t == 0:
                                wait(dve, d_turned, 2 * (i - 3))
                            dve.tensor_tensor(down[:, t, :].rearrange("p (k r) -> p k r", k=3),
                                              ps_d[t % 2][:, 0:RANK3].rearrange("p (k r) -> p k r", k=3),
                                              select[:, t, 2:5].unsqueeze(2).to_broadcast([P, 3, RANK3 // 3]),
                                              ALU.mult).then_inc(down_ready, 1)

                    def add_bits(i, t):
                        n = TILES * (i - 2) + t + 1
                        wait(dve, summed, n)
                        dve.tensor_tensor(ffb[:, t % 2, :], ps_f[t % 2][:, 0:DIM], w["fc2_b"][:, :], ALU.add).then_inc(biased, 1)
                        wait(dve, biased, n)
                        if t == 0:
                            wait(dve, r_loaded, 32 * (i - 1))
                            wait(dve, o_turned, 2 * (i - 2))
                            wait(dve, based, i - 2)
                        dve.scalar_tensor_tensor(out[:, t, :], ffb[:, t % 2, :], bits[:, t, 1:2], h5r[:, t, :],
                                                 ALU.mult, ALU.add).then_inc(out_ready, 1)

                    if active(2):
                        for t in range(TILES):
                            add_bits(i, t)
                    if active(3):
                        wait(dve, based, i - 2)
                        wait(dve, stored, 16 * (i - 3))
                        for t in range(TILES):
                            wait(dve, upped, TILES * (i - 3) + t + 1)
                            dve.tensor_tensor(fin[:, t, :], ps_d[t % 2][:, 0:DIM], base[:, t, :], ALU.add).then_inc(fin_ready, 1)

                sweep(dve, GROUPS, 3, turn)



def vit_tower(nc, ins, out, scratch):
    tiles4 = lambda x: x.rearrange("(g t) p f -> g p t f", t=TILES)
    tiles2 = lambda x: x.rearrange("(g t) p f -> g p t f", t=2)
    s = scratch
    with ExitStack() as ctx:
        mem = Memory(nc, ctx, "weights")
        w = {}
        load_weights(nc, mem, w, ins)
        for name, cols in (("r_in", RHD), ("ffn_qkv", 3 * DIM), ("fc1", MLP)):
            w[name] = mem.sb(name, [HALF + 1, 2, cols])
        patch_phase(nc, w, ins["patches"], tiles4(s["x1"]), s["y"])
        attention_phase(nc, w, "tok", lambda j: s["y"][j], tiles2(s["x1"]), tiles2(s["x2"]), None)
        with nc.sbuf_tensor("by_token", [HALF, 2, TOKENS], F32) as big:
            mlp_phase(nc, w, tiles4(s["x2"]), tiles4(s["h"]), big)
            attention_phase(nc, w, "cos", lambda j: big[0:HALF, :, bass.ds(PART * j, PART)], None, None, big)
            fold_phase(nc, w)
            router_phase(nc, w, big, tiles4(s["h"]), tiles4(s["h4"]), tiles4(s["zb"])[:, :, :, 0:DIM],
                         tiles4(s["zb"])[:, :, :, DIM:ROW], s["zn"])
        attention_phase(nc, w, "ffn", lambda j: s["zn"][j], tiles2(s["zb"]), tiles2(s["h5"]), None)
        last_phase(nc, w, tiles4(s["h5"]), tiles4(s["zb"])[:, :, :, DIM:ROW], tiles4(s["h4"]), tiles4(out))


SCRATCH = {"x1": (TOKENS // P, P, DIM), "x2": (TOKENS // P, P, DIM), "h": (TOKENS // P, P, DIM), "h4": (TOKENS // P, P, DIM),
           "h5": (TOKENS // P, P, DIM), "zb": (TOKENS // P, P, ROW), "y": (PARTS, HALF, 2, PART), "zn": (PARTS, HALF, 2, PART)}


NORMS = ("ffn_r_ln_g", "ffn_r_ln_b", "ffn_ln1_g", "ffn_ln1_b", "ffn_ln2_g", "ffn_ln2_b")
COLUMNS = {"tok_ff2_b": HALF, "head_scale": HALF, "ffn_r_o1_b": RHD, "ffn_r_o2_b": RH2, **dict.fromkeys(NORMS, HALF)}
UNSPREAD = [k for k in COLUMNS if k != "tok_ff2_b"]


def positions():
    pos = np.arange(SEQ, dtype=np.float32)[:, None]
    i = np.arange(DIM // 2, dtype=np.float32)[None, :]
    angle = (pos / np.power(np.float32(10000.0), np.float32(2.0) * i / np.float32(DIM))).astype(np.float32)
    pe = np.zeros((SEQ, DIM), np.float32)
    pe[:, 0::2], pe[:, 1::2] = np.sin(angle), np.cos(angle)
    return pe


def lay_out(inputs):
    x = {k.replace("L0_", ""): np.asarray(v) for k, v in inputs.items()}
    side = x["x"].shape[2] // PATCH
    tokens = x["x"].reshape(IMAGES, CHANNELS, side, PATCH, side, PATCH).transpose(1, 3, 5, 0, 2, 4).reshape(KP, P, GROUPS, GROUP)

    def qkv(wt):
        v = wt[..., 2 * DIM:].reshape(*wt.shape[:-1], HEADS // 2, 2, HD)
        v = np.swapaxes(v, -3, -2).reshape(*wt.shape[:-1], DIM)
        return np.concatenate([wt[..., :2 * DIM], v], axis=-1)

    a = {
        "patches": tokens.transpose(2, 1, 0, 3),
        "patch_w": x["tok_patch_w"].reshape(DIM, FEATS).T,
        "pe": np.concatenate([positions()] * 2),
        "ident": np.eye(P, dtype=np.float32),
        "first_token": (np.arange(P) % SEQ == 0).astype(np.float32)[:, None],
        "tok_qkv_w": qkv(x["tok_qkv_w"]), "tok_qkv_b": qkv(x["tok_qkv_b"]),
        "cos_qkv_w": qkv(x["attn_in_proj_weight"].T), "cos_qkv_b": qkv(x["attn_in_proj_bias"]),
        "cos_proj_w": x["attn_out_w"].T,
        "logit_scale": x["attn_logit_scale"].reshape(HEADS),
        "head_scale": np.repeat(x["attn_head_scale"].reshape(HEADS), HD),
        "ffn_qkv_w": qkv(np.concatenate([x["ffn_wq"].T, x["ffn_wk"].T, x["ffn_wv"].T], axis=1)),
        "ffn_qkv_b": qkv(np.concatenate([x["ffn_bq"], x["ffn_bk"], x["ffn_bv"]])),
        "ffn_proj_w": x["ffn_wo"].T, "r_in_w": x["ffn_r_in_w"].T, "r_o1_w": x["ffn_r_o1_w"].T,
        "r_o2_w": x["ffn_r_o2_w"].T, "r_o3_w": x["ffn_r_o3_w"].T,
        "fc1_w": x["ffn_fc1_w"].T, "fc2_w": x["ffn_fc2_w"].T,
        "lra_down": x["ffn_lra_down"].reshape(RANK3, DIM).T,
        "lra_up": x["ffn_lra_up"].transpose(0, 2, 1).reshape(RANK3, DIM),
    }
    for key in ("tok_patch_b", "tok_ln_g", "tok_ln_b", "tok_ff1_w", "tok_ff1_b", "tok_ff2_w", "tok_ff2_b", "tok_proj_w", "tok_proj_b",
                "attn_out_b", "ffn_bo", "ffn_fc1_b", "ffn_fc2_b", "ffn_r_in_b", "ffn_r_o1_b", "ffn_r_o2_b", "ffn_r_o3_b",
                "ffn_r_ln_g", "ffn_r_ln_b", "ffn_ln1_g", "ffn_ln1_b", "ffn_ln2_g", "ffn_ln2_b"):
        a[key] = x[key]
    for key, rows in COLUMNS.items():
        a[key + "_col"] = a[key].reshape(-1, rows).T
    for key in UNSPREAD:
        del a[key]
    return {k: np.ascontiguousarray(v) for k, v in a.items()}


def kernel(**inputs):
    import concourse.bacc as bacc
    from concourse.bass_utils import run_bass_kernel_spmd

    arrays = lay_out(inputs)
    nc = bacc.Bacc("TRN2", target_bir_lowering=False, num_devices=1)
    ins = {k: nc.dram_tensor(f"in_{k}", v.shape, mybir.dt.from_np(v.dtype), kind="ExternalInput").ap() for k, v in arrays.items()}
    out = nc.dram_tensor("out", (TOKENS // P, P, DIM), F32, kind="ExternalOutput").ap()
    scratch = {k: nc.dram_tensor(f"scratch_{k}", shape, F32, kind="Internal").ap() for k, shape in SCRATCH.items()}
    vit_tower(nc, ins, out, scratch)
    r = run_bass_kernel_spmd(nc, [{f"in_{k}": v for k, v in arrays.items()}], core_ids=[0])
    return r.results[0]["out"].reshape(IMAGES, SEQ, DIM)
```

```python
from contextlib import ExitStack

import numpy as np

import concourse.bass as bass
from concourse import mybir

F32 = mybir.dt.float32
F32R = mybir.dt.float32r
I32 = mybir.dt.int32
ALU = mybir.AluOpType
ACT = mybir.ActivationFunctionType
AX = mybir.AxisListType.X

IMAGES, SEQ, DIM, HEADS, MLP = 64, 64, 192, 12, 768
PATCH, CHANNELS = 16, 3
FEATS = CHANNELS * PATCH * PATCH
P = 128
HALF = DIM // 2
HD = DIM // HEADS
HH = HEADS // 2
TOKENS = IMAGES * SEQ
GROUP = 512
TILES = GROUP // P
GROUPS = TOKENS // GROUP
KP = FEATS // P
KM = MLP // P
PART = 256
PARTS = TOKENS // PART
UNITS = 2 * TOKENS // P
UPP = 2 * PART // P
UPG = 8
RHD, RH2, BITS = 128, 64, 2
RANK3 = 192
ROW = DIM + 8
EPS = 1e-5
LOGIT_SCALE_MAX = float(np.log(100.0))
NORM_MIN2 = 1e-24
HIGH_BITS = -(1 << 12)
RSQRT_BITS = 0x5F3759DF


def sweep(engine, turns, lags, body):
    for i in range(lags + 1):
        body(i, lambda lag, i=i: 0 <= i - lag < turns)
    with engine.Fori(lags + 1, turns) as i:
        body(i, lambda lag: True)
    for i in range(turns, turns + lags):
        body(i, lambda lag, i=i: 0 <= i - lag < turns)


def sweep_pairs(engine, turns, lags, body):
    for i in range(2):
        body(i, i, lambda lag, i=i: 0 <= i - lag < turns)
    with engine.Fori(1, turns // 2) as pair:
        for a in range(2):
            body(2 * pair + a, a, lambda lag: True)
    for i in range(turns, turns + lags):
        body(i, i % 2, lambda lag, i=i: 0 <= i - lag < turns)


def wait(engine, sem, value):
    if isinstance(value, int) and value <= 0:
        return
    engine.wait_ge(sem, value)


def waits(engine, *pairs):
    values = [v for _, v in pairs]
    for v in values:
        if not isinstance(v, int):
            engine.compute_val(v)
    for (sem, _), value in zip(pairs, values):
        wait(engine, sem, value)


class Memory:

    def __init__(self, nc, ctx, phase):
        self.nc, self.ctx, self.phase, self.held = nc, ctx, phase, []
        ctx.callback(self.clear)

    def clear(self):
        self.nc.clear_and_free_semaphores(self.held)
        self.nc.all_engine_barrier()

    def sb(self, name, shape, dtype=F32):
        return self.ctx.enter_context(self.nc.sbuf_tensor(f"{self.phase}_{name}", shape, dtype))

    def ps(self, name, shape=(P, 512)):
        return self.ctx.enter_context(self.nc.psum_tensor(f"{self.phase}_{name}", list(shape), F32))

    def sem(self, name):
        self.held.append(self.nc.alloc_semaphore(f"{self.phase}_{name}"))
        return self.held[-1]

    def sems(self, name, n):
        return [self.sem(f"{name}{i}") for i in range(n)]


def load_weights(nc, mem, w, ins):
    done = {k: mem.sem(f"loaded_{k}") for k in ("patch", "ff", "tok", "cos", "ffn")}
    counts = dict.fromkeys(done, 0)
    plan = {k: [] for k in done}

    def take(which, dst, src):
        plan[which].append((dst, src))
        counts[which] += 16

    def chunked(which, name, key, rows, chunks, cols, bias=None):
        w[name] = mem.sb(name, [rows + (bias is not None), chunks, cols])
        take(which, w[name][0:rows, :, :], ins[key].rearrange("(c p) n -> p c n", p=rows))
        if bias:
            take(which, w[name][rows:rows + 1, chunks - 1, :], ins[bias].rearrange("(a n) -> a n", a=1))

    def column(which, name, key, rows, chunks):
        w[name] = mem.sb(name, [rows, chunks])
        take(which, w[name][:, :], ins[key + "_col"])

    def spread(which, name, key, cols):
        w[name] = mem.sb(name, [P, cols])
        take(which, w[name][:, :], ins[key].rearrange("(a n) -> a n", a=1).to_broadcast([P, cols]))

    def plain(which, name, key, rows, cols):
        w[name] = mem.sb(name, [rows, cols])
        take(which, w[name][:, :], ins[key])

    chunked("patch", "patch_w", "patch_w", P, KP, DIM)
    spread("patch", "patch_b", "tok_patch_b", DIM)
    spread("patch", "ln_g", "tok_ln_g", DIM)
    spread("patch", "ln_b", "tok_ln_b", DIM)
    plain("patch", "pe", "pe", P, DIM)
    plain("patch", "ident", "ident", P, P)
    chunked("ff", "ff1", "tok_ff1_w", HALF, 2, MLP, "tok_ff1_b")
    chunked("ff", "ff2", "tok_ff2_w", P, KM, DIM)
    column("ff", "ff2_col", "tok_ff2_b", HALF, 2)
    spread("ff", "ff2_b", "tok_ff2_b", DIM)
    chunked("tok", "tok_qkv", "tok_qkv_w", HALF, 2, 3 * DIM, "tok_qkv_b")
    chunked("tok", "tok_proj", "tok_proj_w", HALF, 2, DIM, "tok_proj_b")
    chunked("cos", "cos_qkv", "cos_qkv_w", HALF, 2, 3 * DIM, "cos_qkv_b")
    chunked("cos", "cos_proj", "cos_proj_w", HALF, 2, DIM, "attn_out_b")
    spread("cos", "logit_scale", "logit_scale", HEADS)
    column("cos", "head_scale", "head_scale", HALF, 2)
    plain("ffn", "first_token", "first_token", P, 1)
    chunked("ffn", "r_in_raw", "r_in_w", HALF, 2, RHD)
    chunked("ffn", "ffn_qkv_raw", "ffn_qkv_w", HALF, 2, 3 * DIM)
    chunked("ffn", "fc1_raw", "fc1_w", HALF, 2, MLP)
    chunked("ffn", "ffn_proj", "ffn_proj_w", HALF, 2, DIM, "ffn_bo")
    chunked("ffn", "fc2", "fc2_w", P, KM, DIM)
    spread("ffn", "fc2_b", "ffn_fc2_b", DIM)
    chunked("ffn", "r_o1", "r_o1_w", RHD, 2, RHD)
    column("ffn", "r_o1_b", "ffn_r_o1_b", RHD, 1)
    plain("ffn", "r_o2", "r_o2_w", RHD, RH2)
    column("ffn", "r_o2_b", "ffn_r_o2_b", RH2, 1)
    w["r_o3"] = mem.sb("r_o3", [RH2 + 1, 2 * BITS])
    take("ffn", w["r_o3"][0:RH2, :], ins["r_o3_w"])
    take("ffn", w["r_o3"][RH2:RH2 + 1, :], ins["ffn_r_o3_b"].rearrange("(a n) -> a n", a=1))
    chunked("ffn", "lra_down", "lra_down", HALF, 2, RANK3)
    chunked("ffn", "lra_up", "lra_up", HALF, 2, DIM)
    for name in ("r_ln_g", "r_ln_b", "ln1_g", "ln1_b", "ln2_g", "ln2_b"):
        column("ffn", name, "ffn_" + name, HALF, 2)
    w["fold_bias"] = mem.sb("fold_bias", [1, RHD + 3 * DIM + MLP])
    for at, key, n in ((0, "ffn_r_in_b", RHD), (RHD, "ffn_qkv_b", 3 * DIM), (RHD + 3 * DIM, "ffn_fc1_b", MLP)):
        take("ffn", w["fold_bias"][0:1, at:at + n], ins[key].rearrange("(a n) -> a n", a=1))
    w["done"], w["counts"], w["plan"] = done, counts, plan


def start_loads(engine, w, which):
    for dst, src in w["plan"][which]:
        engine.dma_start(dst, src).then_inc(w["done"][which], 16)


def layer(pe, out, lhs, rhs):
    for n, (a, b) in enumerate(zip(lhs, rhs)):
        last = pe.matmul(out, a, b, start=(n == 0), stop=(n == len(lhs) - 1))
    return last


def split_layer(pe, out, lhs, rhs):
    pairs = [(a[m], b[n]) for a, b in zip(lhs, rhs) for m, n in ((0, 0), (0, 1), (1, 0))]
    for n, (a, b) in enumerate(pairs):
        last = pe.matmul(out, a, b, start=(n == 0), stop=(n == len(pairs) - 1))
    return last


def split(dve, x, masked, high, low, steps, n):
    dve.tensor_scalar(masked.bitcast(I32), x.bitcast(I32), HIGH_BITS, None, ALU.bitwise_and).then_inc(steps, 1)
    wait(dve, steps, n + 1)
    dve.tensor_copy(high, masked).then_inc(steps, 1)
    return dve.tensor_tensor(low, x, masked, ALU.subtract)


def split_weights(dve, w, name, steps):
    for c in range(2):
        last = split(dve, *(w[x][0:HALF + c, c, :] for x in (name, "masked", f"{name}_high", f"{name}_low")), steps, 2 * c)
    return last


def split_chunk(high, low, k):
    return [(high[0:HALF + c, c, span(k, P)], low[0:HALF + c, c, span(k, P)]) for c in range(2)]


def split_halves(x):
    return [(x[0:HALF + c, 0, c, :], x[0:HALF + c, 1, c, :]) for c in range(2)]


def halves(x, cols):
    return [x[0:HALF, 0, cols], x[0:HALF + 1, 1, cols]]


def span(n, size):
    return slice(n * size, (n + 1) * size)



def patch_phase(nc, w, patches, x1_dram, y_dram):
    with ExitStack() as ctx:
        mem = Memory(nc, ctx, "patch")
        raw = mem.sb("raw", [P, 2, KP, GROUP])
        xr = mem.sb("xr", [P, TILES, DIM])
        stats = mem.sb("stats", [P, TILES, 6])
        mv = mem.sb("mv", [P, TILES, 2])
        vare = mem.sb("vare", [P, TILES])
        power = mem.sb("power", [P, TILES])
        rstd = mem.sb("rstd", [P, TILES])
        posb = mem.sb("posb", [P, DIM])
        xn = mem.sb("xn", [P, TILES, DIM])
        xg = mem.sb("xg", [P, TILES, DIM])
        x1 = mem.sb("x1", [P, TILES, DIM])
        xm = mem.sb("xm", [HALF, GROUP])
        xT = mem.sb("xT", [HALF + 1, 2, 2, GROUP], F32R)
        hT = mem.sb("hT", [P, KM, GROUP])
        yT = mem.sb("yT", [HALF, 2, GROUP])
        ps_patch = [mem.ps(f"ps_patch{i}") for i in range(2)]
        ps_t = [mem.ps(f"ps_t{i}") for i in range(2)]
        ps_h = [mem.ps(f"ps_h{i}") for i in range(2)]
        ps_y = [mem.ps(f"ps_y{i}") for i in range(2)]

        raw_loaded = mem.sems("raw_loaded", 2)
        const_set = mem.sem("const_set")
        posb_set = mem.sem("posb_set")
        patched = mem.sem("patched")
        evacuated = mem.sem("evacuated")
        counted = mem.sem("counted")
        measured = mem.sem("measured")
        varied = mem.sem("varied")
        rooted = mem.sem("rooted")
        normed = mem.sem("normed")
        gained = mem.sem("gained")
        placed = mem.sem("placed")
        turned = mem.sem("turned")
        weight_step = mem.sem("weight_step")
        weight_split = mem.sem("weight_split")
        xt_step = mem.sem("xt_step")
        xt_ready = mem.sem("xt_ready")
        hidden = mem.sem("hidden")
        gelued = mem.sem("gelued")
        y_summed = mem.sem("y_summed")
        y_ready = mem.sem("y_ready")
        x1_stored = mem.sem("x1_stored")
        y_stored = mem.sem("y_stored")

        with nc.Block() as block:

            @block.sync
            def _(sp):
                start_loads(sp, w, "patch")
                sp.dma_start(raw[:, 0, :, :], patches[0]).then_inc(raw_loaded[0], 16)
                start_loads(sp, w, "ff")

                def turn(i, par, active):
                    if active(0) and not (isinstance(i, int) and i == 0):
                        wait(sp, patched, TILES * (i - 1))
                        sp.dma_start(raw[:, par, :, :], patches[i]).then_inc(raw_loaded[par], 16)
                    if isinstance(i, int) and i == 1:
                        for which in ("tok", "cos", "ffn"):
                            start_loads(sp, w, which)
                    if active(1):
                        wait(sp, placed, TILES * i)
                        sp.dma_start(x1_dram[i - 1], x1[:, :, :]).then_inc(x1_stored, 16)

                sweep_pairs(sp, GROUPS, 1, turn)
                sp.wait_ge(x1_stored, 16 * GROUPS)
                sp.wait_ge(y_stored, 32 * GROUPS)

            @block.tensor
            def _(pe):
                pe.wait_ge(w["done"]["patch"], w["counts"]["patch"])
                pe.wait_ge(const_set, 2)

                def turn(i, par, active):
                    if active(1):
                        wait(pe, placed, TILES * i)
                        for c in range(2):
                            wait(pe, xt_ready, 2 * (i - 2) + c + 1 if not (isinstance(i, int) and i < 2) else 0)
                            for t in range(TILES):
                                last = pe.transpose(ps_t[c][0:HALF, span(t, P)], x1[:, t, span(c, HALF)], w["ident"][:, :])
                            last.then_inc(turned, 1)
                    if active(0):
                        wait(pe, raw_loaded[par], 16 * (i // 2 + 1) if isinstance(i, int) else 8 * (i - par) + 16)
                        for t in range(TILES):
                            wait(pe, evacuated, TILES * i + t - 1)
                            layer(pe, ps_patch[t % 2][:, 0:DIM],
                                  [raw[:, par, k, span(t, P)] for k in range(KP)],
                                  [w["patch_w"][:, k, :] for k in range(KP)]).then_inc(patched, 1)
                    if active(1):
                        wait(pe, w["done"]["ff"], w["counts"]["ff"])
                        wait(pe, weight_split, 1)
                        wait(pe, xt_ready, 2 * i)
                        for k in range(KM):
                            wait(pe, gelued, KM * (i - 1) + k - 1)
                            split_layer(pe, ps_h[k % 2][:, :], split_chunk(w["ff1_high"], w["ff1_low"], k), split_halves(xT)).then_inc(hidden, 1)
                        for m in range(2):
                            wait(pe, y_ready, 2 * (i - 1) + m - 1)
                            for k in range(KM):
                                if m == 0:
                                    wait(pe, gelued, KM * (i - 1) + k + 1)
                                last = pe.matmul(ps_y[m][0:HALF, :], w["ff2"][:, k, span(m, HALF)], hT[:, k, :],
                                                 start=(k == 0), stop=(k == KM - 1))
                            last.then_inc(y_summed, 1)

                sweep_pairs(pe, GROUPS, 1, turn)

            @block.scalar
            def _(act):
                act.wait_ge(w["done"]["ff"], w["counts"]["ff"])

                def turn(i, par, active):
                    if active(1):
                        for k in range(KM):
                            wait(act, hidden, KM * (i - 1) + k + 1)
                            act.activation(hT[:, k, :], ps_h[k % 2][:, :], ACT.Gelu_apprx_tanh).then_inc(gelued, 1)
                        for m in range(2):
                            wait(act, y_summed, 2 * (i - 1) + m + 1)
                            wait(act, y_stored, 32 * (i - 1))
                            act.activation(yT[:, m, :], ps_y[m][0:HALF, :], ACT.Identity,
                                           bias=w["ff2_col"][:, m:m + 1]).then_inc(y_ready, 1)
                        wait(act, y_ready, 2 * i)
                        for a in range(2):
                            act.dma_start(y_dram[2 * (i - 1) + a], yT[:, :, span(a, PART)]).then_inc(y_stored, 16)

                sweep_pairs(act, GROUPS, 1, turn)

            @block.gpsimd
            def _(pool):
                pool.memset(power[:, :], -0.5).then_inc(const_set, 1)
                pool.wait_ge(w["done"]["patch"], w["counts"]["patch"])
                pool.tensor_tensor(posb[:, :], w["ln_b"][:, :], w["pe"][:, :], ALU.add).then_inc(posb_set, 1)
                pool.wait_ge(const_set, 2)
                pool.wait_ge(posb_set, 1)

                def turn(i, par, active):
                    if active(0):
                        wait(pool, varied, i + 1)
                        pool.tensor_tensor(rstd[:, :], vare[:, :], power[:, :], ALU.pow).then_inc(rooted, 1)
                        for t in range(TILES):
                            wait(pool, normed, TILES * i + t + 1)
                            pool.tensor_tensor(xg[:, t, :], xn[:, t, :], w["ln_g"][:, :], ALU.mult).then_inc(gained, 1)
                        wait(pool, x1_stored, 16 * i)
                        wait(pool, turned, 2 * i)
                        for t in range(TILES):
                            wait(pool, gained, TILES * i + t + 1)
                            pool.tensor_tensor(x1[:, t, :], xg[:, t, :], posb[:, :], ALU.add).then_inc(placed, 1)

                sweep_pairs(pool, GROUPS, 1, turn)

            @block.vector
            def _(dve):
                dve.memset(xT[HALF:HALF + 1, 0, :, :].bitcast(F32), 1.0)
                dve.memset(xT[HALF:HALF + 1, 1, :, :].bitcast(F32), 0.0).then_inc(const_set, 1)
                dve.wait_ge(w["done"]["patch"], w["counts"]["patch"])

                def turn(i, par, active):
                    if active(1):
                        for c in range(2):
                            wait(dve, turned, 2 * (i - 1) + c + 1)
                            wait(dve, hidden, KM * (i - 1))
                            wait(dve, xt_ready, 2 * (i - 1) + c)
                            split(dve, ps_t[c][0:HALF, :], xm[:, :], xT[0:HALF, 0, c, :], xT[0:HALF, 1, c, :],
                                  xt_step, 4 * (i - 1) + 2 * c).then_inc(xt_ready, 1)
                    if active(0):
                        for t in range(TILES):
                            wait(dve, patched, TILES * i + t + 1)
                            dve.tensor_tensor(xr[:, t, :], ps_patch[t % 2][:, 0:DIM], w["patch_b"][:, :], ALU.add).then_inc(evacuated, 1)
                            wait(dve, evacuated, TILES * i + t + 1)
                            dve.bn_stats(stats[:, t, :], xr[:, t, :]).then_inc(counted, 1)
                            dve.drain()
                            dve.bn_aggr(mv[:, t, :], stats[:, t, :]).then_inc(measured, 1)
                        wait(dve, measured, TILES * i + TILES)
                        dve.tensor_scalar(vare[:, :], mv[:, :, 1], EPS, None, ALU.add).then_inc(varied, 1)
                        wait(dve, rooted, i + 1)
                        wait(dve, gained, TILES * i)
                        for t in range(TILES):
                            dve.tensor_scalar(xn[:, t, :], xr[:, t, :], mv[:, t, 0:1], rstd[:, t:t + 1],
                                              ALU.subtract, ALU.mult).then_inc(normed, 1)
                    if isinstance(i, int) and i == 0:
                        dve.wait_ge(w["done"]["ff"], w["counts"]["ff"])
                        split_weights(dve, w, "ff1", weight_step).then_inc(weight_split, 1)

                sweep_pairs(dve, GROUPS, 1, turn)



def attention_phase(nc, w, kind, x_src, res_dram, out_dram, big):
    cos = kind == "cos"
    qkv_w = w[{"tok": "tok_qkv", "cos": "cos_qkv", "ffn": "ffn_qkv"}[kind]]
    proj_w = w[{"tok": "tok_proj", "cos": "cos_proj", "ffn": "ffn_proj"}[kind]]
    loaded = w["done"][kind], w["counts"][kind]
    L_S, L_V, L_VCOPY = (9, 6, 8) if cos else (4, 5, 5)
    L_SUM, L_T, L_PV = L_S + 1, L_S + 3, L_S + 4
    L_PROJ = L_PV + 1
    L_N = 6
    row = ROW if kind == "ffn" else DIM
    score_scale = 1.0 if cos else float(HD) ** -0.5
    Q0, K0, V0 = 0, DIM, 2 * DIM

    with ExitStack() as ctx:
        mem = Memory(nc, ctx, kind)
        xT = mem.sb("xT", [HALF + 1, 2, 2, PART])
        qkT = mem.sb("qkT", [P, 2, 4, PART])
        kmask = mem.sb("kmask", [P, 2, 2, HH, PART])
        vblk = mem.sb("vblk", [P, 2, 4, HH, 2 * HD])
        rowmax = mem.sb("rowmax", [P, 2, HH])
        shifted = mem.sb("shifted", [P, 2, HH, SEQ])
        probs = mem.sb("probs", [P, 4, HH, SEQ])
        total = mem.sb("total", [P, 2, HH])
        rtotal = mem.sb("rtotal", [P, 2, HH])
        probsT = mem.sb("probsT", [P, 2, 3, P])
        if cos:
            qk = mem.sb("qk", [P, 2, 2 * DIM])
            square = mem.sb("square", [P, 2, 2 * DIM])
            norm2 = mem.sb("norm2", [P, 2, 2 * HEADS])
            floor2 = mem.sb("floor2", [P, 2, 2 * HEADS])
            rnorm = mem.sb("rnorm", [P, 2, 2 * HEADS])
            half_sq = mem.sb("half_sq", [P, 2, 2 * HEADS])
            product = mem.sb("product", [P, 2, 2 * HEADS])
            squares = mem.sb("squares", [P, 2, 2 * HEADS])
            parts = mem.sb("parts", [P, 2, 2 * HEADS])
            factor = mem.sb("factor", [P, 2, 2 * HEADS])
            minus_half = mem.sb("minus_half", [P, 2, 2 * HEADS])
            three_halves = mem.sb("three_halves", [P, 2, 2 * HEADS])
            scaled = mem.sb("scaled", [P, 2, 2 * HEADS])
            qk_scale = mem.sb("qk_scale", [P, 2, 2 * HEADS])
            scale_min = mem.sb("scale_min", [P, HEADS])
            gain = mem.sb("gain", [P, 2 * HEADS])
            qkn = mem.sb("qkn", [P, 2, 2 * DIM])
        else:
            oT = mem.sb("oT", [HALF + 1, 2, 2, P])
            res = mem.sb("res", [P, 2, 2, row])
            outb = mem.sb("outb", [P, 2, 2, DIM])
        ps_s = [mem.ps(f"ps_s{i}") for i in range(2)]
        ps_pt = [mem.ps(f"ps_pt{i}") for i in range(2)]
        ps_o = mem.ps("ps_o")
        ps_x = [mem.ps(f"ps_x{i}") for i in range(2)]
        ps_r = mem.ps("ps_r")
        ps_v = ps_r if cos else ps_x[0]

        const_set = mem.sem("const_set")
        x_loaded = mem.sems("x_loaded", 2)
        v_mm, v_ready = mem.sem("v_mm"), mem.sem("v_ready")
        kmask_loaded = mem.sems("kmask_loaded", 2)
        scored = mem.sem("scored")
        maxed = mem.sem("maxed")
        shift_done = mem.sem("shift_done")
        exped = mem.sem("exped")
        summed = mem.sem("summed")
        inverted = mem.sem("inverted")
        weighted = mem.sem("weighted")
        turned = mem.sem("turned")
        pt_ready = mem.sem("pt_ready")
        mixed = mem.sem("mixed")
        o_ready = mem.sem("o_ready")
        if cos:
            qk_mm = mem.sem("qk_mm")
            squared = mem.sem("squared")
            qk_copied = mem.sem("qk_copied")
            norm_summed = mem.sem("norm_summed")
            floored = mem.sem("floored")
            guessed = mem.sem("guessed")
            refined = mem.sem("refined")
            newton = mem.sem("newton")
            qkn_ready = mem.sem("qkn_ready")
            qkt = mem.sem("qkt")
            qk_ready = mem.sem("qk_ready")
            capped, gain_set = mem.sem("capped"), mem.sem("gain_set")
            RS, NS = 8, 4
        else:
            k_mm, q_mm = mem.sem("k_mm"), mem.sem("q_mm")
            k_ready, q_ready = mem.sem("k_ready"), mem.sem("q_ready")
            projected = mem.sem("projected")
            out_ready = mem.sem("out_ready")
            res_loaded = mem.sems("res_loaded", 2)
            stored = mem.sems("stored", 2)

        def part(i, u, lag):
            q, r = divmod(u - lag, UPP)
            return 2 * i + q, q % 2, i + q // 2, r

        def run(engine, step, peeled=0):
            turns = UNITS // UPG
            for i in range(2):
                for u in range(UPG):
                    step(i, u, lambda lag, i=i, u=u: 0 <= i * UPG + u - lag < UNITS)
            with engine.Fori(2, turns - peeled) as i:
                for u in range(UPG):
                    step(i, u, lambda lag: True)
            for i in range(turns - peeled, turns + 2):
                for u in range(UPG):
                    step(i, u, lambda lag, i=i, u=u: 0 <= i * UPG + u - lag < UNITS)

        with nc.Block() as block:

            @block.sync
            def _(sp):
                def load(j, par):
                    wait(sp, v_mm, j - 1)
                    sp.dma_start(xT[0:HALF, par, :, :], x_src(j)).then_inc(x_loaded[par], 16)

                def load_res(j, par):
                    wait(sp, out_ready, 2 * (j - 1))
                    sp.dma_start(res[:, par, :, :], res_dram[j]).then_inc(res_loaded[par], 16)

                for j in range(2):
                    load(j, j)
                    if not cos:
                        load_res(j, j)
                sp.wait_ge(const_set, 5)

                def step(i, u, active):
                    lag, at = (7, 0) if cos else (0, 1)
                    j, par, _, r = part(i, u, lag)
                    if active(lag) and r == at:
                        waits(sp, (qk_ready if cos else k_ready, 2 * j + 2 if cos else j + 1), (scored, UPP * (j - 1)))
                        for h in range(HH):
                            rows = span(h, HD)
                            sp.dma_start(kmask[rows, par, :, h, :], qkT[rows, par, 2:4, :]).then_inc(kmask_loaded[par], 16)
                    if not cos:
                        j, par, _, r = part(i, u, L_PROJ + 1)
                        if active(L_PROJ + 1) and r == UPP - 1:
                            wait(sp, out_ready, 2 * (j + 1))
                            sp.dma_start(out_dram[j], outb[:, par, :, :]).then_inc(stored[par], 16)
                            if not (isinstance(j, int) and j + 2 >= PARTS):
                                load_res(j + 2, par)
                    j, par, _, r = part(i, u, L_V)
                    if active(L_V) and r == 0 and not (isinstance(j, int) and j + 2 >= PARTS):
                        load(j + 2, par)

                run(sp, step, peeled=1)
                if not cos:
                    for s in stored:
                        sp.wait_ge(s, 16 * PARTS // 2)

            @block.tensor
            def _(pe):
                pe.wait_ge(*loaded)
                pe.wait_ge(const_set, 5)

                def project_part(out, cols, par, into):
                    for m in range(2):
                        c0 = cols + m * HALF
                        last = layer(pe, out[0:HALF, span(m, PART)],
                                     [qkv_w[0:HALF, 0, c0:c0 + HALF], qkv_w[0:HALF + 1, 1, c0:c0 + HALF]],
                                     [xT[0:HALF, par, 0, :], xT[0:HALF + 1, par, 1, :]])
                    last.then_inc(into, 1)

                def step(i, u, active):
                    if active(L_S):
                        n, (j, par, before, r) = UPG * i + (u - L_S), part(i, u, L_S)
                        c, t, ring = r % 2, r // 2, (u - L_S) % 2
                        if r == 0:
                            wait(pe, kmask_loaded[par], 16 * HH * (before + 1))
                            wait(pe, qk_ready if cos else q_ready, 2 * j + 2 if cos else j + 1)
                        wait(pe, shift_done, n - 1)
                        for a in range(2):
                            cols = slice(t * P + a * SEQ, t * P + (a + 1) * SEQ)
                            last = pe.matmul(ps_s[ring][span(a, SEQ), 0:HH * SEQ], qkT[:, par, c, cols],
                                             kmask[:, par, c, :, cols], start=True, stop=True)
                        last.then_inc(scored, 1)
                    if active(L_T):
                        n, ring = UPG * i + (u - L_T), (u - L_T) % 2
                        wait(pe, weighted, n + 1)
                        wait(pe, pt_ready, n - 1)
                        for b in range(3):
                            last = pe.transpose(ps_pt[ring][:, span(b, P)],
                                                probs[:, (u - L_T) % 4, 2 * b:2 * b + 2, :].rearrange("p h k -> p (h k)"),
                                                w["ident"][:, :])
                        last.then_inc(turned, 1)
                    j, par, before, r = part(i, u, L_N)
                    if cos and active(L_N) and r == 0:
                        for t in range(2):
                            wait(pe, qkn_ready, 2 * j + t + 1)
                            wait(pe, qk_copied, 2 * min(j + 1, PARTS - 1) + t + 1 if isinstance(j, int) else 2 * (j + 1) + t + 1)
                            for m in range(4):
                                last = pe.transpose(ps_x[t][0:HALF, span(m, P)], qkn[:, t, span(m, HALF)], w["ident"][:, :])
                            last.then_inc(qkt, 1)
                    j, par, before, r = part(i, u, 0)
                    if active(0) and not cos and r == 0:
                        wait(pe, x_loaded[par], 16 * (before + 1))
                        wait(pe, v_ready, j - 1)
                        project_part(ps_x[0], K0, par, k_mm)
                    if active(0) and not cos and r == 1:
                        wait(pe, q_ready, j)
                        project_part(ps_x[1], Q0, par, q_mm)
                    j, par, before, r = part(i, u, L_V)
                    if active(L_V) and r == 0:
                        if cos:
                            wait(pe, v_ready, j)
                        else:
                            wait(pe, k_ready, min(j + 2, PARTS) if isinstance(j, int) else j + 2)
                        for a in range(4):
                            for odd in range(2):
                                c0 = V0 + odd * HALF
                                last = layer(pe, ps_v[span(odd, SEQ), span(a, HALF)],
                                             [xT[0:HALF, par, 0, span(a, SEQ)], xT[0:HALF + 1, par, 1, span(a, SEQ)]],
                                             [qkv_w[0:HALF, 0, c0:c0 + HALF], qkv_w[0:HALF + 1, 1, c0:c0 + HALF]])
                        last.then_inc(v_mm, 1)
                    if active(L_PV):
                        n, (j, par, before, r) = UPG * i + (u - L_PV), part(i, u, L_PV)
                        c, t, ring = r % 2, r // 2, (u - L_PV) % 2
                        if r == 0:
                            wait(pe, v_ready, j + 1)
                        wait(pe, pt_ready, n + 1)
                        if c == 0:
                            wait(pe, o_ready, 2 * j + t)
                        for a in range(2):
                            for b in range(3):
                                last = pe.matmul(ps_o[span(b, 2 * HD), c * P + a * SEQ:c * P + (a + 1) * SEQ],
                                                 vblk[:, par, 2 * t + a, 3 * c + b, :], probsT[:, ring, b, span(a, SEQ)],
                                                 start=True, stop=True)
                        last.then_inc(mixed, 1)
                    j, par, before, r = part(i, u, 0)
                    if active(0) and cos and r == 0:
                        wait(pe, x_loaded[par], 16 * (before + 1))
                        for t in range(2):
                            wait(pe, qk_ready, 2 * (j - 2) + t + 1 if not (isinstance(j, int) and j < 2) else 0)
                            wait(pe, qk_copied, 2 * (j - 1) + t + 1 if not (isinstance(j, int) and j < 1) else 0)
                            layer(pe, ps_x[t][:, 0:2 * DIM], [xT[0:HALF, par, 0, span(t, P)], xT[0:HALF + 1, par, 1, span(t, P)]],
                                  [qkv_w[0:HALF, 0, 0:2 * DIM], qkv_w[0:HALF + 1, 1, 0:2 * DIM]]).then_inc(qk_mm, 1)
                    if not cos and active(L_PROJ):
                        j, par, before, r = part(i, u, L_PROJ)
                        if r % 2:
                            t = r // 2
                            wait(pe, o_ready, 2 * j + t + 1)
                            wait(pe, out_ready, 2 * j + t)
                            layer(pe, ps_r[:, 0:DIM], [oT[0:HALF, t, 0, :], oT[0:HALF + 1, t, 1, :]],
                                  [proj_w[0:HALF, 0, :], proj_w[0:HALF + 1, 1, :]]).then_inc(projected, 1)

                run(pe, step)

            @block.scalar
            def _(act):
                if cos:
                    act.wait_ge(capped, 1)
                    act.activation(gain[:, 0:HEADS], scale_min[:, :], ACT.Exp).then_inc(gain_set, 1)

                def step(i, u, active):
                    j, par, before, r = part(i, u, L_PV + 1)
                    if active(L_PV + 1) and r % 2:
                        t = r // 2
                        wait(act, mixed, UPP * j + 2 * t + 2)
                        source = ps_o[0:HALF, 0:2 * P].rearrange("p (c t) -> p c t", c=2)
                        if cos:
                            act.activation(big[0:HALF, :, bass.ds(P * (2 * j + t), P)], source, ACT.Copy).then_inc(o_ready, 1)
                        else:
                            wait(act, projected, 2 * j + t - 1)
                            act.activation(oT[0:HALF, t, :, :], source, ACT.Copy).then_inc(o_ready, 1)
                    j, par, before, r = part(i, u, 0)
                    if active(0) and cos and r == 1:
                        for t in range(2):
                            wait(act, qk_mm, 2 * j + t + 1)
                            wait(act, norm_summed, 2 * (j - 1) + t + 1 if not (isinstance(j, int) and j == 0) else 0)
                            act.activation(square[:, t, :], ps_x[t][:, 0:2 * DIM], ACT.Square).then_inc(squared, 1)
                            wait(act, qkn_ready, 2 * (j - 1) + t + 1 if not (isinstance(j, int) and j == 0) else 0)
                            act.activation(qk[:, t, :], ps_x[t][:, 0:2 * DIM], ACT.Copy).then_inc(qk_copied, 1)
                    if active(L_T):
                        n, ring = UPG * i + (u - L_T), (u - L_T) % 2
                        wait(act, turned, n + 1)
                        wait(act, mixed, n - 1)
                        act.activation(probsT[:, ring, :, :].rearrange("p b q -> p (b q)"), ps_pt[ring][:, 0:3 * P],
                                       ACT.Copy).then_inc(pt_ready, 1)
                    if active(L_S):
                        n = UPG * i + (u - L_S)
                        wait(act, shift_done, n + 1)
                        wait(act, turned, n - 3)
                        act.activation(probs[:, (u - L_S) % 4, :, :], shifted[:, (u - L_S) % 2, :, :], ACT.Exp,
                                       scale=score_scale).then_inc(exped, 1)
                    j, par, before, r = part(i, u, 0)
                    if active(0) and not cos and r == 1:
                        wait(act, q_mm, j + 1)
                        wait(act, scored, UPP * (j - 1))
                        act.activation(qkT[0:HALF, par, 0:2, :], ps_x[1][0:HALF, :].rearrange("p (c t) -> p c t", c=2),
                                       ACT.Copy).then_inc(q_ready, 1)
                    j, par, before, r = part(i, u, L_N)
                    if cos and active(L_N) and r == 0:
                        for t in range(2):
                            wait(act, qkt, 2 * j + t + 1)
                            if t == 0:
                                wait(act, scored, UPP * (j - 1))
                                wait(act, kmask_loaded[par], 16 * HH * before)
                            act.activation(qkT[0:HALF, par, :, span(t, P)],
                                           ps_x[t][0:HALF, :].rearrange("p (c t) -> p c t", c=4), ACT.Copy).then_inc(qk_ready, 1)
                    j, par, before, r = part(i, u, L_VCOPY)
                    if active(L_VCOPY) and r == 0:
                        wait(act, v_mm, j + 1)
                        wait(act, mixed, UPP * (j - 1))
                        for odd in range(2):
                            last = act.activation(vblk[span(odd, SEQ), par, :, :, span(odd, HD)],
                                                   ps_v[span(odd, SEQ), 0:4 * HALF].rearrange("p (a b d) -> p a b d", a=4, d=HD),
                                                  ACT.Copy)
                        last.then_inc(v_ready, 1)

                run(act, step)

            @block.gpsimd
            def _(pool):
                pool.memset(kmask[:, 0, :, :, :], 0.0).then_inc(const_set, 1)
                pool.memset(kmask[:, 1, :, :, :], 0.0).then_inc(const_set, 1)

                if cos:
                    pool.wait_ge(gain_set, 2)

                def newton_step(n):
                    pool.tensor_tensor(squares[:, :, :], rnorm[:, :, :], rnorm[:, :, :], ALU.mult).then_inc(refined, 1)
                    wait(pool, refined, n + 1)
                    pool.tensor_tensor(parts[:, :, :], squares[:, :, :], minus_half[:, :, :], ALU.mult).then_inc(refined, 1)
                    wait(pool, refined, n + 2)
                    pool.tensor_tensor(factor[:, :, :], parts[:, :, :], three_halves[:, :, :], ALU.add).then_inc(refined, 1)
                    wait(pool, refined, n + 3)
                    pool.tensor_tensor(rnorm[:, :, :], rnorm[:, :, :], factor[:, :, :], ALU.mult).then_inc(refined, 1)

                def step(i, u, active):
                    if active(L_SUM):
                        n, ring = UPG * i + (u - L_SUM), (u - L_SUM) % 4
                        wait(pool, inverted, n + 1)
                        pool.tensor_tensor(probs[:, ring, :, :], probs[:, ring, :, :],
                                           rtotal[:, ring % 2, :].unsqueeze(2).to_broadcast([P, HH, SEQ]),
                                           ALU.mult).then_inc(weighted, 1)
                    j, par, before, r = part(i, u, 0)
                    if cos and active(0) and r == 1:
                        wait(pool, guessed, j + 1)
                        newton_step(RS * j)
                    if cos and active(0) and r == 2:
                        wait(pool, refined, RS * j + 4)
                        newton_step(RS * j + 4)

                run(pool, step)

            @block.vector
            def _(dve):
                dve.memset(xT[HALF:HALF + 1, :, :, :], 1.0).then_inc(const_set, 1)
                dve.memset(qkT[HALF:P, :, :, :], 0.0).then_inc(const_set, 1)
                if not cos:
                    dve.memset(oT[HALF:HALF + 1, :, :, :], 1.0)
                dve.memset(vblk[:, :, :, :, :], 0.0).then_inc(const_set, 1)
                if cos:
                    dve.wait_ge(*loaded)
                    dve.tensor_scalar(scale_min[:, :], w["logit_scale"][:, :], LOGIT_SCALE_MAX, None, ALU.min).then_inc(capped, 1)
                    dve.memset(three_halves[:, :, :], 1.5)
                    dve.memset(gain[:, HEADS:2 * HEADS], 1.0).then_inc(gain_set, 1)
                    dve.wait_ge(gain_set, 2)
                dve.wait_ge(const_set, 5)

                def step(i, u, active):
                    if not cos:
                        j, par, before, r = part(i, u, L_PROJ + 1)
                        if active(L_PROJ + 1) and r % 2:
                            t = r // 2
                            wait(dve, projected, 2 * j + t + 1)
                            wait(dve, res_loaded[par], 16 * (before + 1))
                            wait(dve, stored[par], 16 * before)
                            if kind == "tok":
                                dve.tensor_tensor(outb[:, par, t, :], ps_r[:, 0:DIM], res[:, par, t, :], ALU.add).then_inc(out_ready, 1)
                            else:
                                dve.scalar_tensor_tensor(outb[:, par, t, :], ps_r[:, 0:DIM], res[:, par, t, DIM:DIM + 1],
                                                         res[:, par, t, 0:DIM], ALU.mult, ALU.add).then_inc(out_ready, 1)
                    if active(L_S):
                        n, ring = UPG * i + (u - L_S), (u - L_S) % 2
                        scores = ps_s[ring][:, 0:HH * SEQ].rearrange("p (h k) -> p h k", k=SEQ)
                        wait(dve, scored, n + 1)
                        dve.tensor_reduce(rowmax[:, ring, :], scores, AX, ALU.max).then_inc(maxed, 1)
                        wait(dve, maxed, n + 1)
                        wait(dve, exped, n - 1)
                        dve.tensor_tensor(shifted[:, ring, :, :], scores,
                                          rowmax[:, ring, :].unsqueeze(2).to_broadcast([P, HH, SEQ]), ALU.subtract).then_inc(shift_done, 1)
                    if active(L_SUM):
                        n, ring = UPG * i + (u - L_SUM), (u - L_SUM) % 2
                        wait(dve, exped, n + 1)
                        dve.tensor_reduce(total[:, ring, :], probs[:, (u - L_SUM) % 4, :, :], AX, ALU.add).then_inc(summed, 1)
                        wait(dve, summed, n + 1)
                        wait(dve, weighted, n - 1)
                        dve.reciprocal(rtotal[:, ring, :], total[:, ring, :]).then_inc(inverted, 1)
                    j, par, before, r = part(i, u, 0)
                    if cos and active(0) and r == 1:
                        for t in range(2):
                            wait(dve, squared, 2 * j + t + 1)
                            dve.tensor_reduce(norm2[:, t, :], square[:, t, :].rearrange("p (h d) -> p h d", d=HD), AX,
                                              ALU.add).then_inc(norm_summed, 1)
                        wait(dve, norm_summed, 2 * j + 2)
                        wait(dve, refined, RS * j)
                        dve.tensor_scalar(floor2[:, :, :], norm2[:, :, :], NORM_MIN2, None, ALU.max).then_inc(floored, 1)
                        wait(dve, floored, j + 1)
                        dve.tensor_scalar(minus_half[:, :, :], floor2[:, :, :], -0.5, None, ALU.mult)
                        dve.tensor_scalar(rnorm[:, :, :].bitcast(I32), floor2[:, :, :].bitcast(I32), -0.5, float(RSQRT_BITS),
                                          ALU.mult, ALU.add).then_inc(guessed, 1)
                    j, par, before, r = part(i, u, 4)
                    if cos and active(4) and r == 0:
                        n = NS * j
                        wait(dve, refined, RS * (j + 1))
                        dve.scalar_tensor_tensor(half_sq[:, :, :], rnorm[:, :, :], -0.5, rnorm[:, :, :],
                                                 ALU.mult, ALU.mult).then_inc(newton, 1)
                        dve.tensor_tensor(scaled[:, :, :], rnorm[:, :, :],
                                          gain[:, :].unsqueeze(1).to_broadcast([P, 2, 2 * HEADS]), ALU.mult).then_inc(newton, 1)
                        wait(dve, newton, n + 2)
                        dve.tensor_tensor(product[:, :, :], half_sq[:, :, :], floor2[:, :, :], ALU.mult).then_inc(newton, 1)
                        wait(dve, newton, n + 3)
                        dve.scalar_tensor_tensor(qk_scale[:, :, :], product[:, :, :], 1.5, scaled[:, :, :],
                                                 ALU.add, ALU.mult).then_inc(newton, 1)
                        wait(dve, newton, n + NS)
                        for t in range(2):
                            wait(dve, qk_copied, 2 * j + t + 1)
                            wait(dve, qkt, 2 * (j - 1) + t + 1 if not (isinstance(j, int) and j == 0) else 0)
                            dve.tensor_tensor(qkn[:, t, :].rearrange("p (h d) -> p h d", d=HD),
                                              qk[:, t, :].rearrange("p (h d) -> p h d", d=HD),
                                              qk_scale[:, t, :].unsqueeze(2).to_broadcast([P, 2 * HEADS, HD]),
                                              ALU.mult).then_inc(qkn_ready, 1)
                    j, par, before, r = part(i, u, 0)
                    if not cos and active(0) and r == 0:
                        wait(dve, k_mm, j + 1)
                        wait(dve, kmask_loaded[par], 16 * HH * before)
                        dve.tensor_copy(qkT[0:HALF, par, 2:4, :],
                                        ps_x[0][0:HALF, :].rearrange("p (c t) -> p c t", c=2)).then_inc(k_ready, 1)

                run(dve, step)



def mlp_phase(nc, w, x2_dram, h_dram, big):
    with ExitStack() as ctx:
        mem = Memory(nc, ctx, "mlp")
        x2 = mem.sb("x2", [P, TILES, DIM])
        x2b = mem.sb("x2b", [P, TILES, DIM])
        xm = mem.sb("xm", [HALF, GROUP])
        xT = mem.sb("xT", [HALF + 1, 2, 2, GROUP], F32R)
        hT = mem.sb("hT", [P, KM, GROUP])
        h = mem.sb("h", [P, TILES, DIM])
        stats = mem.sb("stats", [P, TILES, 6])
        mv = mem.sb("mv", [P, TILES, 2])
        vare = mem.sb("vare", [P, TILES])
        power = mem.sb("power", [P, TILES])
        rstd = mem.sb("rstd", [P, TILES])
        un = mem.sb("un", [P, TILES, DIM])
        ps_t = [mem.ps(f"ps_t{i}") for i in range(2)]
        ps_u = [mem.ps(f"ps_u{i}") for i in range(2)]
        ps_h = [mem.ps(f"ps_h{i}") for i in range(2)]
        ps_f = [mem.ps(f"ps_f{i}") for i in range(2)]
        const_set = mem.sem("const_set")
        x2_loaded = mem.sem("x2_loaded")
        biased = mem.sem("biased")
        turned = mem.sem("turned")
        xt_step = mem.sem("xt_step")
        xt_ready = mem.sem("xt_ready")
        hidden = mem.sem("hidden")
        gelued = mem.sem("gelued")
        summed = mem.sem("summed")
        added = mem.sem("added")
        counted, measured = mem.sem("counted"), mem.sem("measured")
        varied, rooted = mem.sem("varied"), mem.sem("rooted")
        normed = mem.sem("normed")
        u_turned = mem.sem("u_turned")
        u_ready = mem.sem("u_ready")
        h_stored = mem.sem("h_stored")

        with nc.Block() as block:

            @block.sync
            def _(sp):
                def turn(i, active):
                    if active(0):
                        waits(sp, (biased, i), (turned, 2 * i))
                        sp.dma_start(x2[:, :, :], x2_dram[i]).then_inc(x2_loaded, 16)
                    if active(1):
                        wait(sp, added, TILES * i)
                        sp.dma_start(h_dram[i - 1], h[:, :, :]).then_inc(h_stored, 16)

                sweep(sp, GROUPS, 2, turn)
                sp.wait_ge(h_stored, 16 * GROUPS)

            @block.tensor
            def _(pe):
                pe.wait_ge(const_set, 2)

                def turn(i, active):
                    if active(1):
                        wait(pe, xt_ready, 2 * i)
                        for k in range(KM):
                            wait(pe, gelued, KM * (i - 1) + k - 1)
                            split_layer(pe, ps_h[k % 2][:, :], split_chunk(w["ff1_high"], w["ff1_low"], k), split_halves(xT)).then_inc(hidden, 1)
                    if active(2):
                        wait(pe, normed, i - 1)
                        for c in range(2):
                            wait(pe, u_ready, 2 * (i - 3) + c + 1 if not (isinstance(i, int) and i < 3) else 0)
                            for t in range(TILES):
                                last = pe.transpose(ps_u[c][0:HALF, span(t, P)], un[:, t, span(c, HALF)], w["ident"][:, :])
                            last.then_inc(u_turned, 1)
                    if active(0):
                        wait(pe, x2_loaded, 16 * (i + 1))
                        for c in range(2):
                            wait(pe, xt_ready, 2 * (i - 1) + c + 1 if not (isinstance(i, int) and i < 1) else 0)
                            for t in range(TILES):
                                last = pe.transpose(ps_t[c][0:HALF, span(t, P)], x2[:, t, span(c, HALF)], w["ident"][:, :])
                            last.then_inc(turned, 1)
                    if active(1):
                        wait(pe, gelued, KM * i)
                        for t in range(TILES):
                            wait(pe, added, TILES * (i - 1) + t - 1)
                            layer(pe, ps_f[t % 2][:, 0:DIM], [hT[:, k, span(t, P)] for k in range(KM)],
                                  [w["ff2"][:, k, :] for k in range(KM)]).then_inc(summed, 1)

                sweep(pe, GROUPS, 2, turn)

            @block.scalar
            def _(act):
                def turn(i, active):
                    if active(1):
                        for k in range(KM):
                            wait(act, hidden, KM * (i - 1) + k + 1)
                            wait(act, summed, TILES * (i - 1))
                            act.activation(hT[:, k, :], ps_h[k % 2][:, :], ACT.Gelu_apprx_tanh).then_inc(gelued, 1)
                    if active(2):
                        for c in range(2):
                            wait(act, u_turned, 2 * (i - 2) + c + 1)
                            columns = big[0:HALF, c, :].rearrange("p (n b) -> p b n", b=IMAGES)
                            act.activation(columns[:, bass.ds(8 * (i - 2), 8), :],
                                           ps_u[c][0:HALF, :].rearrange("p (b n) -> p b n", n=SEQ), ACT.Copy).then_inc(u_ready, 1)

                sweep(act, GROUPS, 2, turn)

            @block.gpsimd
            def _(pool):
                pool.memset(power[:, :], -0.5).then_inc(const_set, 1)
                pool.wait_ge(const_set, 2)

                def turn(i, active):
                    if active(1):
                        wait(pool, x2_loaded, 16 * i)
                        wait(pool, added, TILES * (i - 1))
                        pool.tensor_tensor(x2b[:, :, :], x2[:, :, :],
                                           w["ff2_b"][:, :].unsqueeze(1).to_broadcast([P, TILES, DIM]), ALU.add).then_inc(biased, 1)
                        wait(pool, varied, i)
                        pool.tensor_tensor(rstd[:, :], vare[:, :], power[:, :], ALU.pow).then_inc(rooted, 1)

                sweep(pool, GROUPS, 2, turn)

            @block.vector
            def _(dve):
                dve.memset(xT[HALF:HALF + 1, 0, :, :].bitcast(F32), 1.0)
                dve.memset(xT[HALF:HALF + 1, 1, :, :].bitcast(F32), 0.0).then_inc(const_set, 1)

                def turn(i, active):
                    if active(0):
                        for c in range(2):
                            wait(dve, turned, 2 * i + c + 1)
                            wait(dve, hidden, KM * i)
                            wait(dve, xt_ready, 2 * i + c)
                            split(dve, ps_t[c][0:HALF, :], xm[:, :], xT[0:HALF, 0, c, :], xT[0:HALF, 1, c, :],
                                  xt_step, 4 * i + 2 * c).then_inc(xt_ready, 1)
                    if active(1):
                        wait(dve, biased, i)
                        wait(dve, h_stored, 16 * (i - 1))
                        for t in range(TILES):
                            n = TILES * (i - 1) + t + 1
                            wait(dve, summed, n)
                            dve.tensor_tensor(h[:, t, :], ps_f[t % 2][:, 0:DIM], x2b[:, t, :], ALU.add).then_inc(added, 1)
                            wait(dve, added, n)
                            dve.bn_stats(stats[:, t, :], h[:, t, :]).then_inc(counted, 1)
                            dve.drain()
                            dve.bn_aggr(mv[:, t, :], stats[:, t, :]).then_inc(measured, 1)
                        wait(dve, measured, TILES * i)
                        dve.tensor_scalar(vare[:, :], mv[:, :, 1], EPS, None, ALU.add).then_inc(varied, 1)
                        wait(dve, rooted, i)
                        wait(dve, u_turned, 2 * (i - 1))
                        for t in range(TILES):
                            last = dve.tensor_scalar(un[:, t, :], h[:, t, :], mv[:, t, 0:1], rstd[:, t:t + 1],
                                                     ALU.subtract, ALU.mult)
                        last.then_inc(normed, 1)

                sweep(dve, GROUPS, 2, turn)



def fold_phase(nc, w):
    jobs = (("r_in", "r_ln", RHD, 0), ("ffn_qkv", "ln1", 3 * DIM, RHD), ("fc1", "ln2", MLP, RHD + 3 * DIM))
    pieces = [(name, norm, a, min(a + 512, n), at) for name, norm, n, at in jobs for a in range(0, n, 512)]
    with ExitStack() as ctx:
        mem = Memory(nc, ctx, "fold")
        bias_row = mem.sb("bias_row", [1, RHD + 3 * DIM + MLP])
        banks = [mem.ps(f"bank{n}") for n in range(len(pieces))]
        shifted = mem.sem("shifted")
        rowed = mem.sem("rowed")
        scaled = mem.sem("scaled")
        placed = mem.sem("placed")
        with nc.Block() as block:

            @block.tensor
            def _(pe):
                pe.wait_ge(w["done"]["ffn"], w["counts"]["ffn"])
                for (name, norm, a, b, at), bank in zip(pieces, banks):
                    raw = w[name + "_raw"]
                    layer(pe, bank[0:1, 0:b - a], [w[norm + "_b"][:, c:c + 1] for c in range(2)],
                          [raw[:, c, a:b] for c in range(2)]).then_inc(shifted, 1)

            @block.vector
            def _(dve):
                dve.wait_ge(w["done"]["ffn"], w["counts"]["ffn"])
                dve.wait_ge(w["done"]["cos"], w["counts"]["cos"])
                for name, norm, n, at in jobs:
                    for c in range(2):
                        dve.tensor_scalar(w[name][0:HALF, c, :], w[name + "_raw"][:, c, :], w[norm + "_g"][:, c:c + 1], None,
                                          ALU.mult).then_inc(scaled, 1)
                for c in range(2):
                    dve.tensor_scalar(w["cos_proj"][0:HALF, c, :], w["cos_proj"][0:HALF, c, :], w["head_scale"][:, c:c + 1], None,
                                      ALU.mult).then_inc(scaled, 1)
                for n, (name, norm, a, b, at) in enumerate(pieces):
                    dve.wait_ge(shifted, n + 1)
                    dve.tensor_tensor(bias_row[0:1, at + a:at + b], banks[n][0:1, 0:b - a], w["fold_bias"][0:1, at + a:at + b],
                                      ALU.add).then_inc(rowed, 1)
                dve.wait_ge(scaled, 2 * len(jobs) + 2)

            @block.sync
            def _(sp):
                sp.wait_ge(rowed, len(pieces))
                for name, norm, n, at in jobs:
                    sp.dma_start(w[name][HALF:HALF + 1, 1, :], bias_row[0:1, at:at + n]).then_inc(placed, 16)
                sp.wait_ge(placed, 16 * len(jobs))



def router_phase(nc, w, big, h_dram, h4_dram, z_dram, bits_dram, zn_dram):
    with ExitStack() as ctx:
        mem = Memory(nc, ctx, "router")
        oT = mem.sb("oT", [HALF + 1, 2, GROUP])
        h = mem.sb("h", [P, TILES, DIM])
        h4 = mem.sb("h4", [P, TILES, DIM])
        stats = mem.sb("stats", [P, TILES, 6])
        mv = mem.sb("mv", [P, TILES, 2])
        vare = mem.sb("vare", [P, TILES])
        power = mem.sb("power", [P, TILES])
        rstd = mem.sb("rstd", [P, TILES])
        varz = mem.sb("varz", [P, TILES])
        varz2 = mem.sb("varz2", [P, TILES])
        varz3 = mem.sb("varz3", [P, TILES])
        rz = mem.sb("rz", [P, TILES])
        z = mem.sb("z", [P, TILES, DIM])
        zn = mem.sb("zn", [P, TILES, DIM])
        znT = mem.sb("znT", [HALF + 1, 2, GROUP])
        eT = mem.sb("eT", [P, GROUP])
        esum = mem.sb("esum", [P, 8])
        emean = mem.sb("emean", [P, 8])
        h1 = mem.sb("h1", [P, GROUP])
        h2 = mem.sb("h2", [RH2 + 1, GROUP])
        logits = mem.sb("logits", [P, TILES, 2 * BITS])
        beat = mem.sb("beat", [P, TILES, BITS])
        both = mem.sb("both", [P, TILES])
        route = mem.sb("route", [P, TILES, 8])
        ps_a = [mem.ps(f"ps_a{i}") for i in range(2)]
        ps_t = [mem.ps(f"ps_t{i}") for i in range(2)]
        ps_e, ps_1, ps_2, ps_l = (mem.ps(f"ps_{x}") for x in "e12l")
        const_set = mem.sem("const_set")
        h_loaded = mem.sem("h_loaded")
        o_ready = mem.sem("o_ready")
        projected = mem.sem("projected")
        added = mem.sem("added")
        counted, measured = mem.sem("counted"), mem.sem("measured")
        varied = mem.sem("varied")
        rooted = mem.sem("rooted")
        var_step = mem.sem("var_step")
        z_rooted = mem.sem("z_rooted")
        z_ready = mem.sem("z_ready")
        zn_ready = mem.sem("zn_ready")
        turned = mem.sem("turned")
        znt_ready = mem.sem("znt_ready")
        e_mm, e_ready = mem.sem("e_mm"), mem.sem("e_ready")
        e_summed, mean_ready = mem.sem("e_summed"), mem.sem("mean_ready")
        h1_mm, h1_ready = mem.sem("h1_mm"), mem.sem("h1_ready")
        h2_mm, h2_ready = mem.sem("h2_mm"), mem.sem("h2_ready")
        l_mm = mem.sem("l_mm")
        route_step = mem.sem("route_step")
        h4_stored, z_stored, zn_stored, bits_stored = (mem.sem(x) for x in ("h4_stored", "z_stored", "zn_stored", "bits_stored"))
        RS = 7

        with nc.Block() as block:

            @block.sync
            def _(sp):
                def turn(i, active):
                    if active(0):
                        wait(sp, added, TILES * i)
                        sp.dma_start(h[:, :, :], h_dram[i]).then_inc(h_loaded, 16)
                    if active(1):
                        wait(sp, added, TILES * i)
                        sp.dma_start(h4_dram[i - 1], h4[:, :, :]).then_inc(h4_stored, 16)
                        wait(sp, z_ready, TILES * i)
                        sp.dma_start(z_dram[i - 1], z[:, :, :]).then_inc(z_stored, 16)
                    if active(2):
                        wait(sp, znt_ready, 2 * (i - 1))
                        for a in range(2):
                            sp.dma_start(zn_dram[2 * (i - 2) + a], znT[0:HALF, :, span(a, PART)]).then_inc(zn_stored, 16)
                    if active(4):
                        wait(sp, route_step, RS * (i - 3))
                        sp.dma_start(bits_dram[i - 4], route[:, :, :]).then_inc(bits_stored, 16)

                sweep(sp, GROUPS, 4, turn)
                sp.wait_ge(h4_stored, 16 * GROUPS)
                sp.wait_ge(z_stored, 16 * GROUPS)
                sp.wait_ge(zn_stored, 32 * GROUPS)
                sp.wait_ge(bits_stored, 16 * GROUPS)

            @block.tensor
            def _(pe):
                pe.wait_ge(const_set, 5)

                def turn(i, active):
                    if active(4):
                        wait(pe, mean_ready, i - 3)
                        wait(pe, h1_ready, i - 4)
                        layer(pe, ps_1[:, :].rearrange("p (b n) -> p b n", n=SEQ), [w["r_o1"][:, 0, :], w["r_o1"][:, 1, :]],
                              [eT[:, :].rearrange("p (b n) -> p b n", n=SEQ),
                               emean[:, :].unsqueeze(2).to_broadcast([P, 8, SEQ])]).then_inc(h1_mm, 1)
                    if active(1):
                        wait(pe, o_ready, 2 * i)
                        for t in range(TILES):
                            wait(pe, added, TILES * (i - 1) + t - 1)
                            layer(pe, ps_a[t % 2][:, 0:DIM], halves(oT, span(t, P)),
                                  [w["cos_proj"][0:HALF, 0, :], w["cos_proj"][0:HALF + 1, 1, :]]).then_inc(projected, 1)
                    if active(3):
                        wait(pe, znt_ready, 2 * (i - 2))
                        wait(pe, e_ready, i - 3)
                        layer(pe, ps_e[:, :], [w["r_in"][0:HALF, 0, :], w["r_in"][0:HALF + 1, 1, :]],
                              halves(znT, slice(0, GROUP))).then_inc(e_mm, 1)
                    if active(4):
                        wait(pe, h1_ready, i - 3)
                        wait(pe, h2_ready, i - 4)
                        pe.matmul(ps_2[0:RH2, :], w["r_o2"][:, :], h1[:, :], start=True, stop=True).then_inc(h2_mm, 1)
                    if active(2):
                        wait(pe, zn_ready, i - 1)
                        for c in range(2):
                            wait(pe, znt_ready, 2 * (i - 3) + c + 1 if not (isinstance(i, int) and i < 3) else 0)
                            for t in range(TILES):
                                last = pe.transpose(ps_t[c][0:HALF, span(t, P)], zn[:, t, span(c, HALF)], w["ident"][:, :])
                            last.then_inc(turned, 1)
                    if active(4):
                        wait(pe, h2_ready, i - 3)
                        wait(pe, route_step, RS * (i - 4))
                        for t in range(TILES):
                            last = pe.matmul(ps_l[:, span(t, 2 * BITS)], h2[:, span(t, P)], w["r_o3"][:, :], start=True, stop=True)
                        last.then_inc(l_mm, 1)

                sweep(pe, GROUPS, 4, turn)

            @block.scalar
            def _(act):
                def turn(i, active):
                    if active(4):
                        wait(act, h1_mm, i - 3)
                        wait(act, h2_mm, i - 4)
                        act.activation(h1[:, :], ps_1[:, :], ACT.Gelu, bias=w["r_o1_b"][:, 0:1]).then_inc(h1_ready, 1)
                    if active(0):
                        wait(act, projected, TILES * i)
                        for c in range(2):
                            columns = big[0:HALF, c, :].rearrange("p (n b) -> p b n", b=IMAGES)
                            act.activation(oT[0:HALF, c, :].rearrange("p (b n) -> p b n", n=SEQ), columns[:, bass.ds(8 * i, 8), :],
                                           ACT.Copy).then_inc(o_ready, 1)
                    if active(3):
                        wait(act, e_mm, i - 2)
                        wait(act, h1_mm, i - 3)
                        act.activation(eT[:, :], ps_e[:, :], ACT.Gelu).then_inc(e_ready, 1)
                    if active(4):
                        wait(act, h2_mm, i - 3)
                        wait(act, l_mm, i - 4)
                        act.activation(h2[0:RH2, :], ps_2[0:RH2, :], ACT.Gelu, bias=w["r_o2_b"][:, 0:1]).then_inc(h2_ready, 1)
                    if active(2):
                        for c in range(2):
                            wait(act, turned, 2 * (i - 2) + c + 1)
                            wait(act, e_mm, i - 2)
                            wait(act, zn_stored, 32 * (i - 2))
                            act.activation(znT[0:HALF, c, :], ps_t[c][0:HALF, :], ACT.Copy).then_inc(znt_ready, 1)

                sweep(act, GROUPS, 4, turn)

            @block.gpsimd
            def _(pool):
                pool.memset(power[:, :], -0.5).then_inc(const_set, 1)
                pool.wait_ge(const_set, 5)

                def turn(i, active):
                    if active(1):
                        wait(pool, varied, i)
                        pool.tensor_tensor(rstd[:, :], vare[:, :], power[:, :], ALU.pow).then_inc(rooted, 1)
                        wait(pool, var_step, 3 * i)
                        pool.tensor_tensor(rz[:, :], varz3[:, :], power[:, :], ALU.pow).then_inc(z_rooted, 1)

                sweep(pool, GROUPS, 4, turn)

            @block.vector
            def _(dve):
                dve.memset(oT[HALF:HALF + 1, :, :], 1.0).then_inc(const_set, 1)
                dve.memset(znT[HALF:HALF + 1, :, :], 1.0).then_inc(const_set, 1)
                dve.memset(h2[RH2:RH2 + 1, :], 1.0).then_inc(const_set, 1)
                dve.memset(route[:, :, :], 0.0).then_inc(const_set, 1)
                dve.wait_ge(const_set, 5)

                def turn(i, active):
                    if active(1):
                        wait(dve, h_loaded, 16 * i)
                        wait(dve, h4_stored, 16 * (i - 1))
                        for t in range(TILES):
                            n = TILES * (i - 1) + t + 1
                            wait(dve, projected, n)
                            dve.tensor_tensor(h4[:, t, :], ps_a[t % 2][:, 0:DIM], h[:, t, :], ALU.add).then_inc(added, 1)
                            wait(dve, added, n)
                            dve.bn_stats(stats[:, t, :], h4[:, t, :]).then_inc(counted, 1)
                            dve.drain()
                            dve.bn_aggr(mv[:, t, :], stats[:, t, :]).then_inc(measured, 1)
                        wait(dve, measured, TILES * i)
                        dve.tensor_scalar(vare[:, :], mv[:, :, 1], EPS, None, ALU.add).then_inc(varied, 1)
                    if active(3):
                        wait(dve, e_ready, i - 2)
                        dve.tensor_reduce(esum[:, :], eT[:, :].rearrange("p (b n) -> p b n", n=SEQ)[:, :, 1:SEQ], AX, ALU.add).then_inc(e_summed, 1)
                        wait(dve, e_summed, i - 2)
                        wait(dve, h1_mm, i - 3)
                        dve.tensor_scalar(emean[:, :], esum[:, :], 1.0 / (SEQ - 1), None, ALU.mult).then_inc(mean_ready, 1)
                    if active(1):
                        wait(dve, rooted, i)
                        dve.tensor_tensor(varz[:, :], mv[:, :, 1], rstd[:, :], ALU.mult).then_inc(var_step, 1)
                        wait(dve, var_step, 3 * (i - 1) + 1)
                        dve.tensor_tensor(varz2[:, :], varz[:, :], rstd[:, :], ALU.mult).then_inc(var_step, 1)
                        wait(dve, var_step, 3 * (i - 1) + 2)
                        dve.tensor_scalar(varz3[:, :], varz2[:, :], EPS, None, ALU.add).then_inc(var_step, 1)
                        wait(dve, z_stored, 16 * (i - 1))
                        for t in range(TILES):
                            dve.tensor_scalar(z[:, t, :], h4[:, t, :], mv[:, t, 0:1], rstd[:, t:t + 1],
                                              ALU.subtract, ALU.mult).then_inc(z_ready, 1)
                        wait(dve, z_rooted, i)
                        wait(dve, z_ready, TILES * i)
                        wait(dve, turned, 2 * (i - 1))
                        for t in range(TILES):
                            last = dve.tensor_scalar(zn[:, t, :], z[:, t, :], rz[:, t:t + 1], None, ALU.mult)
                        last.then_inc(zn_ready, 1)
                    if active(4):
                        n = RS * (i - 4)
                        wait(dve, l_mm, i - 3)
                        wait(dve, bits_stored, 16 * (i - 4))
                        dve.tensor_copy(logits[:, :, :], ps_l[:, 0:TILES * 2 * BITS].rearrange("p (t l) -> p t l", t=TILES)).then_inc(route_step, 1)
                        wait(dve, route_step, n + 1)
                        pairs = logits[:, :, :].rearrange("p t (b l) -> p t b l", l=2)
                        dve.tensor_tensor(beat[:, :, :], pairs[:, :, :, 1], pairs[:, :, :, 0], ALU.is_gt).then_inc(route_step, 1)
                        wait(dve, route_step, n + 2)
                        dve.tensor_scalar(route[:, :, 0:BITS], beat[:, :, :], w["first_token"][:, 0:1], None, ALU.max).then_inc(route_step, 1)
                        wait(dve, route_step, n + 3)
                        dve.tensor_tensor(both[:, :], route[:, :, 0], route[:, :, 1], ALU.mult).then_inc(route_step, 1)
                        wait(dve, route_step, n + 4)
                        dve.tensor_tensor(route[:, :, 3], route[:, :, 1], both[:, :], ALU.subtract).then_inc(route_step, 1)
                        dve.tensor_tensor(route[:, :, 4], route[:, :, 0], both[:, :], ALU.subtract).then_inc(route_step, 1)
                        dve.scalar_tensor_tensor(beat[:, :, 0], route[:, :, 0], -1.0, route[:, :, 1], ALU.mult, ALU.subtract).then_inc(select_step, 1)
                        wait(dve, select_step, 2 * (i - 4) + 1)
                        dve.scalar_tensor_tensor(beat[:, :, 1], beat[:, :, 0], 1.0, both[:, :], ALU.add, ALU.add).then_inc(select_step, 1)
                        wait(dve, select_step, 2 * (i - 4) + 2)
                        dve.tensor_copy(route[:, :, 2], beat[:, :, 1]).then_inc(route_step, 1)

                select_step = mem.sem("select_step")
                sweep(dve, GROUPS, 4, turn)



def last_phase(nc, w, h5_dram, bits_dram, h4_dram, out_dram):
    with ExitStack() as ctx:
        mem = Memory(nc, ctx, "last")
        h5 = mem.sb("h5", [P, TILES, DIM])
        h5r = mem.sb("h5r", [P, TILES, DIM])
        bits = mem.sb("bits", [P, TILES, 8])
        h4 = mem.sb("h4", [P, TILES, DIM])
        select = mem.sb("select", [P, TILES, 8])
        stats = mem.sb("stats", [P, TILES, 6])
        mv = mem.sb("mv", [P, TILES, 2])
        vare = mem.sb("vare", [P, TILES])
        power = mem.sb("power", [P, TILES])
        rstd = mem.sb("rstd", [P, TILES])
        xn = mem.sb("xn", [P, TILES, DIM])
        xm = mem.sb("xm", [HALF, GROUP])
        xT = mem.sb("xT", [HALF + 1, 2, 2, GROUP], F32R)
        hT = mem.sb("hT", [P, KM, GROUP])
        ffb = mem.sb("ffb", [P, 2, DIM])
        out = mem.sb("out", [P, TILES, DIM])
        outT = mem.sb("outT", [HALF, 2, GROUP])
        down = mem.sb("down", [P, TILES, RANK3])
        downT = mem.sb("downT", [HALF, 2, GROUP])
        base = mem.sb("base", [P, TILES, DIM])
        fin = mem.sb("fin", [P, TILES, DIM])
        ps_t = [mem.ps(f"ps_t{i}") for i in range(2)]
        ps_h = [mem.ps(f"ps_h{i}") for i in range(2)]
        ps_f = [mem.ps(f"ps_f{i}") for i in range(2)]
        ps_d = [mem.ps(f"ps_d{i}") for i in range(2)]
        const_set = mem.sem("const_set")
        h5_loaded, r_loaded, s_loaded = mem.sem("h5_loaded"), mem.sem("r_loaded"), mem.sem("s_loaded")
        counted, measured = mem.sem("counted"), mem.sem("measured")
        varied, rooted = mem.sem("varied"), mem.sem("rooted")
        normed = mem.sem("normed")
        turned = mem.sem("turned")
        weight_step = mem.sem("weight_step")
        weight_split = mem.sem("weight_split")
        xt_step = mem.sem("xt_step")
        xt_ready = mem.sem("xt_ready")
        hidden, gelued = mem.sem("hidden"), mem.sem("gelued")
        summed = mem.sem("summed")
        biased = mem.sem("biased")
        out_ready = mem.sem("out_ready")
        o_turned, ot_ready = mem.sem("o_turned"), mem.sem("ot_ready")
        downed, down_ready = mem.sem("downed"), mem.sem("down_ready")
        d_turned, dt_ready = mem.sem("d_turned"), mem.sem("dt_ready")
        upped = mem.sem("upped")
        based = mem.sem("based")
        fin_ready = mem.sem("fin_ready")
        stored = mem.sem("stored")

        with nc.Block() as block:

            @block.sync
            def _(sp):
                def turn(i, active):
                    if active(0):
                        wait(sp, normed, i)
                        sp.dma_start(h5[:, :, :], h5_dram[i]).then_inc(h5_loaded, 16)
                    if active(1):
                        wait(sp, out_ready, TILES * (i - 1))
                        sp.dma_start(h5r[:, :, :], h5_dram[i - 1]).then_inc(r_loaded, 16)
                        sp.dma_start(bits[:, :, :], bits_dram[i - 1]).then_inc(r_loaded, 16)
                    if active(2):
                        waits(sp, (based, i - 2), (down_ready, TILES * (i - 2)))
                        sp.dma_start(h4[:, :, :], h4_dram[i - 2]).then_inc(s_loaded, 16)
                        sp.dma_start(select[:, :, :], bits_dram[i - 2]).then_inc(s_loaded, 16)
                    if active(3):
                        wait(sp, fin_ready, TILES * (i - 2))
                        sp.dma_start(out_dram[i - 3], fin[:, :, :]).then_inc(stored, 16)

                sweep(sp, GROUPS, 3, turn)
                sp.wait_ge(stored, 16 * GROUPS)

            @block.tensor
            def _(pe):
                pe.wait_ge(const_set, 2)

                def transposes(source, into, rows=HALF):
                    for c in range(2):
                        for t in range(TILES):
                            last = pe.transpose(ps_t[c][0:rows, span(t, P)], source[:, t, span(c, HALF)], w["ident"][:, :])
                        last.then_inc(into, 1)

                def second(i, t):
                    wait(pe, biased, TILES * (i - 2) + t - 1)
                    layer(pe, ps_f[t % 2][:, 0:DIM], [hT[:, k, span(t, P)] for k in range(KM)],
                          [w["fc2"][:, k, :] for k in range(KM)]).then_inc(summed, 1)

                def turn(i, active):
                    if active(2):
                        wait(pe, weight_split, 1)
                        wait(pe, xt_ready, 2 * (i - 1))
                        for k in range(KM):
                            wait(pe, gelued, KM * (i - 2) + k - 1)
                            split_layer(pe, ps_h[k % 2][:, :], split_chunk(w["fc1_high"], w["fc1_low"], k), split_halves(xT)).then_inc(hidden, 1)
                    if active(3):
                        wait(pe, out_ready, TILES * (i - 2))
                        wait(pe, dt_ready, 2 * (i - 3))
                        wait(pe, xt_ready, 2 * (i - 1) if not isinstance(i, int) else 2 * min(i - 1, GROUPS))
                        transposes(out, o_turned)
                    if active(2):
                        wait(pe, gelued, KM * (i - 1))
                        second(i, 0)
                    if active(1):
                        wait(pe, normed, i)
                        wait(pe, ot_ready, 2 * (i - 2))
                        if isinstance(i, int):
                            wait(pe, dt_ready, 2 * (i - 3))
                        transposes(xn, turned)
                    if active(3):
                        wait(pe, ot_ready, 2 * (i - 2))
                        for t in range(TILES):
                            n = TILES * (i - 3) + t
                            if t < 2:
                                wait(pe, fin_ready, n - t)
                            else:
                                wait(pe, down_ready, n - 1)
                            layer(pe, ps_d[t % 2][:, 0:RANK3], [outT[:, c, span(t, P)] for c in range(2)],
                                  [w["lra_down"][:, c, :] for c in range(2)]).then_inc(downed, 1)
                    if active(2):
                        second(i, 1)
                        second(i, 2)
                    if active(3):
                        wait(pe, down_ready, TILES * (i - 2))
                        wait(pe, xt_ready, 2 * i if not isinstance(i, int) else 2 * min(i, GROUPS))
                        transposes(down, d_turned)
                    if active(2):
                        second(i, 3)
                    if active(3):
                        wait(pe, dt_ready, 2 * (i - 2))
                        for t in range(TILES):
                            if t >= 2:
                                wait(pe, fin_ready, TILES * (i - 3) + t - 1)
                            layer(pe, ps_d[t % 2][:, 0:DIM], [downT[:, c, span(t, P)] for c in range(2)],
                                  [w["lra_up"][:, c, :] for c in range(2)]).then_inc(upped, 1)

                sweep(pe, GROUPS, 3, turn)

            @block.scalar
            def _(act):
                def turn(i, active):
                    if active(2):
                        for k in range(KM):
                            wait(act, hidden, KM * (i - 2) + k + 1)
                            wait(act, summed, TILES * (i - 2))
                            act.activation(hT[:, k, :], ps_h[k % 2][:, :], ACT.Gelu).then_inc(gelued, 1)
                    if active(3):
                        for c in range(2):
                            wait(act, o_turned, 2 * (i - 3) + c + 1)
                            wait(act, downed, TILES * (i - 3))
                            act.activation(outT[:, c, :], ps_t[c][0:HALF, :], ACT.Copy).then_inc(ot_ready, 1)
                        for c in range(2):
                            wait(act, d_turned, 2 * (i - 3) + c + 1)
                            wait(act, upped, TILES * (i - 3))
                            act.activation(downT[:, c, :], ps_t[c][0:HALF, :], ACT.Copy).then_inc(dt_ready, 1)

                sweep(act, GROUPS, 3, turn)

            @block.gpsimd
            def _(pool):
                pool.memset(power[:, :], -0.5).then_inc(const_set, 1)
                pool.wait_ge(const_set, 2)

                def turn(i, active):
                    if active(1):
                        wait(pool, varied, i)
                        pool.tensor_tensor(rstd[:, :], vare[:, :], power[:, :], ALU.pow).then_inc(rooted, 1)
                    if active(3):
                        wait(pool, s_loaded, 32 * (i - 2))
                        wait(pool, out_ready, TILES * (i - 2))
                        wait(pool, fin_ready, TILES * (i - 3))
                        pool.tensor_tensor(base[:, :, :], h4[:, :, :], out[:, :, :], ALU.add).then_inc(based, 1)

                sweep(pool, GROUPS, 3, turn)

            @block.vector
            def _(dve):
                dve.memset(xT[HALF:HALF + 1, 0, :, :].bitcast(F32), 1.0)
                dve.memset(xT[HALF:HALF + 1, 1, :, :].bitcast(F32), 0.0).then_inc(const_set, 1)
                split_weights(dve, w, "fc1", weight_step).then_inc(weight_split, 1)

                def add_bits(i, t):
                    n = TILES * (i - 2) + t + 1
                    wait(dve, summed, n)
                    dve.tensor_tensor(ffb[:, t % 2, :], ps_f[t % 2][:, 0:DIM], w["fc2_b"][:, :], ALU.add).then_inc(biased, 1)
                    wait(dve, biased, n)
                    if t == 0:
                        wait(dve, r_loaded, 32 * (i - 1))
                        wait(dve, o_turned, 2 * (i - 2))
                        wait(dve, based, i - 2)
                    dve.scalar_tensor_tensor(out[:, t, :], ffb[:, t % 2, :], bits[:, t, 1:2], h5r[:, t, :],
                                             ALU.mult, ALU.add).then_inc(out_ready, 1)

                def turn(i, active):
                    if active(1):
                        wait(dve, h5_loaded, 16 * i)
                        for t in range(TILES):
                            n = TILES * (i - 1) + t + 1
                            dve.bn_stats(stats[:, t, :], h5[:, t, :]).then_inc(counted, 1)
                            dve.drain()
                            dve.bn_aggr(mv[:, t, :], stats[:, t, :]).then_inc(measured, 1)
                        wait(dve, measured, TILES * i)
                        dve.tensor_scalar(vare[:, :], mv[:, :, 1], EPS, None, ALU.add).then_inc(varied, 1)
                        wait(dve, rooted, i)
                        wait(dve, turned, 2 * (i - 1))
                        for t in range(TILES):
                            last = dve.tensor_scalar(xn[:, t, :], h5[:, t, :], mv[:, t, 0:1], rstd[:, t:t + 1],
                                                     ALU.subtract, ALU.mult)
                        last.then_inc(normed, 1)
                    if active(3):
                        wait(dve, s_loaded, 32 * (i - 2))
                        for t in range(TILES):
                            wait(dve, downed, TILES * (i - 3) + t + 1)
                            if t == 0:
                                wait(dve, d_turned, 2 * (i - 3))
                            dve.tensor_tensor(down[:, t, :].rearrange("p (k r) -> p k r", k=3),
                                              ps_d[t % 2][:, 0:RANK3].rearrange("p (k r) -> p k r", k=3),
                                              select[:, t, 2:5].unsqueeze(2).to_broadcast([P, 3, RANK3 // 3]),
                                              ALU.mult).then_inc(down_ready, 1)

                    if active(2):
                        add_bits(i, 0)
                    if active(1):
                        for c in range(2):
                            wait(dve, turned, 2 * (i - 1) + c + 1)
                            wait(dve, hidden, KM * (i - 1))
                            wait(dve, xt_ready, 2 * (i - 1) + c)
                            split(dve, ps_t[c][0:HALF, :], xm[:, :], xT[0:HALF, 0, c, :], xT[0:HALF, 1, c, :],
                                  xt_step, 4 * (i - 1) + 2 * c).then_inc(xt_ready, 1)
                    if active(2):
                        for t in range(1, TILES):
                            add_bits(i, t)
                    if active(3):
                        wait(dve, based, i - 2)
                        wait(dve, stored, 16 * (i - 3))
                        for t in range(TILES):
                            wait(dve, upped, TILES * (i - 3) + t + 1)
                            dve.tensor_tensor(fin[:, t, :], ps_d[t % 2][:, 0:DIM], base[:, t, :], ALU.add).then_inc(fin_ready, 1)

                sweep(dve, GROUPS, 3, turn)



def vit_tower(nc, ins, out, scratch):
    tiles4 = lambda x: x.rearrange("(g t) p f -> g p t f", t=TILES)
    tiles2 = lambda x: x.rearrange("(g t) p f -> g p t f", t=2)
    s = scratch
    with ExitStack() as ctx:
        mem = Memory(nc, ctx, "weights")
        w = {}
        load_weights(nc, mem, w, ins)
        for name, cols in (("r_in", RHD), ("ffn_qkv", 3 * DIM), ("fc1", MLP), ("masked", MLP)):
            w[name] = mem.sb(name, [HALF + 1, 2, cols])
        for name in ("ff1_high", "ff1_low", "fc1_high", "fc1_low"):
            w[name] = mem.sb(name, [HALF + 1, 2, MLP], F32R)
        patch_phase(nc, w, ins["patches"], tiles4(s["x1"]), s["y"])
        attention_phase(nc, w, "tok", lambda j: s["y"][j], tiles2(s["x1"]), tiles2(s["x2"]), None)
        with nc.sbuf_tensor("by_token", [HALF, 2, TOKENS], F32) as big:
            mlp_phase(nc, w, tiles4(s["x2"]), tiles4(s["h"]), big)
            attention_phase(nc, w, "cos", lambda j: big[0:HALF, :, bass.ds(PART * j, PART)], None, None, big)
            fold_phase(nc, w)
            router_phase(nc, w, big, tiles4(s["h"]), tiles4(s["h4"]), tiles4(s["zb"])[:, :, :, 0:DIM],
                         tiles4(s["zb"])[:, :, :, DIM:ROW], s["zn"])
        attention_phase(nc, w, "ffn", lambda j: s["zn"][j], tiles2(s["zb"]), tiles2(s["h5"]), None)
        last_phase(nc, w, tiles4(s["h5"]), tiles4(s["zb"])[:, :, :, DIM:ROW], tiles4(s["h4"]), tiles4(out))


SCRATCH = {"x1": (TOKENS // P, P, DIM), "x2": (TOKENS // P, P, DIM), "h": (TOKENS // P, P, DIM), "h4": (TOKENS // P, P, DIM),
           "h5": (TOKENS // P, P, DIM), "zb": (TOKENS // P, P, ROW), "y": (PARTS, HALF, 2, PART), "zn": (PARTS, HALF, 2, PART)}


NORMS = ("ffn_r_ln_g", "ffn_r_ln_b", "ffn_ln1_g", "ffn_ln1_b", "ffn_ln2_g", "ffn_ln2_b")
COLUMNS = {"tok_ff2_b": HALF, "head_scale": HALF, "ffn_r_o1_b": RHD, "ffn_r_o2_b": RH2, **dict.fromkeys(NORMS, HALF)}
UNSPREAD = [k for k in COLUMNS if k != "tok_ff2_b"]


def positions():
    pos = np.arange(SEQ, dtype=np.float32)[:, None]
    i = np.arange(DIM // 2, dtype=np.float32)[None, :]
    angle = (pos / np.power(np.float32(10000.0), np.float32(2.0) * i / np.float32(DIM))).astype(np.float32)
    pe = np.zeros((SEQ, DIM), np.float32)
    pe[:, 0::2], pe[:, 1::2] = np.sin(angle), np.cos(angle)
    return pe


def lay_out(inputs):
    x = {k.replace("L0_", ""): np.asarray(v) for k, v in inputs.items()}
    side = x["x"].shape[2] // PATCH
    tokens = x["x"].reshape(IMAGES, CHANNELS, side, PATCH, side, PATCH).transpose(1, 3, 5, 0, 2, 4).reshape(KP, P, GROUPS, GROUP)

    def qkv(wt):
        v = wt[..., 2 * DIM:].reshape(*wt.shape[:-1], HEADS // 2, 2, HD)
        v = np.swapaxes(v, -3, -2).reshape(*wt.shape[:-1], DIM)
        return np.concatenate([wt[..., :2 * DIM], v], axis=-1)

    a = {
        "patches": tokens.transpose(2, 1, 0, 3),
        "patch_w": x["tok_patch_w"].reshape(DIM, FEATS).T,
        "pe": np.concatenate([positions()] * 2),
        "ident": np.eye(P, dtype=np.float32),
        "first_token": (np.arange(P) % SEQ == 0).astype(np.float32)[:, None],
        "tok_qkv_w": qkv(x["tok_qkv_w"]), "tok_qkv_b": qkv(x["tok_qkv_b"]),
        "cos_qkv_w": qkv(x["attn_in_proj_weight"].T), "cos_qkv_b": qkv(x["attn_in_proj_bias"]),
        "cos_proj_w": x["attn_out_w"].T,
        "logit_scale": x["attn_logit_scale"].reshape(HEADS),
        "head_scale": np.repeat(x["attn_head_scale"].reshape(HEADS), HD),
        "ffn_qkv_w": qkv(np.concatenate([x["ffn_wq"].T, x["ffn_wk"].T, x["ffn_wv"].T], axis=1)),
        "ffn_qkv_b": qkv(np.concatenate([x["ffn_bq"], x["ffn_bk"], x["ffn_bv"]])),
        "ffn_proj_w": x["ffn_wo"].T, "r_in_w": x["ffn_r_in_w"].T, "r_o1_w": x["ffn_r_o1_w"].T,
        "r_o2_w": x["ffn_r_o2_w"].T, "r_o3_w": x["ffn_r_o3_w"].T,
        "fc1_w": x["ffn_fc1_w"].T, "fc2_w": x["ffn_fc2_w"].T,
        "lra_down": x["ffn_lra_down"].reshape(RANK3, DIM).T,
        "lra_up": x["ffn_lra_up"].transpose(0, 2, 1).reshape(RANK3, DIM),
    }
    for key in ("tok_patch_b", "tok_ln_g", "tok_ln_b", "tok_ff1_w", "tok_ff1_b", "tok_ff2_w", "tok_ff2_b", "tok_proj_w", "tok_proj_b",
                "attn_out_b", "ffn_bo", "ffn_fc1_b", "ffn_fc2_b", "ffn_r_in_b", "ffn_r_o1_b", "ffn_r_o2_b", "ffn_r_o3_b",
                "ffn_r_ln_g", "ffn_r_ln_b", "ffn_ln1_g", "ffn_ln1_b", "ffn_ln2_g", "ffn_ln2_b"):
        a[key] = x[key]
    for key, rows in COLUMNS.items():
        a[key + "_col"] = a[key].reshape(-1, rows).T
    for key in UNSPREAD:
        del a[key]
    return {k: np.ascontiguousarray(v) for k, v in a.items()}


def kernel(**inputs):
    import concourse.bacc as bacc
    from concourse.bass_utils import run_bass_kernel_spmd

    arrays = lay_out(inputs)
    nc = bacc.Bacc("TRN2", target_bir_lowering=False, num_devices=1)
    ins = {k: nc.dram_tensor(f"in_{k}", v.shape, mybir.dt.from_np(v.dtype), kind="ExternalInput").ap() for k, v in arrays.items()}
    out = nc.dram_tensor("out", (TOKENS // P, P, DIM), F32, kind="ExternalOutput").ap()
    scratch = {k: nc.dram_tensor(f"scratch_{k}", shape, F32, kind="Internal").ap() for k, shape in SCRATCH.items()}
    vit_tower(nc, ins, out, scratch)
    r = run_bass_kernel_spmd(nc, [{f"in_{k}": v for k, v in arrays.items()}], core_ids=[0])
    return r.results[0]["out"].reshape(IMAGES, SEQ, DIM)
```

```python
from contextlib import ExitStack

import numpy as np

import concourse.bass as bass
from concourse import mybir

F32 = mybir.dt.float32
F32R = mybir.dt.float32r
I32 = mybir.dt.int32
ALU = mybir.AluOpType
ACT = mybir.ActivationFunctionType
AX = mybir.AxisListType.X

IMAGES, SEQ, DIM, HEADS, MLP = 64, 64, 192, 12, 768
PATCH, CHANNELS = 16, 3
FEATS = CHANNELS * PATCH * PATCH
P = 128
HALF = DIM // 2
HD = DIM // HEADS
HH = HEADS // 2
TOKENS = IMAGES * SEQ
GROUP = 512
TILES = GROUP // P
GROUPS = TOKENS // GROUP
KP = FEATS // P
KM = MLP // P
PART = 256
PARTS = TOKENS // PART
UNITS = 2 * TOKENS // P
UPP = 2 * PART // P
UPG = 8
RHD, RH2, BITS = 128, 64, 2
RANK3 = 192
ROW = DIM + 8
EPS = 1e-5
LOGIT_SCALE_MAX = float(np.log(100.0))
NORM_MIN2 = 1e-24
HIGH_BITS = -(1 << 12)
RSQRT_BITS = 0x5F3759DF


def sweep(engine, turns, lags, body):
    for i in range(lags + 1):
        body(i, lambda lag, i=i: 0 <= i - lag < turns)
    with engine.Fori(lags + 1, turns) as i:
        body(i, lambda lag: True)
    for i in range(turns, turns + lags):
        body(i, lambda lag, i=i: 0 <= i - lag < turns)


def sweep_pairs(engine, turns, lags, body):
    for i in range(2):
        body(i, i, lambda lag, i=i: 0 <= i - lag < turns)
    with engine.Fori(1, turns // 2) as pair:
        for a in range(2):
            body(2 * pair + a, a, lambda lag: True)
    for i in range(turns, turns + lags):
        body(i, i % 2, lambda lag, i=i: 0 <= i - lag < turns)


def wait(engine, sem, value):
    if isinstance(value, int) and value <= 0:
        return
    engine.wait_ge(sem, value)


def waits(engine, *pairs):
    values = [v for _, v in pairs]
    for v in values:
        if not isinstance(v, int):
            engine.compute_val(v)
    for (sem, _), value in zip(pairs, values):
        wait(engine, sem, value)


class Memory:

    def __init__(self, nc, ctx, phase):
        self.nc, self.ctx, self.phase, self.held = nc, ctx, phase, []
        ctx.callback(self.clear)

    def clear(self):
        self.nc.clear_and_free_semaphores(self.held)
        self.nc.all_engine_barrier()

    def sb(self, name, shape, dtype=F32):
        return self.ctx.enter_context(self.nc.sbuf_tensor(f"{self.phase}_{name}", shape, dtype))

    def ps(self, name, shape=(P, 512)):
        return self.ctx.enter_context(self.nc.psum_tensor(f"{self.phase}_{name}", list(shape), F32))

    def sem(self, name):
        self.held.append(self.nc.alloc_semaphore(f"{self.phase}_{name}"))
        return self.held[-1]

    def sems(self, name, n):
        return [self.sem(f"{name}{i}") for i in range(n)]


def load_weights(nc, mem, w, ins):
    done = {k: mem.sem(f"loaded_{k}") for k in ("patch_w", "patch", "ff", "tok", "cos", "ffn")}
    counts = dict.fromkeys(done, 0)
    plan = {k: [] for k in done}

    def take(which, dst, src):
        plan[which].append((dst, src))
        counts[which] += 16

    def chunked(which, name, key, rows, chunks, cols, bias=None):
        w[name] = mem.sb(name, [rows + (bias is not None), chunks, cols])
        take(which, w[name][0:rows, :, :], ins[key].rearrange("(c p) n -> p c n", p=rows))
        if bias:
            take(which, w[name][rows:rows + 1, chunks - 1, :], ins[bias].rearrange("(a n) -> a n", a=1))

    def column(which, name, key, rows, chunks):
        w[name] = mem.sb(name, [rows, chunks])
        take(which, w[name][:, :], ins[key + "_col"])

    def spread(which, name, key, cols):
        w[name] = mem.sb(name, [P, cols])
        take(which, w[name][:, :], ins[key].rearrange("(a n) -> a n", a=1).to_broadcast([P, cols]))

    def plain(which, name, key, rows, cols):
        w[name] = mem.sb(name, [rows, cols])
        take(which, w[name][:, :], ins[key])

    chunked("patch_w", "patch_w", "patch_w", P, KP, DIM)
    spread("patch", "patch_b", "tok_patch_b", DIM)
    spread("patch", "ln_g", "tok_ln_g", DIM)
    spread("patch", "ln_b", "tok_ln_b", DIM)
    plain("patch", "pe", "pe", P, DIM)
    plain("patch", "ident", "ident", P, P)
    chunked("ff", "ff1", "tok_ff1_w", HALF, 2, MLP, "tok_ff1_b")
    chunked("ff", "ff2", "tok_ff2_w", P, KM, DIM)
    column("ff", "ff2_col", "tok_ff2_b", HALF, 2)
    spread("ff", "ff2_b", "tok_ff2_b", DIM)
    chunked("tok", "tok_qkv", "tok_qkv_w", HALF, 2, 3 * DIM, "tok_qkv_b")
    chunked("tok", "tok_proj", "tok_proj_w", HALF, 2, DIM, "tok_proj_b")
    chunked("cos", "cos_qkv", "cos_qkv_w", HALF, 2, 3 * DIM, "cos_qkv_b")
    chunked("cos", "cos_proj", "cos_proj_w", HALF, 2, DIM, "attn_out_b")
    spread("cos", "logit_scale", "logit_scale", HEADS)
    column("cos", "head_scale", "head_scale", HALF, 2)
    plain("ffn", "first_token", "first_token", P, 1)
    chunked("ffn", "r_in_raw", "r_in_w", HALF, 2, RHD)
    chunked("ffn", "ffn_qkv_raw", "ffn_qkv_w", HALF, 2, 3 * DIM)
    chunked("ffn", "fc1_raw", "fc1_w", HALF, 2, MLP)
    chunked("ffn", "ffn_proj", "ffn_proj_w", HALF, 2, DIM, "ffn_bo")
    chunked("ffn", "fc2", "fc2_w", P, KM, DIM)
    spread("ffn", "fc2_b", "ffn_fc2_b", DIM)
    chunked("ffn", "r_o1", "r_o1_w", RHD, 2, RHD)
    column("ffn", "r_o1_b", "ffn_r_o1_b", RHD, 1)
    plain("ffn", "r_o2", "r_o2_w", RHD, RH2)
    column("ffn", "r_o2_b", "ffn_r_o2_b", RH2, 1)
    w["r_o3"] = mem.sb("r_o3", [RH2 + 1, 2 * BITS])
    take("ffn", w["r_o3"][0:RH2, :], ins["r_o3_w"])
    take("ffn", w["r_o3"][RH2:RH2 + 1, :], ins["ffn_r_o3_b"].rearrange("(a n) -> a n", a=1))
    chunked("ffn", "lra_down", "lra_down", HALF, 2, RANK3)
    chunked("ffn", "lra_up", "lra_up", HALF, 2, DIM)
    for name in ("r_ln_g", "r_ln_b", "ln1_g", "ln1_b", "ln2_g", "ln2_b"):
        column("ffn", name, "ffn_" + name, HALF, 2)
    w["fold_bias"] = mem.sb("fold_bias", [1, RHD + 3 * DIM + MLP])
    for at, key, n in ((0, "ffn_r_in_b", RHD), (RHD, "ffn_qkv_b", 3 * DIM), (RHD + 3 * DIM, "ffn_fc1_b", MLP)):
        take("ffn", w["fold_bias"][0:1, at:at + n], ins[key].rearrange("(a n) -> a n", a=1))
    w["done"], w["counts"], w["plan"] = done, counts, plan


def start_loads(engine, w, which):
    for dst, src in w["plan"][which]:
        engine.dma_start(dst, src).then_inc(w["done"][which], 16)


def layer(pe, out, lhs, rhs):
    for n, (a, b) in enumerate(zip(lhs, rhs)):
        last = pe.matmul(out, a, b, start=(n == 0), stop=(n == len(lhs) - 1))
    return last


def keep_warm(pe, tile, bank, n):
    for _ in range(n):
        pe.matmul(bank[:, 0:P], tile[:, 0:P], tile[:, 0:P], start=True, stop=True)


def split_layer(pe, out, lhs, rhs):
    pairs = [(a[m], b[n]) for a, b in zip(lhs, rhs) for m, n in ((0, 0), (0, 1), (1, 0))]
    for n, (a, b) in enumerate(pairs):
        last = pe.matmul(out, a, b, start=(n == 0), stop=(n == len(pairs) - 1))
    return last


def split(dve, x, masked, high, low, steps, n):
    dve.tensor_scalar(masked.bitcast(I32), x.bitcast(I32), HIGH_BITS, None, ALU.bitwise_and).then_inc(steps, 1)
    wait(dve, steps, n + 1)
    dve.tensor_copy(high, masked).then_inc(steps, 1)
    return dve.tensor_tensor(low, x, masked, ALU.subtract)


def split_weights(dve, w, name, steps):
    for c in range(2):
        last = split(dve, *(w[x][0:HALF + c, c, :] for x in (name, "masked", f"{name}_high", f"{name}_low")), steps, 2 * c)
    return last


def split_chunk(high, low, k):
    return [(high[0:HALF + c, c, span(k, P)], low[0:HALF + c, c, span(k, P)]) for c in range(2)]


def split_halves(x):
    return [(x[0:HALF + c, 0, c, :], x[0:HALF + c, 1, c, :]) for c in range(2)]


def halves(x, cols):
    return [x[0:HALF, 0, cols], x[0:HALF + 1, 1, cols]]


def span(n, size):
    return slice(n * size, (n + 1) * size)



def patch_phase(nc, w, patches, x1_dram, y_dram):
    with ExitStack() as ctx:
        mem = Memory(nc, ctx, "patch")
        raw = mem.sb("raw", [P, 2, KP, GROUP])
        xr = mem.sb("xr", [P, TILES, DIM])
        stats = mem.sb("stats", [P, TILES, 6])
        mv = mem.sb("mv", [P, TILES, 2])
        vare = mem.sb("vare", [P, TILES])
        power = mem.sb("power", [P, TILES])
        rstd = mem.sb("rstd", [P, TILES])
        idle = mem.sb("idle", [P, P])
        posb = mem.sb("posb", [P, DIM])
        xn = mem.sb("xn", [P, TILES, DIM])
        xg = mem.sb("xg", [P, TILES, DIM])
        x1 = mem.sb("x1", [P, TILES, DIM])
        xm = mem.sb("xm", [HALF, GROUP])
        xT = mem.sb("xT", [HALF + 1, 2, 2, GROUP], F32R)
        hT = mem.sb("hT", [P, KM, GROUP])
        y = mem.sb("y", [P, TILES, DIM])
        yT = mem.sb("yT", [HALF, 2, GROUP])
        ps_patch = [mem.ps(f"ps_patch{i}") for i in range(2)]
        ps_t = [mem.ps(f"ps_t{i}") for i in range(2)]
        ps_h = [mem.ps(f"ps_h{i}") for i in range(2)]
        ps_y = [mem.ps(f"ps_y{i}") for i in range(2)]

        raw_loaded = mem.sems("raw_loaded", 2)
        const_set = mem.sem("const_set")
        idle_set = mem.sem("idle_set")
        posb_set = mem.sem("posb_set")
        patched = mem.sem("patched")
        evacuated = mem.sem("evacuated")
        counted = mem.sem("counted")
        measured = mem.sem("measured")
        varied = mem.sem("varied")
        rooted = mem.sem("rooted")
        normed = mem.sem("normed")
        gained = mem.sem("gained")
        placed = mem.sem("placed")
        turned = mem.sem("turned")
        weight_step = mem.sem("weight_step")
        weight_split = mem.sem("weight_split")
        xt_step = mem.sem("xt_step")
        xt_ready = mem.sem("xt_ready")
        hidden = mem.sem("hidden")
        gelued = mem.sem("gelued")
        y_summed = mem.sem("y_summed")
        y_copied = mem.sem("y_copied")
        y_turned = mem.sem("y_turned")
        y_ready = mem.sem("y_ready")
        x1_stored = mem.sem("x1_stored")
        y_stored = mem.sem("y_stored")

        with nc.Block() as block:

            @block.sync
            def _(sp):
                start_loads(sp, w, "patch_w")
                sp.dma_start(raw[:, 0, :, :], patches[0]).then_inc(raw_loaded[0], 16)
                start_loads(sp, w, "patch")
                start_loads(sp, w, "ff")

                def turn(i, par, active):
                    if active(0) and not (isinstance(i, int) and i == 0):
                        wait(sp, patched, TILES * (i - 1))
                        sp.dma_start(raw[:, par, :, :], patches[i]).then_inc(raw_loaded[par], 16)
                    if isinstance(i, int) and i == 1:
                        for which in ("tok", "cos", "ffn"):
                            start_loads(sp, w, which)
                    if active(1):
                        wait(sp, placed, TILES * i)
                        sp.dma_start(x1_dram[i - 1], x1[:, :, :]).then_inc(x1_stored, 16)

                sweep_pairs(sp, GROUPS, 1, turn)
                sp.wait_ge(y_stored, 32)
                for j in range(2):
                    sp.dma_start(w["part_xT"][0:HALF, j, :, :], y_dram[j]).then_inc(w["tok_x_loaded"][j], 16)
                sp.wait_ge(x1_stored, 16 * GROUPS)
                sp.wait_ge(y_stored, 32 * GROUPS)

            @block.tensor
            def _(pe):
                pe.wait_ge(idle_set, 1)
                keep_warm(pe, idle, ps_h[0], 16)
                pe.wait_ge(w["done"]["patch_w"], w["counts"]["patch_w"])
                pe.wait_ge(const_set, 3)

                def patch_tile(i, par, t):
                    wait(pe, evacuated, TILES * i + t - 1)
                    layer(pe, ps_patch[t % 2][:, 0:DIM],
                          [raw[:, par, k, span(t, P)] for k in range(KP)],
                          [w["patch_w"][:, k, :] for k in range(KP)]).then_inc(patched, 1)

                def turn(i, par, active):
                    if active(0):
                        wait(pe, raw_loaded[par], 16 * (i // 2 + 1) if isinstance(i, int) else 8 * (i - par) + 16)
                        patch_tile(i, par, 0)
                        patch_tile(i, par, 1)
                    if isinstance(i, int) and i == 1:
                        keep_warm(pe, idle, ps_h[0], 12)
                    if active(1):
                        wait(pe, w["done"]["patch"], w["counts"]["patch"])
                        wait(pe, placed, TILES * i)
                        for c in range(2):
                            wait(pe, xt_ready, 2 * (i - 2) + c + 1 if not (isinstance(i, int) and i < 2) else 0)
                            for t in range(TILES):
                                last = pe.transpose(ps_t[c][0:HALF, span(t, P)], x1[:, t, span(c, HALF)], w["ident"][:, :])
                            last.then_inc(turned, 1)
                    if active(0):
                        patch_tile(i, par, 2)
                        patch_tile(i, par, 3)
                    if active(1):
                        wait(pe, w["done"]["ff"], w["counts"]["ff"])
                        if isinstance(i, int) and i == GROUPS:
                            wait(pe, y_ready, 2 * (i - 1))
                            keep_warm(pe, idle, ps_h[0], 14)
                        wait(pe, weight_split, 1)
                        wait(pe, xt_ready, 2 * i)
                        for k in range(KM):
                            if k < 2:
                                wait(pe, y_ready, 2 * (i - 1))
                            else:
                                wait(pe, gelued, KM * (i - 1) + k - 1)
                            split_layer(pe, ps_h[k % 2][:, :], split_chunk(w["ff1_high"], w["ff1_low"], k),
                                        split_halves(xT)).then_inc(hidden, 1)
                        for t in range(TILES):
                            wait(pe, y_copied, TILES * (i - 1) + t - 1)
                            for k in range(KM):
                                if t == 0:
                                    wait(pe, gelued, KM * (i - 1) + k + 1)
                                last = pe.matmul(ps_y[t % 2][:, 0:DIM], hT[:, k, span(t, P)], w["ff2"][:, k, :],
                                                 start=(k == 0), stop=(k == KM - 1))
                            last.then_inc(y_summed, 1)
                        for t in range(TILES):
                            wait(pe, y_copied, TILES * (i - 1) + t + 1)
                            for c in range(2):
                                last = pe.transpose(ps_h[c][0:HALF, span(t, P)], y[:, t, span(c, HALF)], w["ident"][:, :])
                        last.then_inc(y_turned, 1)

                sweep_pairs(pe, GROUPS, 1, turn)

            @block.scalar
            def _(act):
                act.wait_ge(w["done"]["ff"], w["counts"]["ff"])

                def turn(i, par, active):
                    if active(1):
                        for k in range(KM):
                            wait(act, hidden, KM * (i - 1) + k + 1)
                            act.activation(hT[:, k, :], ps_h[k % 2][:, :], ACT.Gelu_apprx_tanh).then_inc(gelued, 1)
                        for t in range(TILES):
                            wait(act, y_summed, TILES * (i - 1) + t + 1)
                            wait(act, y_turned, i - 1)
                            act.activation(y[:, t, :], ps_y[t % 2][:, 0:DIM], ACT.Copy).then_inc(y_copied, 1)
                        for c in range(2):
                            wait(act, y_turned, i)
                            wait(act, y_stored, 32 * (i - 1))
                            act.activation(yT[:, c, :], ps_h[c][0:HALF, :], ACT.Identity,
                                           bias=w["ff2_col"][:, c:c + 1]).then_inc(y_ready, 1)
                        wait(act, y_ready, 2 * i)
                        for a in range(2):
                            act.dma_start(y_dram[2 * (i - 1) + a], yT[:, :, span(a, PART)]).then_inc(y_stored, 16)

                sweep_pairs(act, GROUPS, 1, turn)

            @block.gpsimd
            def _(pool):
                pool.memset(power[:, :], -0.5).then_inc(const_set, 1)
                pool.wait_ge(w["done"]["patch"], w["counts"]["patch"])
                pool.tensor_tensor(posb[:, :], w["ln_b"][:, :], w["pe"][:, :], ALU.add).then_inc(posb_set, 1)
                pool.wait_ge(const_set, 3)
                pool.wait_ge(posb_set, 1)

                def turn(i, par, active):
                    if active(0):
                        wait(pool, varied, i + 1)
                        pool.tensor_tensor(rstd[:, :], vare[:, :], power[:, :], ALU.pow).then_inc(rooted, 1)
                        for t in range(TILES):
                            wait(pool, normed, TILES * i + t + 1)
                            pool.tensor_tensor(xg[:, t, :], xn[:, t, :], w["ln_g"][:, :], ALU.mult).then_inc(gained, 1)
                        wait(pool, x1_stored, 16 * i)
                        wait(pool, turned, 2 * i)
                        for t in range(TILES):
                            wait(pool, gained, TILES * i + t + 1)
                            pool.tensor_tensor(x1[:, t, :], xg[:, t, :], posb[:, :], ALU.add).then_inc(placed, 1)

                sweep_pairs(pool, GROUPS, 1, turn)

            @block.vector
            def _(dve):
                dve.memset(idle[:, :], 0.0).then_inc(idle_set, 1)
                dve.memset(xT[HALF:HALF + 1, 0, 1, :].bitcast(F32), 1.0)
                dve.memset(xT[HALF:HALF + 1, 1, 1, :].bitcast(F32), 0.0).then_inc(const_set, 1)
                dve.memset(w["part_xT"][HALF:HALF + 1, :, 1, :], 1.0).then_inc(const_set, 1)
                dve.wait_ge(w["done"]["patch"], w["counts"]["patch"])

                def measure(i, t):
                    wait(dve, normed, TILES * i)
                    wait(dve, patched, TILES * i + t + 1)
                    dve.tensor_tensor(xr[:, t, :], ps_patch[t % 2][:, 0:DIM], w["patch_b"][:, :], ALU.add).then_inc(evacuated, 1)
                    wait(dve, evacuated, TILES * i + t + 1)
                    dve.bn_stats(stats[:, t, :], xr[:, t, :]).then_inc(counted, 1)
                    dve.drain()
                    dve.bn_aggr(mv[:, t, :], stats[:, t, :]).then_inc(measured, 1)

                def turn(i, par, active):
                    if active(0):
                        measure(i, 0)
                        measure(i, 1)
                    if active(1):
                        for c in range(2):
                            wait(dve, turned, 2 * (i - 1) + c + 1)
                            wait(dve, hidden, KM * (i - 1))
                            wait(dve, xt_ready, 2 * (i - 1) + c)
                            split(dve, ps_t[c][0:HALF, :], xm[:, :], xT[0:HALF, 0, c, :], xT[0:HALF, 1, c, :],
                                  xt_step, 4 * (i - 1) + 2 * c).then_inc(xt_ready, 1)
                    if active(0):
                        measure(i, 2)
                        measure(i, 3)
                        wait(dve, measured, TILES * i + TILES)
                        dve.tensor_scalar(vare[:, :], mv[:, :, 1], EPS, None, ALU.add).then_inc(varied, 1)
                        wait(dve, rooted, i + 1)
                        wait(dve, gained, TILES * i)
                        for t in range(TILES):
                            dve.tensor_scalar(xn[:, t, :], xr[:, t, :], mv[:, t, 0:1], rstd[:, t:t + 1],
                                              ALU.subtract, ALU.mult).then_inc(normed, 1)
                    if isinstance(i, int) and i == 0:
                        dve.wait_ge(w["done"]["ff"], w["counts"]["ff"])
                        split_weights(dve, w, "ff1", weight_step).then_inc(weight_split, 1)

                sweep_pairs(dve, GROUPS, 1, turn)



def attention_phase(nc, w, kind, x_src, res_dram, out_dram, big, first_group=None):
    cos = kind == "cos"
    qkv_w = w[{"tok": "tok_qkv", "cos": "cos_qkv", "ffn": "ffn_qkv"}[kind]]
    proj_w = w[{"tok": "tok_proj", "cos": "cos_proj", "ffn": "ffn_proj"}[kind]]
    loaded = w["done"][kind], w["counts"][kind]
    L_S, L_V, L_VCOPY = (10, 6, 9) if cos else (4, 3, 4)
    L_SUM, L_T, L_PV = L_S + 1, L_S + 3, L_S + 4
    L_O = L_PV if cos else L_PV + 1
    L_PROJ = L_PV + 1
    L_N = 6
    row = ROW if kind == "ffn" else DIM
    score_scale = 1.0 if cos else float(HD) ** -0.5
    Q0, K0, V0 = 0, DIM, 2 * DIM

    with ExitStack() as ctx:
        mem = Memory(nc, ctx, kind)
        xT = w["part_xT"]
        qkT = mem.sb("qkT", [P, 2, 4, PART])
        kmask = mem.sb("kmask", [P, 2, 2, HH, PART])
        vblk = mem.sb("vblk", [P, 2, 4, HH, 2 * HD])
        rowmax = mem.sb("rowmax", [P, 2, HH])
        shifted = mem.sb("shifted", [P, 2, HH, SEQ])
        probs = mem.sb("probs", [P, 4, HH, SEQ])
        total = mem.sb("total", [P, 2, HH])
        rtotal = mem.sb("rtotal", [P, 2, HH])
        probsT = mem.sb("probsT", [P, 2, 3, P])
        if cos:
            qk = mem.sb("qk", [P, 2, 2 * DIM])
            square = mem.sb("square", [P, 2, 2 * DIM])
            norm2 = mem.sb("norm2", [P, 2, 2 * HEADS])
            floor2 = mem.sb("floor2", [P, 2, 2 * HEADS])
            rnorm = mem.sb("rnorm", [P, 2, 2 * HEADS])
            half_sq = mem.sb("half_sq", [P, 2, 2 * HEADS])
            product = mem.sb("product", [P, 2, 2 * HEADS])
            squares = mem.sb("squares", [P, 2, 2 * HEADS])
            parts = mem.sb("parts", [P, 2, 2 * HEADS])
            factor = mem.sb("factor", [P, 2, 2 * HEADS])
            minus_half = mem.sb("minus_half", [P, 2, 2 * HEADS])
            three_halves = mem.sb("three_halves", [P, 2, 2 * HEADS])
            scaled = mem.sb("scaled", [P, 2, 2 * HEADS])
            qk_scale = mem.sb("qk_scale", [P, 2, 2 * HEADS])
            scale_min = mem.sb("scale_min", [P, HEADS])
            gain = mem.sb("gain", [P, 2 * HEADS])
            qkn = mem.sb("qkn", [P, 2, 2 * DIM])
        else:
            x_masked = mem.sb("x_masked", [HALF + 1, 2, PART])
            xs = mem.sb("xs", [HALF + 1, 2, 2, 2, PART], F32R)
            qk_high = mem.sb("qk_high", [HALF + 1, 2, 2 * DIM], F32R)
            qk_low = mem.sb("qk_low", [HALF + 1, 2, 2 * DIM], F32R)
            oT = mem.sb("oT", [HALF + 1, 2, 2, P])
            res = mem.sb("res", [P, 2, 2, row])
            outb = mem.sb("outb", [P, 2, 2, DIM])
        ps_s = [mem.ps(f"ps_s{i}") for i in range(2)]
        ps_pt = [mem.ps(f"ps_pt{i}") for i in range(2)]
        ps_o = mem.ps("ps_o")
        ps_x = [mem.ps(f"ps_x{i}") for i in range(2)]
        ps_r = mem.ps("ps_r")
        ps_v = ps_r if cos else ps_x[1]

        zeros_set = mem.sem("zeros_set")
        kmask_zeroed = mem.sem("kmask_zeroed")
        x_loaded = w[f"{kind}_x_loaded"]
        v_mm, v_ready = mem.sem("v_mm"), mem.sem("v_ready")
        kmask_loaded = mem.sems("kmask_loaded", 2)
        scored = mem.sem("scored")
        maxed = mem.sem("maxed")
        shift_done = mem.sem("shift_done")
        exped = mem.sem("exped")
        summed = mem.sem("summed")
        inverted = mem.sem("inverted")
        weighted = mem.sem("weighted")
        turned = mem.sem("turned")
        pt_ready = mem.sem("pt_ready")
        mixed = mem.sem("mixed")
        o_ready = mem.sem("o_ready")
        if cos:
            qk_mm = mem.sem("qk_mm")
            squared = mem.sem("squared")
            qk_copied = mem.sem("qk_copied")
            norm_summed = mem.sem("norm_summed")
            floored = mem.sem("floored")
            guessed = mem.sem("guessed")
            refined = mem.sem("refined")
            newton = mem.sem("newton")
            qkn_ready = mem.sem("qkn_ready")
            qkt = mem.sem("qkt")
            qk_ready = mem.sem("qk_ready")
            capped, gain_set = mem.sem("capped"), mem.sem("gain_set")
            RS, NS = 8, 4
        else:
            k_mm, q_mm = mem.sem("k_mm"), mem.sem("q_mm")
            k_ready, q_ready = mem.sem("k_ready"), mem.sem("q_ready")
            w_step, w_split = mem.sem("w_step"), mem.sem("w_split")
            x_step, x_split = mem.sem("x_step"), mem.sem("x_split")
            projected = mem.sem("projected")
            out_ready = mem.sem("out_ready")
            res_loaded = mem.sems("res_loaded", 2)
            stored = mem.sems("stored", 2)

        def part(i, u, lag):
            q, r = divmod(u - lag, UPP)
            return 2 * i + q, q % 2, i + q // 2, r

        def run(engine, step, peeled=0):
            turns = UNITS // UPG
            for i in range(2):
                for u in range(UPG):
                    step(i, u, lambda lag, i=i, u=u: 0 <= i * UPG + u - lag < UNITS)
            with engine.Fori(2, turns - peeled) as i:
                for u in range(UPG):
                    step(i, u, lambda lag: True)
            for i in range(turns - peeled, turns + 2):
                for u in range(UPG):
                    step(i, u, lambda lag, i=i, u=u: 0 <= i * UPG + u - lag < UNITS)

        with nc.Block() as block:

            @block.sync
            def _(sp):
                def load(j, par):
                    wait(sp, v_mm, j - 1)
                    sp.dma_start(xT[0:HALF, par, :, :], x_src(j)).then_inc(x_loaded[par], 16)

                def load_res(j, par):
                    wait(sp, out_ready, 2 * (j - 1))
                    sp.dma_start(res[:, par, :, :], res_dram[j]).then_inc(res_loaded[par], 16)

                for j in range(2):
                    if cos:
                        load(j, j)
                    else:
                        load_res(j, j)

                def step(i, u, active):
                    lag, at = (7, 0) if cos else (0, 1)
                    j, par, _, r = part(i, u, lag)
                    if active(lag) and r == at:
                        waits(sp, (qk_ready if cos else k_ready, 2 * j + 2 if cos else j + 1), (scored, UPP * (j - 1)))
                        if isinstance(j, int):
                            wait(sp, kmask_zeroed, min(j + 1, 2))
                        for h in range(HH):
                            rows = span(h, HD)
                            sp.dma_start(kmask[rows, par, :, h, :], qkT[rows, par, 2:4, :]).then_inc(kmask_loaded[par], 16)
                    if not cos:
                        j, par, _, r = part(i, u, L_PROJ + 1)
                        if active(L_PROJ + 1) and r == UPP - 1:
                            wait(sp, out_ready, 2 * (j + 1))
                            sp.dma_start(out_dram[j], outb[:, par, :, :]).then_inc(stored[par], 16)
                            if not (isinstance(j, int) and j + 2 >= PARTS):
                                load_res(j + 2, par)
                    j, par, _, r = part(i, u, L_V)
                    if active(L_V) and r == 0 and not (isinstance(j, int) and j + 2 >= PARTS):
                        load(j + 2, par)

                run(sp, step, peeled=1)
                if not cos:
                    for s in stored:
                        sp.wait_ge(s, 16)
                    sp.dma_start(w["group_x"][:, :, :], first_group).then_inc(w[f"{kind}_group_loaded"], 16)
                    for s in stored:
                        sp.wait_ge(s, 16 * PARTS // 2)

            @block.tensor
            def _(pe):
                pe.wait_ge(*loaded)

                def project_part(out, cols, j, par, into):
                    first = isinstance(j, int) and j == 0
                    if not first:
                        wait(pe, w_split, 1)
                        wait(pe, x_split, j)
                    for m in range(2):
                        c0 = cols + m * HALF
                        if not first:
                            last = split_layer(pe, out[0:HALF, span(m, PART)],
                                               [[y[0:HALF + c, c, c0:c0 + HALF] for y in (qk_high, qk_low)] for c in range(2)],
                                               [[xs[0:HALF + c, par, z, c, :] for z in range(2)] for c in range(2)])
                            continue
                        last = layer(pe, out[0:HALF, span(m, PART)],
                                     [qkv_w[0:HALF, 0, c0:c0 + HALF], qkv_w[0:HALF + 1, 1, c0:c0 + HALF]],
                                     [xT[0:HALF, par, 0, :], xT[0:HALF + 1, par, 1, :]])
                    last.then_inc(into, 1)

                def project_values(i, u, active):
                    j, par, before, r = part(i, u, L_V)
                    if active(L_V) and r == 0:
                        if cos:
                            wait(pe, v_ready, j)
                        else:
                            wait(pe, q_ready, j + 1)
                        for a in range(4):
                            for c in range(2):
                                rows = HALF + c
                                for odd in range(2):
                                    c0 = V0 + odd * HALF
                                    last = pe.matmul(ps_v[span(odd, SEQ), span(a, HALF)], xT[0:rows, par, c, span(a, SEQ)],
                                                     qkv_w[0:rows, c, c0:c0 + HALF], start=(c == 0), stop=(c == 1))
                        last.then_inc(v_mm, 1)

                def step(i, u, active):
                    if active(L_S):
                        n, (j, par, before, r) = UPG * i + (u - L_S), part(i, u, L_S)
                        c, t, ring = r % 2, r // 2, (u - L_S) % 2
                        if isinstance(j, int) and j == 0:
                            wait(pe, zeros_set, 2)
                        if r == 0:
                            wait(pe, kmask_loaded[par], 16 * HH * (before + 1))
                            wait(pe, qk_ready if cos else q_ready, 2 * j + 2 if cos else j + 1)
                        wait(pe, shift_done, n - 1)
                        for a in range(2):
                            cols = slice(t * P + a * SEQ, t * P + (a + 1) * SEQ)
                            last = pe.matmul(ps_s[ring][span(a, SEQ), 0:HH * SEQ], qkT[:, par, c, cols],
                                             kmask[:, par, c, :, cols], start=True, stop=True)
                        last.then_inc(scored, 1)
                    if active(L_T):
                        n, ring = UPG * i + (u - L_T), (u - L_T) % 2
                        wait(pe, weighted, n + 1)
                        wait(pe, pt_ready, n - 1)
                        for b in range(3):
                            last = pe.transpose(ps_pt[ring][:, span(b, P)],
                                                probs[:, (u - L_T) % 4, 2 * b:2 * b + 2, :].rearrange("p h k -> p (h k)"),
                                                w["ident"][:, :])
                        last.then_inc(turned, 1)
                    j, par, before, r = part(i, u, L_N)
                    if cos and active(L_N) and r == 0:
                        for t in range(2):
                            wait(pe, qkn_ready, 2 * j + t + 1)
                            wait(pe, qk_copied, 2 * min(j + 1, PARTS - 1) + t + 1 if isinstance(j, int) else 2 * (j + 1) + t + 1)
                            for m in range(4):
                                last = pe.transpose(ps_x[t][0:HALF, span(m, P)], qkn[:, t, span(m, HALF)], w["ident"][:, :])
                            last.then_inc(qkt, 1)
                    j, par, before, r = part(i, u, 0)
                    if active(0) and not cos and r == 0:
                        wait(pe, x_loaded[par], 16 * (before + 1))
                        wait(pe, k_ready, j)
                        project_part(ps_x[0], K0, j, par, k_mm)
                    if active(0) and not cos and r == 1:
                        wait(pe, v_ready, j)
                        project_part(ps_x[1], Q0, j, par, q_mm)
                    if not cos:
                        project_values(i, u, active)
                    if active(L_PV):
                        n, (j, par, before, r) = UPG * i + (u - L_PV), part(i, u, L_PV)
                        c, t, ring = r % 2, r // 2, (u - L_PV) % 2
                        if r == 0:
                            wait(pe, v_ready, j + 1)
                        wait(pe, pt_ready, n + 1)
                        if c == 0:
                            wait(pe, o_ready, 2 * j + t)
                        for a in range(2):
                            for b in range(3):
                                last = pe.matmul(ps_o[span(b, 2 * HD), c * P + a * SEQ:c * P + (a + 1) * SEQ],
                                                 vblk[:, par, 2 * t + a, 3 * c + b, :], probsT[:, ring, b, span(a, SEQ)],
                                                 start=True, stop=True)
                        last.then_inc(mixed, 1)
                    if cos:
                        project_values(i, u, active)
                    j, par, before, r = part(i, u, 0)
                    if active(0) and cos and r == 0:
                        wait(pe, x_loaded[par], 16 * (before + 1))
                        for t in range(2):
                            wait(pe, qk_ready, 2 * (j - 2) + t + 1 if not (isinstance(j, int) and j < 2) else 0)
                            wait(pe, qk_copied, 2 * (j - 1) + t + 1 if not (isinstance(j, int) and j < 1) else 0)
                            layer(pe, ps_x[t][:, 0:2 * DIM], [xT[0:HALF, par, 0, span(t, P)], xT[0:HALF + 1, par, 1, span(t, P)]],
                                  [qkv_w[0:HALF, 0, 0:2 * DIM], qkv_w[0:HALF + 1, 1, 0:2 * DIM]]).then_inc(qk_mm, 1)
                    if not cos and active(L_PROJ):
                        j, par, before, r = part(i, u, L_PROJ)
                        if r % 2:
                            t = r // 2
                            wait(pe, o_ready, 2 * j + t + 1)
                            wait(pe, out_ready, 2 * j + t)
                            layer(pe, ps_r[:, 0:DIM], [oT[0:HALF, t, 0, :], oT[0:HALF + 1, t, 1, :]],
                                  [proj_w[0:HALF, 0, :], proj_w[0:HALF + 1, 1, :]]).then_inc(projected, 1)

                run(pe, step)

            @block.scalar
            def _(act):
                if cos:
                    act.wait_ge(capped, 1)
                    act.activation(gain[:, 0:HEADS], scale_min[:, :], ACT.Exp).then_inc(gain_set, 1)

                def finish_tile(i, u, active):
                    j, par, before, r = part(i, u, L_O)
                    if active(L_O) and r % 2:
                        t = r // 2
                        wait(act, mixed, UPP * j + 2 * t + 2)
                        source = ps_o[0:HALF, 0:2 * P].rearrange("p (c t) -> p c t", c=2)
                        if cos:
                            act.activation(big[0:HALF, :, bass.ds(P * (2 * j + t), P)], source, ACT.Copy).then_inc(o_ready, 1)
                        else:
                            wait(act, projected, 2 * j + t - 1)
                            act.activation(oT[0:HALF, t, :, :], source, ACT.Copy).then_inc(o_ready, 1)

                def step(i, u, active):
                    if not cos:
                        finish_tile(i, u, active)
                    j, par, before, r = part(i, u, 0)
                    if active(0) and cos and r == 1:
                        for t in range(2):
                            wait(act, qk_mm, 2 * j + t + 1)
                            wait(act, norm_summed, 2 * (j - 1) + t + 1 if not (isinstance(j, int) and j == 0) else 0)
                            act.activation(square[:, t, :], ps_x[t][:, 0:2 * DIM], ACT.Square).then_inc(squared, 1)
                            wait(act, qkn_ready, 2 * (j - 1) + t + 1 if not (isinstance(j, int) and j == 0) else 0)
                            act.activation(qk[:, t, :], ps_x[t][:, 0:2 * DIM], ACT.Copy).then_inc(qk_copied, 1)
                    if active(L_T):
                        n, ring = UPG * i + (u - L_T), (u - L_T) % 2
                        wait(act, turned, n + 1)
                        wait(act, mixed, n - 1)
                        act.activation(probsT[:, ring, :, :].rearrange("p b q -> p (b q)"), ps_pt[ring][:, 0:3 * P],
                                       ACT.Copy).then_inc(pt_ready, 1)
                    if cos:
                        finish_tile(i, u, active)
                    if active(L_S):
                        n = UPG * i + (u - L_S)
                        wait(act, shift_done, n + 1)
                        wait(act, turned, n - 3)
                        act.activation(probs[:, (u - L_S) % 4, :, :], shifted[:, (u - L_S) % 2, :, :], ACT.Exp,
                                       scale=score_scale).then_inc(exped, 1)
                    j, par, before, r = part(i, u, 0)
                    if active(0) and not cos and r == 1:
                        wait(act, q_mm, j + 1)
                        wait(act, scored, UPP * (j - 1))
                        act.activation(qkT[0:HALF, par, 0:2, :], ps_x[1][0:HALF, :].rearrange("p (c t) -> p c t", c=2),
                                       ACT.Copy).then_inc(q_ready, 1)
                    j, par, before, r = part(i, u, L_N)
                    if cos and active(L_N) and r == 0:
                        for t in range(2):
                            wait(act, qkt, 2 * j + t + 1)
                            if t == 0:
                                wait(act, scored, UPP * (j - 1))
                                wait(act, kmask_loaded[par], 16 * HH * before)
                            act.activation(qkT[0:HALF, par, :, span(t, P)],
                                           ps_x[t][0:HALF, :].rearrange("p (c t) -> p c t", c=4), ACT.Copy).then_inc(qk_ready, 1)
                    j, par, before, r = part(i, u, L_VCOPY)
                    if active(L_VCOPY) and r == 0:
                        wait(act, v_mm, j + 1)
                        if isinstance(j, int) and j == 0:
                            wait(act, zeros_set, 2)
                        wait(act, mixed, UPP * (j - 1))
                        for odd in range(2):
                            last = act.activation(vblk[span(odd, SEQ), par, :, :, span(odd, HD)],
                                                   ps_v[span(odd, SEQ), 0:4 * HALF].rearrange("p (a b d) -> p a b d", a=4, d=HD),
                                                  ACT.Copy)
                        last.then_inc(v_ready, 1)

                run(act, step)

            @block.gpsimd
            def _(pool):
                pool.memset(kmask[:, 0, :, :, :], 0.0).then_inc(kmask_zeroed, 1)
                pool.memset(kmask[:, 1, :, :, :], 0.0).then_inc(kmask_zeroed, 1)

                if cos:
                    pool.wait_ge(gain_set, 2)

                def newton_step(n):
                    pool.tensor_tensor(squares[:, :, :], rnorm[:, :, :], rnorm[:, :, :], ALU.mult).then_inc(refined, 1)
                    wait(pool, refined, n + 1)
                    pool.tensor_tensor(parts[:, :, :], squares[:, :, :], minus_half[:, :, :], ALU.mult).then_inc(refined, 1)
                    wait(pool, refined, n + 2)
                    pool.tensor_tensor(factor[:, :, :], parts[:, :, :], three_halves[:, :, :], ALU.add).then_inc(refined, 1)
                    wait(pool, refined, n + 3)
                    pool.tensor_tensor(rnorm[:, :, :], rnorm[:, :, :], factor[:, :, :], ALU.mult).then_inc(refined, 1)

                def step(i, u, active):
                    if active(L_SUM):
                        n, ring = UPG * i + (u - L_SUM), (u - L_SUM) % 4
                        wait(pool, inverted, n + 1)
                        pool.tensor_tensor(probs[:, ring, :, :], probs[:, ring, :, :],
                                           rtotal[:, ring % 2, :].unsqueeze(2).to_broadcast([P, HH, SEQ]),
                                           ALU.mult).then_inc(weighted, 1)
                    j, par, before, r = part(i, u, 0)
                    if cos and active(0) and r == 1:
                        wait(pool, guessed, j + 1)
                        newton_step(RS * j)
                    if cos and active(0) and r == 2:
                        wait(pool, refined, RS * j + 4)
                        newton_step(RS * j + 4)

                run(pool, step)

            @block.vector
            def _(dve):
                dve.memset(qkT[HALF:P, :, :, :], 0.0).then_inc(zeros_set, 1)
                if not cos:
                    dve.memset(oT[HALF:HALF + 1, :, 1, :], 1.0)
                dve.memset(vblk[:, :, :, :, :], 0.0).then_inc(zeros_set, 1)
                if cos:
                    dve.wait_ge(*loaded)
                    dve.tensor_scalar(scale_min[:, :], w["logit_scale"][:, :], LOGIT_SCALE_MAX, None, ALU.min).then_inc(capped, 1)
                    dve.memset(three_halves[:, :, :], 1.5)
                    dve.memset(gain[:, HEADS:2 * HEADS], 1.0).then_inc(gain_set, 1)
                    dve.wait_ge(gain_set, 2)

                def step(i, u, active):
                    if not cos:
                        j, par, before, r = part(i, u, L_PROJ + 1)
                        if active(L_PROJ + 1) and r % 2:
                            t = r // 2
                            wait(dve, projected, 2 * j + t + 1)
                            wait(dve, res_loaded[par], 16 * (before + 1))
                            wait(dve, stored[par], 16 * before)
                            if kind == "tok":
                                dve.tensor_tensor(outb[:, par, t, :], ps_r[:, 0:DIM], res[:, par, t, :], ALU.add).then_inc(out_ready, 1)
                            else:
                                dve.scalar_tensor_tensor(outb[:, par, t, :], ps_r[:, 0:DIM], res[:, par, t, DIM:DIM + 1],
                                                         res[:, par, t, 0:DIM], ALU.mult, ALU.add).then_inc(out_ready, 1)
                    if active(L_S):
                        n, ring = UPG * i + (u - L_S), (u - L_S) % 2
                        scores = ps_s[ring][:, 0:HH * SEQ].rearrange("p (h k) -> p h k", k=SEQ)
                        wait(dve, scored, n + 1)
                        dve.tensor_reduce(rowmax[:, ring, :], scores, AX, ALU.max).then_inc(maxed, 1)
                        wait(dve, maxed, n + 1)
                        wait(dve, exped, n - 1)
                        dve.tensor_tensor(shifted[:, ring, :, :], scores,
                                          rowmax[:, ring, :].unsqueeze(2).to_broadcast([P, HH, SEQ]), ALU.subtract).then_inc(shift_done, 1)
                    if active(L_SUM):
                        n, ring = UPG * i + (u - L_SUM), (u - L_SUM) % 2
                        wait(dve, exped, n + 1)
                        dve.tensor_reduce(total[:, ring, :], probs[:, (u - L_SUM) % 4, :, :], AX, ALU.add).then_inc(summed, 1)
                        wait(dve, summed, n + 1)
                        wait(dve, weighted, n - 1)
                        dve.reciprocal(rtotal[:, ring, :], total[:, ring, :]).then_inc(inverted, 1)
                    j, par, before, r = part(i, u, 0)
                    if cos and active(0) and r == 1:
                        for t in range(2):
                            wait(dve, squared, 2 * j + t + 1)
                            dve.tensor_reduce(norm2[:, t, :], square[:, t, :].rearrange("p (h d) -> p h d", d=HD), AX,
                                              ALU.add).then_inc(norm_summed, 1)
                        wait(dve, norm_summed, 2 * j + 2)
                        wait(dve, refined, RS * j)
                        dve.tensor_scalar(floor2[:, :, :], norm2[:, :, :], NORM_MIN2, None, ALU.max).then_inc(floored, 1)
                        wait(dve, floored, j + 1)
                        dve.tensor_scalar(minus_half[:, :, :], floor2[:, :, :], -0.5, None, ALU.mult)
                        dve.tensor_scalar(rnorm[:, :, :].bitcast(I32), floor2[:, :, :].bitcast(I32), -0.5, float(RSQRT_BITS),
                                          ALU.mult, ALU.add).then_inc(guessed, 1)
                    j, par, before, r = part(i, u, 4)
                    if cos and active(4) and r == 0:
                        n = NS * j
                        wait(dve, refined, RS * (j + 1))
                        dve.scalar_tensor_tensor(half_sq[:, :, :], rnorm[:, :, :], -0.5, rnorm[:, :, :],
                                                 ALU.mult, ALU.mult).then_inc(newton, 1)
                        dve.tensor_tensor(scaled[:, :, :], rnorm[:, :, :],
                                          gain[:, :].unsqueeze(1).to_broadcast([P, 2, 2 * HEADS]), ALU.mult).then_inc(newton, 1)
                        wait(dve, newton, n + 2)
                        dve.tensor_tensor(product[:, :, :], half_sq[:, :, :], floor2[:, :, :], ALU.mult).then_inc(newton, 1)
                        wait(dve, newton, n + 3)
                        dve.scalar_tensor_tensor(qk_scale[:, :, :], product[:, :, :], 1.5, scaled[:, :, :],
                                                 ALU.add, ALU.mult).then_inc(newton, 1)
                        wait(dve, newton, n + NS)
                        for t in range(2):
                            wait(dve, qk_copied, 2 * j + t + 1)
                            wait(dve, qkt, 2 * (j - 1) + t + 1 if not (isinstance(j, int) and j == 0) else 0)
                            dve.tensor_tensor(qkn[:, t, :].rearrange("p (h d) -> p h d", d=HD),
                                              qk[:, t, :].rearrange("p (h d) -> p h d", d=HD),
                                              qk_scale[:, t, :].unsqueeze(2).to_broadcast([P, 2 * HEADS, HD]),
                                              ALU.mult).then_inc(qkn_ready, 1)
                    j, par, before, r = part(i, u, 0)
                    if not cos and active(0) and r == 0:
                        wait(dve, k_mm, j + 1)
                        wait(dve, kmask_loaded[par], 16 * HH * before)
                        dve.tensor_copy(qkT[0:HALF, par, 2:4, :],
                                        ps_x[0][0:HALF, :].rearrange("p (c t) -> p c t", c=2)).then_inc(k_ready, 1)
                    j, par, before, r = part(i, u, -2)
                    if not cos and r == 0 and not (isinstance(j, int) and j >= PARTS):
                        if isinstance(j, int) and j == 1:
                            for c in range(2):
                                last = split(dve, qkv_w[0:HALF + c, c, 0:2 * DIM], w["masked"][0:HALF + c, c, 0:2 * DIM],
                                             qk_high[0:HALF + c, c, :], qk_low[0:HALF + c, c, :], w_step, 2 * c)
                            last.then_inc(w_split, 1)
                        wait(dve, x_loaded[par], 16 * (before + 1))
                        wait(dve, q_mm, j - 1)
                        wait(dve, x_split, j - 1)
                        for c in range(2):
                            last = split(dve, xT[0:HALF + c, par, c, :], x_masked[0:HALF + c, c, :], xs[0:HALF + c, par, 0, c, :],
                                         xs[0:HALF + c, par, 1, c, :], x_step, 4 * (j - 1) + 2 * c)
                        last.then_inc(x_split, 1)

                run(dve, step, peeled=1)



def mlp_phase(nc, w, x2_dram, h_dram, big):
    jobs = (("r_in", "r_ln", RHD, 0), ("ffn_qkv", "ln1", 3 * DIM, RHD), ("fc1", "ln2", MLP, RHD + 3 * DIM))
    pieces = [(name, norm, a, min(a + 512, n), at) for name, norm, n, at in jobs for a in range(0, n, 512)]
    with ExitStack() as ctx:
        mem = Memory(nc, ctx, "mlp")
        x2 = w["group_x"]
        x2b = mem.sb("x2b", [P, TILES, DIM])
        xm = mem.sb("xm", [HALF, GROUP])
        xT = mem.sb("xT", [HALF + 1, 2, 2, GROUP], F32R)
        hT = mem.sb("hT", [P, KM, GROUP])
        h = mem.sb("h", [P, TILES, DIM])
        stats = mem.sb("stats", [P, TILES, 6])
        mv = mem.sb("mv", [P, TILES, 2])
        vare = mem.sb("vare", [P, TILES])
        power = mem.sb("power", [P, TILES])
        rstd = mem.sb("rstd", [P, TILES])
        un = mem.sb("un", [P, TILES, DIM])
        ps_t = [mem.ps(f"ps_t{i}") for i in range(2)]
        ps_u = [mem.ps(f"ps_u{i}") for i in range(2)]
        ps_h = [mem.ps(f"ps_h{i}") for i in range(2)]
        ps_f = [mem.ps(f"ps_f{i}") for i in range(2)]
        bias_row = mem.sb("bias_row", [1, RHD + 3 * DIM + MLP])
        fold_banks = [*ps_t, *ps_h, ps_f[0]]
        shifted = mem.sem("shifted")
        rowed = mem.sem("rowed")
        scaled = mem.sem("scaled")
        placed = mem.sem("placed")
        const_set = mem.sem("const_set")
        x2_loaded = w["tok_group_loaded"]
        biased = mem.sem("biased")
        turned = mem.sem("turned")
        xt_step = mem.sem("xt_step")
        xt_ready = mem.sem("xt_ready")
        hidden = mem.sem("hidden")
        gelued = mem.sem("gelued")
        summed = mem.sem("summed")
        added = mem.sem("added")
        counted, measured = mem.sem("counted"), mem.sem("measured")
        varied, rooted = mem.sem("varied"), mem.sem("rooted")
        normed = mem.sem("normed")
        u_turned = mem.sem("u_turned")
        u_ready = mem.sem("u_ready")
        h_stored = mem.sem("h_stored")

        with nc.Block() as block:

            @block.sync
            def _(sp):
                def turn(i, active):
                    if active(0) and not (isinstance(i, int) and i == 0):
                        waits(sp, (biased, i), (turned, 2 * i))
                        sp.dma_start(x2[:, :, :], x2_dram[i]).then_inc(x2_loaded, 16)
                    if active(1):
                        wait(sp, added, TILES * i)
                        sp.dma_start(h_dram[i - 1], h[:, :, :]).then_inc(h_stored, 16)

                sweep(sp, GROUPS, 2, turn)
                sp.wait_ge(rowed, len(pieces))
                for name, norm, n, at in jobs:
                    sp.dma_start(w[name][HALF:HALF + 1, 1, :], bias_row[0:1, at:at + n]).then_inc(placed, 16)
                sp.wait_ge(placed, 16 * len(jobs))
                sp.wait_ge(h_stored, 16 * GROUPS)

            @block.tensor
            def _(pe):
                def fold_shifts():
                    pe.wait_ge(w["done"]["ffn"], w["counts"]["ffn"])
                    pe.wait_ge(gelued, KM * GROUPS)
                    pe.wait_ge(added, TILES * GROUPS - 1)
                    for (name, norm, a, b, at), bank in zip(pieces, fold_banks):
                        raw = w[name + "_raw"]
                        layer(pe, bank[0:1, 0:b - a], [w[norm + "_b"][:, c:c + 1] for c in range(2)],
                              [raw[:, c, a:b] for c in range(2)]).then_inc(shifted, 1)

                def turn(i, active):
                    if isinstance(i, int) and i == GROUPS + 1:
                        fold_shifts()
                    if active(1):
                        if isinstance(i, int) and i == 1:
                            keep_warm(pe, w["ident"], ps_h[0], 12)
                            wait(pe, const_set, 2)
                        wait(pe, xt_ready, 2 * i)
                        for k in range(KM):
                            wait(pe, gelued, KM * (i - 1) + k - 1)
                            split_layer(pe, ps_h[k % 2][:, :], split_chunk(w["ff1_high"], w["ff1_low"], k),
                                        split_halves(xT)).then_inc(hidden, 1)
                    if active(2):
                        wait(pe, normed, i - 1)
                        for c in range(2):
                            wait(pe, u_ready, 2 * (i - 3) + c + 1 if not (isinstance(i, int) and i < 3) else 0)
                            for t in range(TILES):
                                last = pe.transpose(ps_u[c][0:HALF, span(t, P)], un[:, t, span(c, HALF)], w["ident"][:, :])
                            last.then_inc(u_turned, 1)
                    if active(0):
                        wait(pe, x2_loaded, 16 * (i + 1))
                        for c in range(2):
                            wait(pe, xt_ready, 2 * (i - 1) + c + 1 if not (isinstance(i, int) and i < 1) else 0)
                            for t in range(TILES):
                                last = pe.transpose(ps_t[c][0:HALF, span(t, P)], x2[:, t, span(c, HALF)], w["ident"][:, :])
                            last.then_inc(turned, 1)
                    if active(1):
                        wait(pe, gelued, KM * i)
                        for t in range(TILES):
                            wait(pe, added, TILES * (i - 1) + t - 1)
                            layer(pe, ps_f[t % 2][:, 0:DIM], [hT[:, k, span(t, P)] for k in range(KM)],
                                  [w["ff2"][:, k, :] for k in range(KM)]).then_inc(summed, 1)

                sweep(pe, GROUPS, 2, turn)

            @block.scalar
            def _(act):
                def turn(i, active):
                    if active(1):
                        for k in range(KM):
                            wait(act, hidden, KM * (i - 1) + k + 1)
                            wait(act, summed, TILES * (i - 1))
                            act.activation(hT[:, k, :], ps_h[k % 2][:, :], ACT.Gelu_apprx_tanh).then_inc(gelued, 1)
                    if active(2):
                        for c in range(2):
                            wait(act, u_turned, 2 * (i - 2) + c + 1)
                            columns = big[0:HALF, c, :].rearrange("p (n b) -> p b n", b=IMAGES)
                            act.activation(columns[:, bass.ds(8 * (i - 2), 8), :],
                                           ps_u[c][0:HALF, :].rearrange("p (b n) -> p b n", n=SEQ), ACT.Copy).then_inc(u_ready, 1)

                sweep(act, GROUPS, 2, turn)

            @block.gpsimd
            def _(pool):
                pool.memset(power[:, :], -0.5).then_inc(const_set, 1)
                pool.wait_ge(const_set, 2)

                def turn(i, active):
                    if active(1):
                        wait(pool, x2_loaded, 16 * i)
                        wait(pool, added, TILES * (i - 1))
                        pool.tensor_tensor(x2b[:, :, :], x2[:, :, :],
                                           w["ff2_b"][:, :].unsqueeze(1).to_broadcast([P, TILES, DIM]), ALU.add).then_inc(biased, 1)
                        wait(pool, varied, i)
                        pool.tensor_tensor(rstd[:, :], vare[:, :], power[:, :], ALU.pow).then_inc(rooted, 1)

                sweep(pool, GROUPS, 2, turn)

            @block.vector
            def _(dve):
                def fold_gains():
                    dve.wait_ge(w["done"]["ffn"], w["counts"]["ffn"])
                    dve.wait_ge(w["done"]["cos"], w["counts"]["cos"])
                    for name, norm, n, at in jobs:
                        for c in range(2):
                            dve.tensor_scalar(w[name][0:HALF, c, :], w[name + "_raw"][:, c, :], w[norm + "_g"][:, c:c + 1], None,
                                              ALU.mult).then_inc(scaled, 1)
                    for c in range(2):
                        dve.tensor_scalar(w["cos_proj"][0:HALF, c, :], w["cos_proj"][0:HALF, c, :], w["head_scale"][:, c:c + 1],
                                          None, ALU.mult).then_inc(scaled, 1)

                dve.memset(xT[HALF:HALF + 1, 0, 1, :].bitcast(F32), 1.0)
                dve.memset(xT[HALF:HALF + 1, 1, 1, :].bitcast(F32), 0.0).then_inc(const_set, 1)

                def turn(i, active):
                    if active(0):
                        for c in range(2):
                            wait(dve, turned, 2 * i + c + 1)
                            wait(dve, hidden, KM * i)
                            wait(dve, xt_ready, 2 * i + c)
                            split(dve, ps_t[c][0:HALF, :], xm[:, :], xT[0:HALF, 0, c, :], xT[0:HALF, 1, c, :],
                                  xt_step, 4 * i + 2 * c).then_inc(xt_ready, 1)
                    if active(1):
                        wait(dve, biased, i)
                        wait(dve, h_stored, 16 * (i - 1))
                        for t in range(TILES):
                            n = TILES * (i - 1) + t + 1
                            wait(dve, summed, n)
                            dve.tensor_tensor(h[:, t, :], ps_f[t % 2][:, 0:DIM], x2b[:, t, :], ALU.add).then_inc(added, 1)
                            wait(dve, added, n)
                            dve.bn_stats(stats[:, t, :], h[:, t, :]).then_inc(counted, 1)
                            dve.drain()
                            dve.bn_aggr(mv[:, t, :], stats[:, t, :]).then_inc(measured, 1)
                        wait(dve, measured, TILES * i)
                        dve.tensor_scalar(vare[:, :], mv[:, :, 1], EPS, None, ALU.add).then_inc(varied, 1)
                        wait(dve, rooted, i)
                        wait(dve, u_turned, 2 * (i - 1))
                        for t in range(TILES):
                            last = dve.tensor_scalar(un[:, t, :], h[:, t, :], mv[:, t, 0:1], rstd[:, t:t + 1],
                                                     ALU.subtract, ALU.mult)
                        last.then_inc(normed, 1)

                    if isinstance(i, int) and i == 2:
                        fold_gains()

                sweep(dve, GROUPS, 2, turn)
                for n, (name, norm, a, b, at) in enumerate(pieces):
                    dve.wait_ge(shifted, n + 1)
                    dve.tensor_tensor(bias_row[0:1, at + a:at + b], fold_banks[n][0:1, 0:b - a], w["fold_bias"][0:1, at + a:at + b],
                                      ALU.add).then_inc(rowed, 1)
                dve.wait_ge(scaled, 2 * len(jobs) + 2)



def router_phase(nc, w, big, h_dram, h4_dram, z_dram, bits_dram, zn_dram):
    with ExitStack() as ctx:
        mem = Memory(nc, ctx, "router")
        oT = mem.sb("oT", [HALF + 1, 2, GROUP])
        h = mem.sb("h", [P, TILES, DIM])
        h4 = mem.sb("h4", [P, TILES, DIM])
        stats = mem.sb("stats", [P, TILES, 6])
        mv = mem.sb("mv", [P, TILES, 2])
        vare = mem.sb("vare", [P, TILES])
        power = mem.sb("power", [P, TILES])
        rstd = mem.sb("rstd", [P, TILES])
        varz = mem.sb("varz", [P, TILES])
        varz2 = mem.sb("varz2", [P, TILES])
        varz3 = mem.sb("varz3", [P, TILES])
        rz = mem.sb("rz", [P, TILES])
        z = mem.sb("z", [P, TILES, DIM])
        zn = mem.sb("zn", [P, TILES, DIM])
        znT = mem.sb("znT", [HALF + 1, 2, GROUP])
        eT = mem.sb("eT", [P, GROUP])
        esum = mem.sb("esum", [P, 8])
        emean = mem.sb("emean", [P, 8])
        h1 = mem.sb("h1", [P, GROUP])
        h2 = mem.sb("h2", [RH2 + 1, GROUP])
        logits = mem.sb("logits", [P, TILES, 2 * BITS])
        beat = mem.sb("beat", [P, TILES, BITS])
        both = mem.sb("both", [P, TILES])
        route = mem.sb("route", [P, TILES, 8])
        ps_a = [mem.ps(f"ps_a{i}") for i in range(2)]
        ps_t = [mem.ps(f"ps_t{i}") for i in range(2)]
        ps_e, ps_1, ps_2, ps_l = (mem.ps(f"ps_{x}") for x in "e12l")
        weight_step, weight_split = mem.sem("weight_step"), mem.sem("weight_split")
        const_set = mem.sem("const_set")
        h_loaded = mem.sem("h_loaded")
        o_ready = mem.sem("o_ready")
        projected = mem.sem("projected")
        added = mem.sem("added")
        counted, measured = mem.sem("counted"), mem.sem("measured")
        varied = mem.sem("varied")
        rooted = mem.sem("rooted")
        var_step = mem.sem("var_step")
        z_rooted = mem.sem("z_rooted")
        z_ready = mem.sem("z_ready")
        zn_ready = mem.sem("zn_ready")
        turned = mem.sem("turned")
        znt_ready = mem.sem("znt_ready")
        e_mm, e_ready = mem.sem("e_mm"), mem.sem("e_ready")
        e_summed, mean_ready = mem.sem("e_summed"), mem.sem("mean_ready")
        h1_mm, h1_ready = mem.sem("h1_mm"), mem.sem("h1_ready")
        h2_mm, h2_ready = mem.sem("h2_mm"), mem.sem("h2_ready")
        l_mm = mem.sem("l_mm")
        route_step = mem.sem("route_step")
        h4_stored, z_stored, zn_stored, bits_stored = (mem.sem(x) for x in ("h4_stored", "z_stored", "zn_stored", "bits_stored"))
        RS = 7

        with nc.Block() as block:

            @block.sync
            def _(sp):
                def turn(i, active):
                    if active(0):
                        wait(sp, added, TILES * i)
                        sp.dma_start(h[:, :, :], h_dram[i]).then_inc(h_loaded, 16)
                    if active(1):
                        wait(sp, added, TILES * i)
                        sp.dma_start(h4_dram[i - 1], h4[:, :, :]).then_inc(h4_stored, 16)
                        wait(sp, z_ready, TILES * i)
                        sp.dma_start(z_dram[i - 1], z[:, :, :]).then_inc(z_stored, 16)
                    if active(2):
                        wait(sp, znt_ready, 2 * (i - 1))
                        for a in range(2):
                            sp.dma_start(zn_dram[2 * (i - 2) + a], znT[0:HALF, :, span(a, PART)]).then_inc(zn_stored, 16)
                    if active(4):
                        wait(sp, route_step, RS * (i - 3))
                        sp.dma_start(bits_dram[i - 4], route[:, :, :]).then_inc(bits_stored, 16)

                sweep(sp, GROUPS, 4, turn)
                sp.wait_ge(zn_stored, 32)
                for j in range(2):
                    sp.dma_start(w["part_xT"][0:HALF, j, :, :], zn_dram[j]).then_inc(w["ffn_x_loaded"][j], 16)
                sp.wait_ge(h4_stored, 16 * GROUPS)
                sp.wait_ge(z_stored, 16 * GROUPS)
                sp.wait_ge(zn_stored, 32 * GROUPS)
                sp.wait_ge(bits_stored, 16 * GROUPS)

            @block.tensor
            def _(pe):
                keep_warm(pe, w["ident"], ps_e, 6)
                pe.wait_ge(const_set, 5)

                def turn(i, active):
                    if active(4):
                        wait(pe, mean_ready, i - 3)
                        wait(pe, h1_ready, i - 4)
                        layer(pe, ps_1[:, :].rearrange("p (b n) -> p b n", n=SEQ), [w["r_o1"][:, 0, :], w["r_o1"][:, 1, :]],
                              [eT[:, :].rearrange("p (b n) -> p b n", n=SEQ),
                               emean[:, :].unsqueeze(2).to_broadcast([P, 8, SEQ])]).then_inc(h1_mm, 1)
                    if active(1):
                        wait(pe, o_ready, 2 * i)
                        for t in range(TILES):
                            wait(pe, added, TILES * (i - 1) + t - 1)
                            layer(pe, ps_a[t % 2][:, 0:DIM], halves(oT, span(t, P)),
                                  [w["cos_proj"][0:HALF, 0, :], w["cos_proj"][0:HALF + 1, 1, :]]).then_inc(projected, 1)
                    if active(3):
                        wait(pe, znt_ready, 2 * (i - 2))
                        wait(pe, e_ready, i - 3)
                        layer(pe, ps_e[:, :], [w["r_in"][0:HALF, 0, :], w["r_in"][0:HALF + 1, 1, :]],
                              halves(znT, slice(0, GROUP))).then_inc(e_mm, 1)
                    if active(4):
                        wait(pe, h1_ready, i - 3)
                        wait(pe, h2_ready, i - 4)
                        pe.matmul(ps_2[0:RH2, :], w["r_o2"][:, :], h1[:, :], start=True, stop=True).then_inc(h2_mm, 1)
                    if active(2):
                        wait(pe, zn_ready, i - 1)
                        for c in range(2):
                            wait(pe, znt_ready, 2 * (i - 3) + c + 1 if not (isinstance(i, int) and i < 3) else 0)
                            for t in range(TILES):
                                last = pe.transpose(ps_t[c][0:HALF, span(t, P)], zn[:, t, span(c, HALF)], w["ident"][:, :])
                            last.then_inc(turned, 1)
                    if active(4):
                        wait(pe, h2_ready, i - 3)
                        wait(pe, route_step, RS * (i - 4))
                        for t in range(TILES):
                            last = pe.matmul(ps_l[:, span(t, 2 * BITS)], h2[:, span(t, P)], w["r_o3"][:, :], start=True, stop=True)
                        last.then_inc(l_mm, 1)

                sweep(pe, GROUPS, 4, turn)

            @block.scalar
            def _(act):
                def turn(i, active):
                    if active(4):
                        wait(act, h1_mm, i - 3)
                        wait(act, h2_mm, i - 4)
                        act.activation(h1[:, :], ps_1[:, :], ACT.Gelu, bias=w["r_o1_b"][:, 0:1]).then_inc(h1_ready, 1)
                    if active(0):
                        wait(act, projected, TILES * i)
                        for c in range(2):
                            columns = big[0:HALF, c, :].rearrange("p (n b) -> p b n", b=IMAGES)
                            act.activation(oT[0:HALF, c, :].rearrange("p (b n) -> p b n", n=SEQ), columns[:, bass.ds(8 * i, 8), :],
                                           ACT.Copy).then_inc(o_ready, 1)
                    if active(3):
                        wait(act, e_mm, i - 2)
                        wait(act, h1_mm, i - 3)
                        act.activation(eT[:, :], ps_e[:, :], ACT.Gelu).then_inc(e_ready, 1)
                    if active(4):
                        wait(act, h2_mm, i - 3)
                        wait(act, l_mm, i - 4)
                        act.activation(h2[0:RH2, :], ps_2[0:RH2, :], ACT.Gelu, bias=w["r_o2_b"][:, 0:1]).then_inc(h2_ready, 1)
                    if active(2):
                        for c in range(2):
                            wait(act, turned, 2 * (i - 2) + c + 1)
                            wait(act, e_mm, i - 2)
                            wait(act, zn_stored, 32 * (i - 2))
                            act.activation(znT[0:HALF, c, :], ps_t[c][0:HALF, :], ACT.Copy).then_inc(znt_ready, 1)
                    if active(1):
                        wait(act, z_rooted, i)
                        wait(act, z_ready, TILES * i)
                        wait(act, turned, 2 * (i - 1))
                        for t in range(TILES):
                            last = act.activation(zn[:, t, :], z[:, t, :], ACT.Identity, scale=rz[:, t:t + 1])
                        last.then_inc(zn_ready, 1)

                sweep(act, GROUPS, 4, turn)

            @block.gpsimd
            def _(pool):
                pool.memset(power[:, :], -0.5).then_inc(const_set, 1)
                pool.wait_ge(const_set, 5)

                def turn(i, active):
                    if active(1):
                        wait(pool, varied, i)
                        pool.tensor_tensor(rstd[:, :], vare[:, :], power[:, :], ALU.pow).then_inc(rooted, 1)
                        wait(pool, var_step, 3 * i)
                        wait(pool, zn_ready, i - 1)
                        pool.tensor_tensor(rz[:, :], varz3[:, :], power[:, :], ALU.pow).then_inc(z_rooted, 1)

                sweep(pool, GROUPS, 4, turn)

            @block.vector
            def _(dve):
                dve.memset(oT[HALF:HALF + 1, 1, :], 1.0).then_inc(const_set, 1)
                dve.memset(znT[HALF:HALF + 1, 1, :], 1.0).then_inc(const_set, 1)
                dve.memset(h2[RH2:RH2 + 1, :], 1.0).then_inc(const_set, 1)
                dve.memset(route[:, :, :], 0.0).then_inc(const_set, 1)
                dve.wait_ge(const_set, 5)

                def turn(i, active):
                    if isinstance(i, int) and i == GROUPS + 1:
                        split_weights(dve, w, "fc1", weight_step).then_inc(weight_split, 1)
                    if active(1):
                        wait(dve, h_loaded, 16 * i)
                        wait(dve, h4_stored, 16 * (i - 1))
                        wait(dve, z_ready, TILES * (i - 1))
                        for t in range(TILES + 1):
                            n = TILES * (i - 1) + t
                            if t < TILES:
                                wait(dve, projected, n + 1)
                                dve.tensor_tensor(h4[:, t, :], ps_a[t % 2][:, 0:DIM], h[:, t, :], ALU.add).then_inc(added, 1)
                            if t > 0:
                                wait(dve, added, n)
                                dve.bn_stats(stats[:, t - 1, :], h4[:, t - 1, :]).then_inc(counted, 1)
                        dve.drain()
                        for t in range(TILES):
                            dve.bn_aggr(mv[:, t, :], stats[:, t, :]).then_inc(measured, 1)
                        wait(dve, measured, TILES * i)
                        dve.tensor_scalar(vare[:, :], mv[:, :, 1], EPS, None, ALU.add).then_inc(varied, 1)
                    if active(3):
                        wait(dve, e_ready, i - 2)
                        dve.tensor_reduce(esum[:, :], eT[:, :].rearrange("p (b n) -> p b n", n=SEQ)[:, :, 1:SEQ], AX, ALU.add).then_inc(e_summed, 1)
                        wait(dve, e_summed, i - 2)
                        wait(dve, h1_mm, i - 3)
                        dve.tensor_scalar(emean[:, :], esum[:, :], 1.0 / (SEQ - 1), None, ALU.mult).then_inc(mean_ready, 1)
                    if active(1):
                        wait(dve, rooted, i)
                        dve.tensor_tensor(varz[:, :], mv[:, :, 1], rstd[:, :], ALU.mult).then_inc(var_step, 1)
                        wait(dve, var_step, 3 * (i - 1) + 1)
                        dve.tensor_tensor(varz2[:, :], varz[:, :], rstd[:, :], ALU.mult).then_inc(var_step, 1)
                        wait(dve, var_step, 3 * (i - 1) + 2)
                        dve.tensor_scalar(varz3[:, :], varz2[:, :], EPS, None, ALU.add).then_inc(var_step, 1)
                        wait(dve, z_stored, 16 * (i - 1))
                        wait(dve, zn_ready, i - 1)
                        for t in range(TILES):
                            dve.tensor_scalar(z[:, t, :], h4[:, t, :], mv[:, t, 0:1], rstd[:, t:t + 1],
                                              ALU.subtract, ALU.mult).then_inc(z_ready, 1)
                    if active(4):
                        n = RS * (i - 4)
                        wait(dve, l_mm, i - 3)
                        wait(dve, bits_stored, 16 * (i - 4))
                        dve.tensor_copy(logits[:, :, :], ps_l[:, 0:TILES * 2 * BITS].rearrange("p (t l) -> p t l", t=TILES)).then_inc(route_step, 1)
                        wait(dve, route_step, n + 1)
                        pairs = logits[:, :, :].rearrange("p t (b l) -> p t b l", l=2)
                        dve.tensor_tensor(beat[:, :, :], pairs[:, :, :, 1], pairs[:, :, :, 0], ALU.is_gt).then_inc(route_step, 1)
                        wait(dve, route_step, n + 2)
                        dve.tensor_scalar(route[:, :, 0:BITS], beat[:, :, :], w["first_token"][:, 0:1], None, ALU.max).then_inc(route_step, 1)
                        wait(dve, route_step, n + 3)
                        dve.tensor_tensor(both[:, :], route[:, :, 0], route[:, :, 1], ALU.mult).then_inc(route_step, 1)
                        wait(dve, route_step, n + 4)
                        dve.tensor_tensor(route[:, :, 3], route[:, :, 1], both[:, :], ALU.subtract).then_inc(route_step, 1)
                        dve.tensor_tensor(route[:, :, 4], route[:, :, 0], both[:, :], ALU.subtract).then_inc(route_step, 1)
                        dve.scalar_tensor_tensor(beat[:, :, 0], route[:, :, 0], -1.0, route[:, :, 1], ALU.mult, ALU.subtract).then_inc(select_step, 1)
                        wait(dve, select_step, 2 * (i - 4) + 1)
                        dve.scalar_tensor_tensor(beat[:, :, 1], beat[:, :, 0], 1.0, both[:, :], ALU.add, ALU.add).then_inc(select_step, 1)
                        wait(dve, select_step, 2 * (i - 4) + 2)
                        dve.tensor_copy(route[:, :, 2], beat[:, :, 1]).then_inc(route_step, 1)

                select_step = mem.sem("select_step")
                sweep(dve, GROUPS, 4, turn)
                dve.wait_ge(weight_split, 1)



def last_phase(nc, w, h5_dram, bits_dram, h4_dram, out_dram):
    with ExitStack() as ctx:
        mem = Memory(nc, ctx, "last")
        h5 = w["group_x"]
        h5r = mem.sb("h5r", [P, TILES, DIM])
        bits = mem.sb("bits", [P, TILES, 8])
        h4 = mem.sb("h4", [P, TILES, DIM])
        select = mem.sb("select", [P, TILES, 8])
        stats = mem.sb("stats", [P, TILES, 6])
        mv = mem.sb("mv", [P, TILES, 2])
        vare = mem.sb("vare", [P, TILES])
        power = mem.sb("power", [P, TILES])
        rstd = mem.sb("rstd", [P, TILES])
        xn = mem.sb("xn", [P, TILES, DIM])
        xm = mem.sb("xm", [HALF, GROUP])
        xT = mem.sb("xT", [HALF + 1, 2, 2, GROUP], F32R)
        hT = mem.sb("hT", [P, KM, GROUP])
        ffb = mem.sb("ffb", [P, 2, DIM])
        out = mem.sb("out", [P, TILES, DIM])
        outT = mem.sb("outT", [HALF, 2, GROUP])
        down = mem.sb("down", [P, TILES, RANK3])
        downT = mem.sb("downT", [HALF, 2, GROUP])
        base = mem.sb("base", [P, TILES, DIM])
        fin = mem.sb("fin", [P, TILES, DIM])
        ps_t = [mem.ps(f"ps_t{i}") for i in range(2)]
        ps_h = [mem.ps(f"ps_h{i}") for i in range(2)]
        ps_f = [mem.ps(f"ps_f{i}") for i in range(2)]
        ps_d = [mem.ps(f"ps_d{i}") for i in range(2)]
        const_set = mem.sem("const_set")
        h5_loaded = w["ffn_group_loaded"]
        r_loaded, s_loaded = mem.sem("r_loaded"), mem.sem("s_loaded")
        counted, measured = mem.sem("counted"), mem.sem("measured")
        varied, rooted = mem.sem("varied"), mem.sem("rooted")
        normed = mem.sem("normed")
        turned = mem.sem("turned")
        xt_step = mem.sem("xt_step")
        xt_ready = mem.sem("xt_ready")
        hidden, gelued = mem.sem("hidden"), mem.sem("gelued")
        summed = mem.sem("summed")
        biased = mem.sem("biased")
        out_ready = mem.sem("out_ready")
        o_turned, ot_ready = mem.sem("o_turned"), mem.sem("ot_ready")
        downed, down_ready = mem.sem("downed"), mem.sem("down_ready")
        d_turned, dt_ready = mem.sem("d_turned"), mem.sem("dt_ready")
        upped = mem.sem("upped")
        based = mem.sem("based")
        fin_ready = mem.sem("fin_ready")
        stored = mem.sem("stored")

        with nc.Block() as block:

            @block.sync
            def _(sp):
                def turn(i, active):
                    if active(0) and not (isinstance(i, int) and i == 0):
                        wait(sp, normed, i)
                        sp.dma_start(h5[:, :, :], h5_dram[i]).then_inc(h5_loaded, 16)
                    if active(1):
                        wait(sp, out_ready, TILES * (i - 1))
                        sp.dma_start(h5r[:, :, :], h5_dram[i - 1]).then_inc(r_loaded, 16)
                        sp.dma_start(bits[:, :, :], bits_dram[i - 1]).then_inc(r_loaded, 16)
                    if active(2):
                        waits(sp, (based, i - 2), (down_ready, TILES * (i - 2)))
                        sp.dma_start(h4[:, :, :], h4_dram[i - 2]).then_inc(s_loaded, 16)
                        sp.dma_start(select[:, :, :], bits_dram[i - 2]).then_inc(s_loaded, 16)
                    if active(3):
                        wait(sp, fin_ready, TILES * (i - 2))
                        sp.dma_start(out_dram[i - 3], fin[:, :, :]).then_inc(stored, 16)

                sweep(sp, GROUPS, 3, turn)
                sp.wait_ge(stored, 16 * GROUPS)

            @block.tensor
            def _(pe):
                keep_warm(pe, w["ident"], ps_h[0], 14)

                def transposes(source, banks, into):
                    for c in range(2):
                        for t in range(TILES):
                            last = pe.transpose(banks[c][0:HALF, span(t, P)], source[:, t, span(c, HALF)], w["ident"][:, :])
                        last.then_inc(into, 1)

                def second(i, t):
                    wait(pe, biased, TILES * (i - 2) + t - 1)
                    layer(pe, ps_f[t % 2][:, 0:DIM], [hT[:, k, span(t, P)] for k in range(KM)],
                          [w["fc2"][:, k, :] for k in range(KM)]).then_inc(summed, 1)

                def turn(i, active):
                    if active(2):
                        if isinstance(i, int) and i == 2:
                            keep_warm(pe, w["ident"], ps_h[0], 12)
                            wait(pe, const_set, 2)
                        wait(pe, xt_ready, 2 * (i - 1))
                        for k in range(KM):
                            wait(pe, gelued, KM * (i - 2) + k - 1)
                            split_layer(pe, ps_h[k % 2][:, :], split_chunk(w["fc1_high"], w["fc1_low"], k),
                                        split_halves(xT)).then_inc(hidden, 1)
                    if active(3):
                        wait(pe, out_ready, TILES * (i - 2))
                        wait(pe, dt_ready, 2 * (i - 3))
                        wait(pe, xt_ready, 2 * (i - 1) if not isinstance(i, int) else 2 * min(i - 1, GROUPS))
                        transposes(out, ps_t, o_turned)
                    if active(2):
                        wait(pe, gelued, KM * (i - 1))
                        second(i, 0)
                    if active(1):
                        wait(pe, normed, i)
                        wait(pe, ot_ready, 2 * (i - 2))
                        transposes(xn, ps_t, turned)
                    if active(3):
                        wait(pe, ot_ready, 2 * (i - 2))
                        for t in range(TILES):
                            n = TILES * (i - 3) + t
                            if t < 2:
                                wait(pe, fin_ready, n - t)
                            else:
                                wait(pe, down_ready, n - 1)
                            layer(pe, ps_d[t % 2][:, 0:RANK3], [outT[:, c, span(t, P)] for c in range(2)],
                                  [w["lra_down"][:, c, :] for c in range(2)]).then_inc(downed, 1)
                    if active(2):
                        second(i, 1)
                        second(i, 2)
                    if active(3):
                        wait(pe, down_ready, TILES * (i - 2))
                        transposes(down, ps_d, d_turned)
                    if active(2):
                        second(i, 3)
                    if active(3):
                        wait(pe, dt_ready, 2 * (i - 2))
                        for t in range(TILES):
                            if t >= 2:
                                wait(pe, fin_ready, TILES * (i - 3) + t - 1)
                            layer(pe, ps_d[t % 2][:, 0:DIM], [downT[:, c, span(t, P)] for c in range(2)],
                                  [w["lra_up"][:, c, :] for c in range(2)]).then_inc(upped, 1)

                sweep(pe, GROUPS, 3, turn)

            @block.scalar
            def _(act):
                def turn(i, active):
                    if active(2):
                        for k in range(KM):
                            wait(act, hidden, KM * (i - 2) + k + 1)
                            wait(act, summed, TILES * (i - 2))
                            act.activation(hT[:, k, :], ps_h[k % 2][:, :], ACT.Gelu).then_inc(gelued, 1)
                    if active(3):
                        for c in range(2):
                            wait(act, o_turned, 2 * (i - 3) + c + 1)
                            wait(act, downed, TILES * (i - 3))
                            act.activation(outT[:, c, :], ps_t[c][0:HALF, :], ACT.Copy).then_inc(ot_ready, 1)
                        for c in range(2):
                            wait(act, d_turned, 2 * (i - 3) + c + 1)
                            wait(act, upped, TILES * (i - 3))
                            act.activation(downT[:, c, :], ps_d[c][0:HALF, :], ACT.Copy).then_inc(dt_ready, 1)

                sweep(act, GROUPS, 3, turn)

            @block.gpsimd
            def _(pool):
                pool.memset(power[:, :], -0.5).then_inc(const_set, 1)
                pool.wait_ge(const_set, 2)

                def turn(i, active):
                    if active(1):
                        wait(pool, varied, i)
                        pool.tensor_tensor(rstd[:, :], vare[:, :], power[:, :], ALU.pow).then_inc(rooted, 1)
                    if active(3):
                        wait(pool, s_loaded, 32 * (i - 2))
                        wait(pool, out_ready, TILES * (i - 2))
                        wait(pool, fin_ready, TILES * (i - 3))
                        pool.tensor_tensor(base[:, :, :], h4[:, :, :], out[:, :, :], ALU.add).then_inc(based, 1)

                sweep(pool, GROUPS, 3, turn)

            @block.vector
            def _(dve):
                dve.memset(xT[HALF:HALF + 1, 0, 1, :].bitcast(F32), 1.0)
                dve.memset(xT[HALF:HALF + 1, 1, 1, :].bitcast(F32), 0.0).then_inc(const_set, 1)

                def add_bits(i, t):
                    n = TILES * (i - 2) + t + 1
                    wait(dve, summed, n)
                    dve.tensor_tensor(ffb[:, t % 2, :], ps_f[t % 2][:, 0:DIM], w["fc2_b"][:, :], ALU.add).then_inc(biased, 1)
                    wait(dve, biased, n)
                    if t == 0:
                        wait(dve, r_loaded, 32 * (i - 1))
                        wait(dve, o_turned, 2 * (i - 2))
                        wait(dve, based, i - 2)
                    dve.scalar_tensor_tensor(out[:, t, :], ffb[:, t % 2, :], bits[:, t, 1:2], h5r[:, t, :],
                                             ALU.mult, ALU.add).then_inc(out_ready, 1)

                def turn(i, active):
                    if active(1):
                        wait(dve, h5_loaded, 16 * i)
                        for t in range(TILES):
                            n = TILES * (i - 1) + t + 1
                            dve.bn_stats(stats[:, t, :], h5[:, t, :]).then_inc(counted, 1)
                            dve.drain()
                            dve.bn_aggr(mv[:, t, :], stats[:, t, :]).then_inc(measured, 1)
                        wait(dve, measured, TILES * i)
                        dve.tensor_scalar(vare[:, :], mv[:, :, 1], EPS, None, ALU.add).then_inc(varied, 1)
                        wait(dve, rooted, i)
                        wait(dve, turned, 2 * (i - 1))
                        for t in range(TILES):
                            last = dve.tensor_scalar(xn[:, t, :], h5[:, t, :], mv[:, t, 0:1], rstd[:, t:t + 1],
                                                     ALU.subtract, ALU.mult)
                        last.then_inc(normed, 1)
                    if active(3):
                        wait(dve, s_loaded, 32 * (i - 2))
                        for t in range(TILES):
                            wait(dve, downed, TILES * (i - 3) + t + 1)
                            if t == 0:
                                wait(dve, d_turned, 2 * (i - 3))
                            dve.tensor_tensor(down[:, t, :].rearrange("p (k r) -> p k r", k=3),
                                              ps_d[t % 2][:, 0:RANK3].rearrange("p (k r) -> p k r", k=3),
                                              select[:, t, 2:5].unsqueeze(2).to_broadcast([P, 3, RANK3 // 3]),
                                              ALU.mult).then_inc(down_ready, 1)

                    if active(2):
                        add_bits(i, 0)
                        add_bits(i, 1)
                    if active(1):
                        for c in range(2):
                            wait(dve, turned, 2 * (i - 1) + c + 1)
                            wait(dve, hidden, KM * (i - 1))
                            wait(dve, xt_ready, 2 * (i - 1) + c)
                            split(dve, ps_t[c][0:HALF, :], xm[:, :], xT[0:HALF, 0, c, :], xT[0:HALF, 1, c, :],
                                  xt_step, 4 * (i - 1) + 2 * c).then_inc(xt_ready, 1)
                    if active(2):
                        for t in range(2, TILES):
                            add_bits(i, t)
                    if active(3):
                        wait(dve, based, i - 2)
                        wait(dve, stored, 16 * (i - 3))
                        for t in range(TILES):
                            wait(dve, upped, TILES * (i - 3) + t + 1)
                            dve.tensor_tensor(fin[:, t, :], ps_d[t % 2][:, 0:DIM], base[:, t, :], ALU.add).then_inc(fin_ready, 1)

                sweep(dve, GROUPS, 3, turn)



def vit_tower(nc, ins, out, scratch):
    tiles4 = lambda x: x.rearrange("(g t) p f -> g p t f", t=TILES)
    tiles2 = lambda x: x.rearrange("(g t) p f -> g p t f", t=2)
    s = scratch
    with ExitStack() as ctx:
        mem = Memory(nc, ctx, "weights")
        w = {}
        load_weights(nc, mem, w, ins)
        for name, cols in (("r_in", RHD), ("ffn_qkv", 3 * DIM), ("fc1", MLP), ("masked", MLP)):
            w[name] = mem.sb(name, [HALF + 1, 2, cols])
        for name in ("ff1_high", "ff1_low", "fc1_high", "fc1_low"):
            w[name] = mem.sb(name, [HALF + 1, 2, MLP], F32R)
        w["part_xT"] = mem.sb("part_xT", [HALF + 1, 2, 2, PART])
        w["group_x"] = mem.sb("group_x", [P, TILES, DIM])
        for kind in ("tok", "cos", "ffn"):
            w[f"{kind}_x_loaded"] = mem.sems(f"{kind}_x_loaded", 2)
        for kind in ("tok", "ffn"):
            w[f"{kind}_group_loaded"] = mem.sem(f"{kind}_group_loaded")
        patch_phase(nc, w, ins["patches"], tiles4(s["x1"]), s["y"])
        attention_phase(nc, w, "tok", lambda j: s["y"][j], tiles2(s["x1"]), tiles2(s["x2"]), None,
                        first_group=tiles4(s["x2"])[0])
        with nc.sbuf_tensor("by_token", [HALF, 2, TOKENS], F32) as big:
            mlp_phase(nc, w, tiles4(s["x2"]), tiles4(s["h"]), big)
            attention_phase(nc, w, "cos", lambda j: big[0:HALF, :, bass.ds(PART * j, PART)], None, None, big)
            router_phase(nc, w, big, tiles4(s["h"]), tiles4(s["h4"]), tiles4(s["zb"])[:, :, :, 0:DIM],
                         tiles4(s["zb"])[:, :, :, DIM:ROW], s["zn"])
        attention_phase(nc, w, "ffn", lambda j: s["zn"][j], tiles2(s["zb"]), tiles2(s["h5"]), None,
                        first_group=tiles4(s["h5"])[0])
        last_phase(nc, w, tiles4(s["h5"]), tiles4(s["zb"])[:, :, :, DIM:ROW], tiles4(s["h4"]), tiles4(out))


SCRATCH = {"x1": (TOKENS // P, P, DIM), "x2": (TOKENS // P, P, DIM), "h": (TOKENS // P, P, DIM), "h4": (TOKENS // P, P, DIM),
           "h5": (TOKENS // P, P, DIM), "zb": (TOKENS // P, P, ROW), "y": (PARTS, HALF, 2, PART), "zn": (PARTS, HALF, 2, PART)}


NORMS = ("ffn_r_ln_g", "ffn_r_ln_b", "ffn_ln1_g", "ffn_ln1_b", "ffn_ln2_g", "ffn_ln2_b")
COLUMNS = {"tok_ff2_b": HALF, "head_scale": HALF, "ffn_r_o1_b": RHD, "ffn_r_o2_b": RH2, **dict.fromkeys(NORMS, HALF)}
UNSPREAD = [k for k in COLUMNS if k != "tok_ff2_b"]


def positions():
    pos = np.arange(SEQ, dtype=np.float32)[:, None]
    i = np.arange(DIM // 2, dtype=np.float32)[None, :]
    angle = (pos / np.power(np.float32(10000.0), np.float32(2.0) * i / np.float32(DIM))).astype(np.float32)
    pe = np.zeros((SEQ, DIM), np.float32)
    pe[:, 0::2], pe[:, 1::2] = np.sin(angle), np.cos(angle)
    return pe


def lay_out(inputs):
    x = {k.replace("L0_", ""): np.asarray(v) for k, v in inputs.items()}
    side = x["x"].shape[2] // PATCH
    tokens = x["x"].reshape(IMAGES, CHANNELS, side, PATCH, side, PATCH).transpose(1, 3, 5, 0, 2, 4).reshape(KP, P, GROUPS, GROUP)

    def qkv(wt):
        v = wt[..., 2 * DIM:].reshape(*wt.shape[:-1], HEADS // 2, 2, HD)
        v = np.swapaxes(v, -3, -2).reshape(*wt.shape[:-1], DIM)
        return np.concatenate([wt[..., :2 * DIM], v], axis=-1)

    a = {
        "patches": tokens.transpose(2, 1, 0, 3),
        "patch_w": x["tok_patch_w"].reshape(DIM, FEATS).T,
        "pe": np.concatenate([positions()] * 2),
        "ident": np.eye(P, dtype=np.float32),
        "first_token": (np.arange(P) % SEQ == 0).astype(np.float32)[:, None],
        "tok_qkv_w": qkv(x["tok_qkv_w"]), "tok_qkv_b": qkv(x["tok_qkv_b"]),
        "cos_qkv_w": qkv(x["attn_in_proj_weight"].T), "cos_qkv_b": qkv(x["attn_in_proj_bias"]),
        "cos_proj_w": x["attn_out_w"].T,
        "logit_scale": x["attn_logit_scale"].reshape(HEADS),
        "head_scale": np.repeat(x["attn_head_scale"].reshape(HEADS), HD),
        "ffn_qkv_w": qkv(np.concatenate([x["ffn_wq"].T, x["ffn_wk"].T, x["ffn_wv"].T], axis=1)),
        "ffn_qkv_b": qkv(np.concatenate([x["ffn_bq"], x["ffn_bk"], x["ffn_bv"]])),
        "ffn_proj_w": x["ffn_wo"].T, "r_in_w": x["ffn_r_in_w"].T, "r_o1_w": x["ffn_r_o1_w"].T,
        "r_o2_w": x["ffn_r_o2_w"].T, "r_o3_w": x["ffn_r_o3_w"].T,
        "fc1_w": x["ffn_fc1_w"].T, "fc2_w": x["ffn_fc2_w"].T,
        "lra_down": x["ffn_lra_down"].reshape(RANK3, DIM).T,
        "lra_up": x["ffn_lra_up"].transpose(0, 2, 1).reshape(RANK3, DIM),
    }
    for key in ("tok_patch_b", "tok_ln_g", "tok_ln_b", "tok_ff1_w", "tok_ff1_b", "tok_ff2_w", "tok_ff2_b", "tok_proj_w", "tok_proj_b",
                "attn_out_b", "ffn_bo", "ffn_fc1_b", "ffn_fc2_b", "ffn_r_in_b", "ffn_r_o1_b", "ffn_r_o2_b", "ffn_r_o3_b",
                "ffn_r_ln_g", "ffn_r_ln_b", "ffn_ln1_g", "ffn_ln1_b", "ffn_ln2_g", "ffn_ln2_b"):
        a[key] = x[key]
    for key, rows in COLUMNS.items():
        a[key + "_col"] = a[key].reshape(-1, rows).T
    for key in UNSPREAD:
        del a[key]
    return {k: np.ascontiguousarray(v) for k, v in a.items()}


def kernel(**inputs):
    import concourse.bacc as bacc
    from concourse.bass_utils import run_bass_kernel_spmd

    arrays = lay_out(inputs)
    nc = bacc.Bacc("TRN2", target_bir_lowering=False, num_devices=1)
    ins = {k: nc.dram_tensor(f"in_{k}", v.shape, mybir.dt.from_np(v.dtype), kind="ExternalInput").ap() for k, v in arrays.items()}
    out = nc.dram_tensor("out", (TOKENS // P, P, DIM), F32, kind="ExternalOutput").ap()
    scratch = {k: nc.dram_tensor(f"scratch_{k}", shape, F32, kind="Internal").ap() for k, shape in SCRATCH.items()}
    vit_tower(nc, ins, out, scratch)
    r = run_bass_kernel_spmd(nc, [{f"in_{k}": v for k, v in arrays.items()}], core_ids=[0])
    return r.results[0]["out"].reshape(IMAGES, SEQ, DIM)
```
